# Optimizing a Trainium2 kernel written in Bass

```python
import numpy as np
import jax
import jax.numpy as jnp

def _softmax(x, axis=-1):
    return jax.nn.softmax(x, axis=axis)

def _gelu(x):
    return jax.nn.gelu(x, approximate=True)

def _silu(x):
    return jax.nn.silu(x)

def _sigmoid(x):
    return jax.nn.sigmoid(x)

def _layernorm(x, axis=-1, eps=1e-05):
    m = jnp.mean(x, axis=axis, keepdims=True)
    v = jnp.var(x, axis=axis, keepdims=True)
    return (x - m) / jnp.sqrt(v + eps)

def _scatter_add(tgt, idx, src, axis=0):
    return tgt.at[idx].add(src)

def _segment_sum(src, seg, n):
    return jax.ops.segment_sum(src, seg, n)
kernel_name = 'mk_macaron_d1_jaxref_r8_806b67'

def setup_inputs(seed: int=0):
    np.random.seed(seed)
    _w = jnp.asarray

    def _L0_attn_setup():
        import jax, jax.numpy as jnp
        import numpy as np
        L, H, D_MODEL, FFN = (2, 8, 128, 512)
        HD = D_MODEL // H
        SCALE_BASE = 64
        EPS = 1e-05

        def _layernorm(x, w, b):
            mu = x.mean(-1, keepdims=True)
            var = ((x - mu) ** 2).mean(-1, keepdims=True)
            return (x - mu) * jax.lax.rsqrt(var + EPS) * w + b

        def _groupnorm(y, w, b):
            B, S, _ = y.shape
            yg = y.reshape(B, S, H, HD)
            mu = yg.mean(-1, keepdims=True)
            var = ((yg - mu) ** 2).mean(-1, keepdims=True)
            yn = ((yg - mu) * jax.lax.rsqrt(var + EPS)).reshape(B, S, H * HD)
            return yn * w + b

        def _xpos_tables(S):
            scale_vec = (np.arange(0, HD, 2) + 0.4 * HD) / (1.4 * HD)
            power = (np.arange(S, dtype=np.float64) / SCALE_BASE)[:, None]
            scale = scale_vec[None, :] ** power
            half = HD // 2
            inv_freq = 1.0 / 10000.0 ** (np.arange(half, dtype=np.float64) / half)
            ang = np.arange(S, dtype=np.float64)[:, None] * inv_freq[None, :]
            sin, cos = (np.sin(ang), np.cos(ang))
            dup = lambda m: jnp.asarray(np.repeat(m, 2, axis=-1).astype(np.float32))
            return (dup(sin * scale), dup(cos * scale), dup(sin / scale), dup(cos / scale))

        def _rotate_every_two(x):
            x1, x2 = (x[..., ::2], x[..., 1::2])
            return jnp.stack((-x2, x1), axis=-1).reshape(x.shape)

        def _decay_mask(S):
            gammas = 1.0 - np.exp(np.linspace(np.log(1.0 / 32), np.log(1.0 / 64), H))
            n = np.arange(S)[:, None]
            m = np.arange(S)[None, :]
            diff = (n - m).astype(np.float64)
            D = np.where(n >= m, gammas[:, None, None] ** diff[None], 0.0)
            return jnp.asarray(D.astype(np.float32))
        key = jax.random.key(seed)
        ks = jax.random.split(key, 8)
        B, S = (2, 256)
        rn = lambda k, shape, s: jax.random.normal(k, shape, dtype=jnp.float32) * s
        return {'X': rn(ks[0], (B, S, D_MODEL), 1.0), 'ln1_w': jnp.ones((L, D_MODEL), jnp.float32), 'ln1_b': jnp.zeros((L, D_MODEL), jnp.float32), 'ln2_w': jnp.ones((L, D_MODEL), jnp.float32), 'ln2_b': jnp.zeros((L, D_MODEL), jnp.float32), 'WQ': rn(ks[1], (L, H, D_MODEL, HD), 1.0 / D_MODEL), 'WK': rn(ks[2], (L, H, D_MODEL, HD), 1.0 / D_MODEL), 'WV': rn(ks[3], (L, H, D_MODEL, HD), 1.0 / D_MODEL), 'gn_w': jnp.ones((L, D_MODEL), jnp.float32), 'gn_b': jnp.zeros((L, D_MODEL), jnp.float32), 'WG': rn(ks[4], (L, D_MODEL, D_MODEL), 1.0 / D_MODEL), 'WO': rn(ks[5], (L, D_MODEL, D_MODEL), 1.0 / D_MODEL), 'ffn_w1': rn(ks[6], (L, D_MODEL, FFN), 1.0 / np.sqrt(D_MODEL)), 'ffn_b1': jnp.zeros((L, FFN), jnp.float32), 'ffn_w2': rn(ks[7], (L, FFN, D_MODEL), 1.0 / np.sqrt(FFN)), 'ffn_b2': jnp.zeros((L, D_MODEL), jnp.float32)}
    _L0_attn_in = _L0_attn_setup()

    def _L0_ffn_setup():
        import jax, jax.numpy as jnp
        import numpy as np
        NUM_EXPERTS = 8
        TOP_K = 2
        NUM_GRIDS = 8
        INV_DENOM = 0.5
        GRID = np.linspace(-1.2, 0.2, NUM_GRIDS).astype(np.float32)
        LN_EPS = 1e-05

        def _layernorm(x, g, b):
            mu = x.mean(-1, keepdims=True)
            var = x.var(-1, keepdims=True)
            return (x - mu) * jax.lax.rsqrt(var + LN_EPS) * g + b

        def _rswaf(x, grid):
            t = jnp.tanh((x[..., None] - grid) * INV_DENOM)
            return 1.0 - t * t
        key = jax.random.key(seed)
        ks = jax.random.split(key, 8)
        B, S, H, F = (1, 256, 128, 512)
        F2 = F // 2
        E2 = NUM_EXPERTS // 2
        G = NUM_GRIDS
        s = 0.02
        return {'hidden_states': jax.random.normal(ks[0], (B, S, H), jnp.float32), 'gate_W': jax.random.normal(ks[1], (H, NUM_EXPERTS), jnp.float32) * s, 'mlp_W1': jax.random.normal(ks[2], (E2, H, F), jnp.float32) * s, 'mlp_b1': jnp.zeros((E2, F), jnp.float32), 'mlp_W2': jax.random.normal(ks[3], (E2, F, H), jnp.float32) * s, 'mlp_b2': jnp.zeros((E2, H), jnp.float32), 'kan_ln_g0': jnp.ones((E2, H), jnp.float32), 'kan_ln_b0': jnp.zeros((E2, H), jnp.float32), 'kan_sl_W0': jax.random.normal(ks[4], (E2, H * G, F2), jnp.float32) * s, 'kan_sl_b0': jnp.zeros((E2, F2), jnp.float32), 'kan_ln_g1': jnp.ones((E2, F2), jnp.float32), 'kan_ln_b1': jnp.zeros((E2, F2), jnp.float32), 'kan_sl_W1': jax.random.normal(ks[5], (E2, F2 * G, H), jnp.float32) * s, 'kan_sl_b1': jnp.zeros((E2, H), jnp.float32)}
    _L0_ffn_in = _L0_ffn_setup()
    _d = {'L0_attn_X': _L0_attn_in['X'], 'L0_attn_ln1_w': _L0_attn_in['ln1_w'], 'L0_attn_ln1_b': _L0_attn_in['ln1_b'], 'L0_attn_ln2_w': _L0_attn_in['ln2_w'], 'L0_attn_ln2_b': _L0_attn_in['ln2_b'], 'L0_attn_WQ': _L0_attn_in['WQ'], 'L0_attn_WK': _L0_attn_in['WK'], 'L0_attn_WV': _L0_attn_in['WV'], 'L0_attn_gn_w': _L0_attn_in['gn_w'], 'L0_attn_gn_b': _L0_attn_in['gn_b'], 'L0_attn_WG': _L0_attn_in['WG'], 'L0_attn_WO': _L0_attn_in['WO'], 'L0_attn_ffn_w1': _L0_attn_in['ffn_w1'], 'L0_attn_ffn_b1': _L0_attn_in['ffn_b1'], 'L0_attn_ffn_w2': _L0_attn_in['ffn_w2'], 'L0_attn_ffn_b2': _L0_attn_in['ffn_b2'], 'L0_ffn_gate_W': _L0_ffn_in['gate_W'], 'L0_ffn_mlp_W1': _L0_ffn_in['mlp_W1'], 'L0_ffn_mlp_b1': _L0_ffn_in['mlp_b1'], 'L0_ffn_mlp_W2': _L0_ffn_in['mlp_W2'], 'L0_ffn_mlp_b2': _L0_ffn_in['mlp_b2'], 'L0_ffn_kan_ln_g0': _L0_ffn_in['kan_ln_g0'], 'L0_ffn_kan_ln_b0': _L0_ffn_in['kan_ln_b0'], 'L0_ffn_kan_sl_W0': _L0_ffn_in['kan_sl_W0'], 'L0_ffn_kan_sl_b0': _L0_ffn_in['kan_sl_b0'], 'L0_ffn_kan_ln_g1': _L0_ffn_in['kan_ln_g1'], 'L0_ffn_kan_ln_b1': _L0_ffn_in['kan_ln_b1'], 'L0_ffn_kan_sl_W1': _L0_ffn_in['kan_sl_W1'], 'L0_ffn_kan_sl_b1': _L0_ffn_in['kan_sl_b1']}
    _x0 = _d['L0_attn_X']
    _d['L0_attn_X'] = jax.random.normal(jax.random.fold_in(jax.random.key(seed), 1), (8, 512, 128), dtype=_x0.dtype)
    del _x0
    return _d

def reference(L0_attn_X, L0_attn_ln1_w, L0_attn_ln1_b, L0_attn_ln2_w, L0_attn_ln2_b, L0_attn_WQ, L0_attn_WK, L0_attn_WV, L0_attn_gn_w, L0_attn_gn_b, L0_attn_WG, L0_attn_WO, L0_attn_ffn_w1, L0_attn_ffn_b1, L0_attn_ffn_w2, L0_attn_ffn_b2, L0_ffn_gate_W, L0_ffn_mlp_W1, L0_ffn_mlp_b1, L0_ffn_mlp_W2, L0_ffn_mlp_b2, L0_ffn_kan_ln_g0, L0_ffn_kan_ln_b0, L0_ffn_kan_sl_W0, L0_ffn_kan_sl_b0, L0_ffn_kan_ln_g1, L0_ffn_kan_ln_b1, L0_ffn_kan_sl_W1, L0_ffn_kan_sl_b1):

    def _L0_attn_ref(X, ln1_w, ln1_b, ln2_w, ln2_b, WQ, WK, WV, gn_w, gn_b, WG, WO, ffn_w1, ffn_b1, ffn_w2, ffn_b2):
        import jax, jax.numpy as jnp
        import numpy as np
        L, H, D_MODEL, FFN = (2, 8, 128, 512)
        HD = D_MODEL // H
        SCALE_BASE = 64
        EPS = 1e-05

        def _layernorm(x, w, b):
            mu = x.mean(-1, keepdims=True)
            var = ((x - mu) ** 2).mean(-1, keepdims=True)
            return (x - mu) * jax.lax.rsqrt(var + EPS) * w + b

        def _groupnorm(y, w, b):
            B, S, _ = y.shape
            yg = y.reshape(B, S, H, HD)
            mu = yg.mean(-1, keepdims=True)
            var = ((yg - mu) ** 2).mean(-1, keepdims=True)
            yn = ((yg - mu) * jax.lax.rsqrt(var + EPS)).reshape(B, S, H * HD)
            return yn * w + b

        def _xpos_tables(S):
            scale_vec = (np.arange(0, HD, 2) + 0.4 * HD) / (1.4 * HD)
            power = (np.arange(S, dtype=np.float64) / SCALE_BASE)[:, None]
            scale = scale_vec[None, :] ** power
            half = HD // 2
            inv_freq = 1.0 / 10000.0 ** (np.arange(half, dtype=np.float64) / half)
            ang = np.arange(S, dtype=np.float64)[:, None] * inv_freq[None, :]
            sin, cos = (np.sin(ang), np.cos(ang))
            dup = lambda m: jnp.asarray(np.repeat(m, 2, axis=-1).astype(np.float32))
            return (dup(sin * scale), dup(cos * scale), dup(sin / scale), dup(cos / scale))

        def _rotate_every_two(x):
            x1, x2 = (x[..., ::2], x[..., 1::2])
            return jnp.stack((-x2, x1), axis=-1).reshape(x.shape)

        def _decay_mask(S):
            gammas = 1.0 - np.exp(np.linspace(np.log(1.0 / 32), np.log(1.0 / 64), H))
            n = np.arange(S)[:, None]
            m = np.arange(S)[None, :]
            diff = (n - m).astype(np.float64)
            D = np.where(n >= m, gammas[:, None, None] ** diff[None], 0.0)
            return jnp.asarray(D.astype(np.float32))
        B, S, _ = X.shape
        sinq, cosq, sink, cosk = _xpos_tables(S)
        Dm = _decay_mask(S)
        for i in range(L):
            Xn = _layernorm(X, ln1_w[i], ln1_b[i])
            Q = jnp.einsum('bsd,hdk->bhsk', Xn, WQ[i])
            K = jnp.einsum('bsd,hdk->bhsk', Xn, WK[i])
            V = jnp.einsum('bsd,hdk->bhsk', Xn, WV[i])
            Q = Q * cosq + _rotate_every_two(Q) * sinq
            K = K * cosk + _rotate_every_two(K) * sink
            scores = jnp.einsum('bhsk,bhtk->bhst', Q, K) * Dm[None]
            Yh = jnp.einsum('bhst,bhtk->bhsk', scores, V)
            Y = Yh.transpose(0, 2, 1, 3).reshape(B, S, H * HD)
            Y = _groupnorm(Y, gn_w[i], gn_b[i])
            G = jax.nn.silu(Xn @ WG[i])
            Y = G * Y @ WO[i] + X
            Yn = _layernorm(Y, ln2_w[i], ln2_b[i])
            X = jax.nn.silu(Yn @ ffn_w1[i] + ffn_b1[i]) @ ffn_w2[i] + ffn_b2[i] + Y
        return X

    def _L0_ffn_ref(hidden_states, gate_W, mlp_W1, mlp_b1, mlp_W2, mlp_b2, kan_ln_g0, kan_ln_b0, kan_sl_W0, kan_sl_b0, kan_ln_g1, kan_ln_b1, kan_sl_W1, kan_sl_b1):
        import jax, jax.numpy as jnp
        import numpy as np
        NUM_EXPERTS = 8
        TOP_K = 2
        NUM_GRIDS = 8
        INV_DENOM = 0.5
        GRID = np.linspace(-1.2, 0.2, NUM_GRIDS).astype(np.float32)
        LN_EPS = 1e-05

        def _layernorm(x, g, b):
            mu = x.mean(-1, keepdims=True)
            var = x.var(-1, keepdims=True)
            return (x - mu) * jax.lax.rsqrt(var + LN_EPS) * g + b

        def _rswaf(x, grid):
            t = jnp.tanh((x[..., None] - grid) * INV_DENOM)
            return 1.0 - t * t
        B, S, H = hidden_states.shape
        E2, _, F2 = (kan_sl_W0.shape[0], kan_sl_W0.shape[1], kan_sl_W0.shape[2])
        G = NUM_GRIDS
        x = hidden_states.reshape(-1, H)
        T = x.shape[0]
        logits = x @ gate_W
        probs = jax.nn.softmax(logits.astype(jnp.float32), axis=-1)
        rw, sel = jax.lax.top_k(probs, TOP_K)
        rw = rw / rw.sum(axis=-1, keepdims=True)
        w_full = jnp.sum(jax.nn.one_hot(sel, NUM_EXPERTS, dtype=rw.dtype) * rw[..., None], axis=1)
        w_full = w_full.astype(x.dtype)
        h = jnp.einsum('th,ehf->etf', x, mlp_W1) + mlp_b1[:, None, :]
        h = jax.nn.gelu(h, approximate=False)
        mlp_out = jnp.einsum('etf,efh->eth', h, mlp_W2) + mlp_b2[:, None, :]
        grid = jnp.asarray(GRID)
        h0 = _layernorm(x[None], kan_ln_g0[:, None, :], kan_ln_b0[:, None, :])
        basis0 = _rswaf(h0, grid).reshape(E2, T, H * G)
        z = jnp.einsum('eti,eio->eto', basis0, kan_sl_W0) + kan_sl_b0[:, None, :]
        h1 = _layernorm(z, kan_ln_g1[:, None, :], kan_ln_b1[:, None, :])
        basis1 = _rswaf(h1, grid).reshape(E2, T, F2 * G)
        kan_out = jnp.einsum('eti,eio->eto', basis1, kan_sl_W1) + kan_sl_b1[:, None, :]
        expert_out = jnp.concatenate([mlp_out, kan_out], axis=0)
        out = jnp.einsum('eth,te->th', expert_out, w_full)
        return out.reshape(B, S, H)
    x = L0_attn_X
    x = x + 0.5 * _L0_ffn_ref(_layernorm(x, axis=-1), L0_ffn_gate_W, L0_ffn_mlp_W1, L0_ffn_mlp_b1, L0_ffn_mlp_W2, L0_ffn_mlp_b2, L0_ffn_kan_ln_g0, L0_ffn_kan_ln_b0, L0_ffn_kan_sl_W0, L0_ffn_kan_sl_b0, L0_ffn_kan_ln_g1, L0_ffn_kan_ln_b1, L0_ffn_kan_sl_W1, L0_ffn_kan_sl_b1)
    x = x + _L0_attn_ref(_layernorm(x, axis=-1), L0_attn_ln1_w, L0_attn_ln1_b, L0_attn_ln2_w, L0_attn_ln2_b, L0_attn_WQ, L0_attn_WK, L0_attn_WV, L0_attn_gn_w, L0_attn_gn_b, L0_attn_WG, L0_attn_WO, L0_attn_ffn_w1, L0_attn_ffn_b1, L0_attn_ffn_w2, L0_attn_ffn_b2)
    x = x + 0.5 * _L0_ffn_ref(_layernorm(x, axis=-1), L0_ffn_gate_W, L0_ffn_mlp_W1, L0_ffn_mlp_b1, L0_ffn_mlp_W2, L0_ffn_mlp_b2, L0_ffn_kan_ln_g0, L0_ffn_kan_ln_b0, L0_ffn_kan_sl_W0, L0_ffn_kan_sl_b0, L0_ffn_kan_ln_g1, L0_ffn_kan_ln_b1, L0_ffn_kan_sl_W1, L0_ffn_kan_sl_b1)
    return x

_drawn_inputs = setup_inputs


def setup_inputs(seed=0):
    import zlib

    import numpy as np

    out = dict(_drawn_inputs(seed))
    spreads = {'L0_attn_ln1_w': (1.0, 0.6),
     'L0_attn_ln1_b': (0.0, 0.8),
     'L0_attn_ln2_w': (1.0, 0.2),
     'L0_attn_ln2_b': (0.0, 0.1),
     'L0_attn_gn_w': (1.0, 0.6),
     'L0_attn_gn_b': (0.0, 0.8),
     'L0_attn_ffn_b1': (0.0, 0.1),
     'L0_attn_ffn_b2': (0.0, 0.1),
     'L0_ffn_mlp_b1': (0.0, 0.782),
     'L0_ffn_mlp_b2': (0.0, 0.1),
     'L0_ffn_kan_ln_g0': (1.0, 0.6),
     'L0_ffn_kan_ln_b0': (0.0, 2.0),
     'L0_ffn_kan_sl_b0': (0.0, 0.413),
     'L0_ffn_kan_ln_g1': (1.0, 0.6),
     'L0_ffn_kan_ln_b1': (0.0, 0.8),
     'L0_ffn_kan_sl_b1': (0.0, 0.1)}
    factors = {'L0_attn_WQ': 8.0,
     'L0_attn_WK': 8.0,
     'L0_attn_WV': 8.0,
     'L0_attn_WG': 8.0,
     'L0_attn_WO': 8.0,
     'L0_ffn_mlp_W1': 2.945}
    for name, (base, spread) in spreads.items():
        noise = np.random.default_rng([zlib.crc32(name.encode()), seed]).standard_normal(out[name].shape)
        drawn = base * np.exp(spread * noise) if base else spread * noise
        out[name] = jnp.asarray(drawn.astype(out[name].dtype))
    for name, factor in factors.items():
        out[name] = (out[name] * factor).astype(out[name].dtype)
    return out
```

```python
from contextlib import ExitStack

import concourse.bass as bass
import numpy as np
from concourse import mybir

F32 = mybir.dt.float32
ACT = mybir.ActivationFunctionType
ALU = mybir.AluOpType
AX_X = mybir.AxisListType.X

P = 128
EPS = 1e-5
NE = 4
NG = 8
FM = 512
F2 = 256
T = 1024
TC = T // P
NT = 4
BANK = 512
RING = 6
L0 = NG
L1 = 2 * NG
SLABS = L0 + L1
LOOK = 4
NL = 2
NH = 8
HD = P // NH
S = 512
NC = S // P
NB = 8
SLOTS = 2
NEG_HALF_GRID = -0.5 * np.linspace(-1.2, 0.2, NG).astype(np.float32)

COLS = {}
_at = 0
for _name, _n in (("gate", 8), ("kan_g0", NE), ("kan_b0", NE), ("kan_g1", 2 * NE), ("kan_b1", 2 * NE),
                  ("mlp_b1", 4 * NE), ("mlp_b2", NE), ("ln1_w", NL), ("ln1_b", NL), ("ln2_w", NL), ("ln2_b", NL),
                  ("gn_w", NL), ("gn_b", NL), ("ffn_b1", 4 * NL), ("neg_half_grid", NG), ("head_mask", NH),
                  ("decay_chunk", 1)):
    COLS[_name] = (_at, _at + _n)
    _at += _n
NCOLS = _at


def build(nc, A):
    ctx = ExitStack()
    with ctx:
        def sb(name, shape, stack=ctx):
            return stack.enter_context(nc.sbuf_tensor(name, shape, F32))

        def sem(name):
            return ctx.enter_context(nc.semaphore(name))

        small_in = sem("small_in")

        x_all = sb("x_all", [P, NB * NC, P])
        cols = sb("cols", [P, NCOLS])
        ident = sb("ident", [P, P])
        ones = sb("ones", [P, P])
        neg_half = sb("neg_half", [P, 64])
        idle = sb("idle", [P, 64])
        idle_word = iter(range(64))
        tril = sb("tril", [P, 8, 8])
        w0 = sb("w0", [P, NE, NG, F2])
        w1 = sb("w1", [P, NE, 2, NG, P])
        mw1 = sb("mw1", [P, NE, FM])
        mw2 = sb("mw2", [P, NE, 4, P])
        z_bias = sb("z_bias", [P, NE, 2])
        o_bias = sb("o_bias", [P, NE])
        scale0 = sb("scale0", [P, NE])
        bias0 = sb("bias0", [P, NE, NG])
        scale1 = sb("scale1", [P, 2 * NE])
        bias1 = sb("bias1", [P, 2 * NE, NG])
        psum = ctx.enter_context(nc.psum_tensor("psum", [P, 8, BANK], F32))

        def hold(eng):
            k = next(idle_word)
            if eng is nc.vector:
                nc.vector.memset(idle[:, k:k + 1], 0.0)
            else:
                nc.gpsimd.tensor_tensor(idle[:, k:k + 1], neg_half[:, 0:1], neg_half[:, 1:2], ALU.add)

        def col(name, i=0, n=1):
            a = COLS[name][0] + i
            return cols[:, a:a + n]

        with ExitStack() as tmp:
            kan_rows = sb("kan_rows", [1, NE, F2 + P], tmp)
            row_mean = sb("row_mean", [P, NE, NG], tmp)
            bias_mean = sb("bias_mean", [1, NE], tmp)
            x_in = sem("x_in")
            w0_in = [sem(f"w0_in{e}") for e in range(NE)]
            w1_in = sem("w1_in")
            mlp_in = sem("mlp_in")
            prep_step = sem("prep_step")
            w0_centred = sem("w0_centred")
            sums_done = sem("sums_done")
            prep_done = sem("prep_done")
            with nc.Block() as block:
                @block.sync
                def _(sp):
                    for dst, src in ((cols[:], A["cols"]), (ident[:], A["ident"]), (tril[:], A["tril"]),
                                     (kan_rows[:], A["kan_rows"])):
                        sp.dma_start(dst, src).then_inc(small_in, 16)
                    for e in range(NE):
                        sp.dma_start(w0[:, e], A["w0"][:, e]).then_inc(w0_in[e], 16)
                    sp.dma_start(x_all[:], A["x"]).then_inc(x_in, 16)
                    sp.dma_start(w1[:], A["w1"]).then_inc(w1_in, 16)
                    sp.dma_start(mw1[:], A["mw1"]).then_inc(mlp_in, 16)
                    sp.dma_start(mw2[:], A["mw2"]).then_inc(mlp_in, 16)
                    sp.wait_ge(x_in, 16)
                    sp.wait_ge(mlp_in, 32)

                @block.vector
                def _(dve):
                    done = [0]

                    def step(ins):
                        done[0] += 1
                        ins.then_inc(prep_step, 1)
                        dve.wait_ge(prep_step, done[0])

                    nc.vector.memset(ones[:], 1.0).then_inc(prep_done, 1)
                    nc.vector.memset(neg_half[:], -0.5).then_inc(prep_done, 1)
                    dve.wait_ge(small_in, 64)
                    nc.vector.tensor_scalar(scale0[:], col("kan_g0", 0, NE), 0.5, None, ALU.mult).then_inc(prep_done, 1)
                    nc.vector.tensor_scalar(scale1[:], col("kan_g1", 0, 2 * NE), 0.5, None,
                                            ALU.mult).then_inc(prep_done, 1)
                    nc.vector.scalar_tensor_tensor(
                        out=bias0[:], in0=col("kan_b0", 0, NE).unsqueeze(2).to_broadcast([P, NE, NG]), scalar=0.5,
                        in1=col("neg_half_grid", 0, NG).unsqueeze(1).to_broadcast([P, NE, NG]),
                        op0=ALU.mult, op1=ALU.add).then_inc(prep_done, 1)
                    nc.vector.scalar_tensor_tensor(
                        out=bias1[:], in0=col("kan_b1", 0, 2 * NE).unsqueeze(2).to_broadcast([P, 2 * NE, NG]),
                        scalar=0.5, in1=col("neg_half_grid", 0, NG).unsqueeze(1).to_broadcast([P, 2 * NE, NG]),
                        op0=ALU.mult, op1=ALU.add).then_inc(prep_done, 1)
                    rows = kan_rows[:, :, 0:F2]
                    step(nc.vector.tensor_reduce(bias_mean[:], rows, AX_X, ALU.add))
                    step(nc.vector.tensor_scalar(bias_mean[:], bias_mean[:], 1.0 / F2, None, ALU.mult))
                    nc.vector.tensor_tensor(rows, rows, bias_mean[:].unsqueeze(2).to_broadcast([1, NE, F2]),
                                            ALU.subtract).then_inc(w0_centred, 1)
                    for e in range(NE):
                        dve.wait_ge(w0_in[e], 16)
                        step(nc.vector.tensor_reduce(row_mean[:, e], w0[:, e], AX_X, ALU.add))
                        step(nc.vector.tensor_scalar(row_mean[:, e], row_mean[:, e], 1.0 / F2, None, ALU.mult))
                        nc.vector.tensor_tensor(w0[:, e], w0[:, e],
                                                row_mean[:, e].unsqueeze(2).to_broadcast([P, NG, F2]),
                                                ALU.subtract).then_inc(w0_centred, 1)
                    dve.wait_ge(sums_done, 1)
                    nc.vector.tensor_copy(z_bias[:], psum[:, 0, 0:2 * NE].rearrange("p (e m) -> p e m", m=2)
                                          ).then_inc(prep_done, 1)
                    nc.vector.tensor_copy(o_bias[:], psum[:, 0, 2 * NE:3 * NE]).then_inc(prep_done, 1)
                    dve.wait_ge(prep_done, 8)

                @block.tensor
                def _(pe):
                    pe.wait_ge(prep_done, 1)
                    pe.wait_ge(w0_centred, 1)
                    for e in range(NE):
                        pe.wait_ge(w0_centred, e + 2)
                        for m in range(2):
                            out = psum[:, 0, 2 * e + m:2 * e + m + 1]
                            for g in range(NG):
                                nc.tensor.matmul(out, w0[:, e, g, m * P:(m + 1) * P], ones[:, 0:1],
                                                 start=(g == 0), stop=False)
                            nc.tensor.matmul(out, kan_rows[:, e, m * P:(m + 1) * P], ones[0:1, 0:1],
                                             start=False, stop=True)
                    pe.wait_ge(w1_in, 16)
                    for e in range(NE):
                        out = psum[:, 0, 2 * NE + e:2 * NE + e + 1]
                        for m in range(2):
                            for g in range(NG):
                                nc.tensor.matmul(out, w1[:, e, m, g, :], ones[:, 0:1],
                                                 start=(m == 0 and g == 0), stop=False)
                        last = nc.tensor.matmul(out, kan_rows[:, e, F2:F2 + P], ones[0:1, 0:1],
                                                start=False, stop=True)
                    last.then_inc(sums_done, 1)

        def feed_forward(tag):
            tmp = ExitStack()
            with tmp:
                acc = sb(f"acc_{tag}", [P, TC, P], tmp)
                a_tok = sb(f"a_tok_{tag}", [P, TC, P], tmp)
                n_tok = sb(f"n_tok_{tag}", [P, TC, P], tmp)
                a_t = sb(f"a_t_{tag}", [P, T], tmp)
                n_t = sb(f"n_t_{tag}", [P, T], tmp)
                stats = sb(f"stats_{tag}", [P, TC, 6], tmp)
                mean_var = sb(f"mean_var_{tag}", [P, TC, 2], tmp)
                var_eps = sb(f"var_eps_{tag}", [P, TC], tmp)
                rstd = sb(f"rstd_{tag}", [P, TC], tmp)
                z_var = sb(f"z_var_{tag}", [P, TC], tmp)
                z_rstd = sb(f"z_rstd_{tag}", [P, TC], tmp)
                top = sb(f"top_{tag}", [P, TC], tmp)
                e_sum = sb(f"e_sum_{tag}", [P, TC], tmp)
                probs = sb(f"probs_{tag}", [P, TC, 8], tmp)
                above = sb(f"above_{tag}", [P, TC, 8, 8], tmp)
                equal = sb(f"equal_{tag}", [P, TC, 8, 8], tmp)
                rank = sb(f"rank_{tag}", [P, TC, 8], tmp)
                gates = sb(f"gates_{tag}", [P, TC, 8], tmp)
                ring = sb(f"ring_{tag}", [P, RING, T], tmp)
                hid = sb(f"hid_{tag}", [P, 2, T], tmp)
                zc = sb(f"zc_{tag}", [P, 2, T], tmp)
                z_sq = sb(f"z_sq_{tag}", [P, 2, T], tmp)
                diag = sb(f"diag_{tag}", [P, TC, P], tmp)
                eo = sb(f"eo_{tag}", [P, T], tmp)

                ps_z = psum[:, 0:4].rearrange("p (m b) t -> p m (b t)", m=2)
                ps_h = psum[:, 4:6].rearrange("p b t -> p (b t)")
                ps_o = psum[:, 6:8].rearrange("p b t -> p (b t)")
                ps_ht = psum[:, 4:6].rearrange("p b (c f) -> p (b c) f", f=P)
                ps_ot = psum[:, 6:8].rearrange("p b (c f) -> p (b c) f", f=P)
                ps_bc = psum[:, 2:4].rearrange("p b t -> p (b t)")
                ps_var = psum[:, 0, 0:TC]
                ps_logit = psum[:, 0, 64:128].rearrange("p (c e) -> p c e", e=8)

                x_copied = sem(f"x_copied_{tag}")
                x_stored = sem(f"x_stored_{tag}")
                dve_step = sem(f"dve_step_{tag}")
                var_asked = sem(f"var_asked_{tag}")
                rstd_given = sem(f"rstd_given_{tag}")
                norm_ready = sem(f"norm_ready_{tag}")
                norm_turned = sem(f"norm_turned_{tag}")
                a_t_ready = sem(f"a_t_ready_{tag}")
                n_t_ready = sem(f"n_t_ready_{tag}")
                logits_done = sem(f"logits_done_{tag}")
                shifted = sem(f"shifted_{tag}")
                exp_done = sem(f"exp_done_{tag}")
                tanh_done = sem(f"tanh_done_{tag}")
                basis_ready = sem(f"basis_ready_{tag}")
                slab_used = sem(f"slab_used_{tag}")
                hid_done = sem(f"hid_done_{tag}")
                gelu_done = sem(f"gelu_done_{tag}")
                hid_used = sem(f"hid_used_{tag}")
                z_sq_ready = sem(f"z_sq_ready_{tag}")
                zc_ready = sem(f"zc_ready_{tag}")
                z_sum_ready = sem(f"z_sum_ready_{tag}")
                z_var_done = sem(f"z_var_done_{tag}")
                z_var_ready = sem(f"z_var_ready_{tag}")
                z_rstd_ready = sem(f"z_rstd_ready_{tag}")
                diag_ready = sem(f"diag_ready_{tag}")
                bc_done = sem(f"bc_done_{tag}")
                n1_ready = sem(f"n1_ready_{tag}")
                eo_ready = sem(f"eo_ready_{tag}")
                eo_turned = sem(f"eo_turned_{tag}")
                acc_done = sem(f"acc_done_{tag}")
                DVE_STEPS = 16

                with nc.Block() as block:
                    @block.gpsimd
                    def _(pool):
                        with pool.Fori(0, NT) as i:
                            nc.gpsimd.tensor_copy(acc[:], x_all[:, bass.ds(i * TC, TC), :]).then_inc(x_copied, 1)
                            for k in range(2):
                                pool.wait_ge(var_asked, i * 2 + k + 1)
                                nc.gpsimd.tensor_tensor(rstd[:], var_eps[:], neg_half[:, 0:TC],
                                                        ALU.pow).then_inc(rstd_given, 1)
                            for e in range(NE):
                                pool.wait_ge(z_sq_ready, i * 2 * NE + 2 * e + 2)
                                nc.gpsimd.tensor_tensor(z_sq[:, 0], z_sq[:, 0], z_sq[:, 1],
                                                        ALU.add).then_inc(z_sum_ready, 1)
                                pool.wait_ge(z_var_ready, i * NE + e + 1)
                                nc.gpsimd.tensor_tensor(z_rstd[:], z_var[:], neg_half[:, 0:TC],
                                                        ALU.pow).then_inc(z_rstd_ready, 1)
                            pool.wait_ge(acc_done, (i + 1) * 2 * NE)
                            hold(pool)
                            nc.gpsimd.tensor_copy(x_all[:, bass.ds(i * TC, TC), :], acc[:]).then_inc(x_stored, 1)
                            pool.wait_ge(x_stored, i + 1)

                    @block.vector
                    def _(dve):
                        with dve.Fori(0, NT) as i:
                            done = [0]

                            def step(ins):
                                done[0] += 1
                                ins.then_inc(dve_step, 1)
                                dve.wait_ge(dve_step, i * DVE_STEPS + done[0])

                            def normalise(dst, src, k):
                                for c in range(TC):
                                    last = nc.vector.bn_stats(stats[:, c], src[:, c])
                                step(last)
                                hold(dve)
                                for c in range(TC):
                                    last = nc.vector.bn_aggr(mean_var[:, c], stats[:, c])
                                step(last)
                                nc.vector.tensor_scalar(var_eps[:], mean_var[:, :, 1], EPS, None,
                                                        ALU.add).then_inc(var_asked, 1)
                                dve.wait_ge(rstd_given, i * 2 + k + 1)
                                for c in range(TC):
                                    last = nc.vector.tensor_scalar(dst[:, c], src[:, c], mean_var[:, c, 0:1],
                                                                   rstd[:, c:c + 1], ALU.subtract, ALU.mult)
                                last.then_inc(norm_ready, 1)
                                dve.wait_ge(norm_ready, i * 2 + k + 1)

                            dve.wait_ge(x_copied, i + 1)
                            normalise(a_tok, acc, 0)
                            normalise(n_tok, a_tok, 1)
                            dve.wait_ge(logits_done, i + 1)
                            step(nc.vector.tensor_reduce(top[:], ps_logit, AX_X, ALU.max))
                            nc.vector.tensor_tensor(probs[:], ps_logit, top[:].unsqueeze(2).to_broadcast([P, TC, 8]),
                                                    ALU.subtract).then_inc(shifted, 1)
                            dve.wait_ge(exp_done, i + 1)
                            step(nc.vector.tensor_reduce(e_sum[:], probs[:], AX_X, ALU.add))
                            step(nc.vector.reciprocal(e_sum[:], e_sum[:]))
                            step(nc.vector.tensor_tensor(probs[:], probs[:],
                                                         e_sum[:].unsqueeze(2).to_broadcast([P, TC, 8]), ALU.mult))
                            pj = probs[:].unsqueeze(2).to_broadcast([P, TC, 8, 8])
                            pi = probs[:].unsqueeze(3).to_broadcast([P, TC, 8, 8])
                            nc.vector.tensor_tensor(above[:], pj, pi, ALU.is_gt)
                            step(nc.vector.tensor_tensor(equal[:], pj, pi, ALU.is_equal))
                            step(nc.vector.tensor_tensor(equal[:], equal[:],
                                                         tril[:].unsqueeze(1).to_broadcast([P, TC, 8, 8]), ALU.mult))
                            step(nc.vector.tensor_tensor(above[:], above[:], equal[:], ALU.add))
                            step(nc.vector.tensor_reduce(rank[:], above[:], AX_X, ALU.add))
                            step(nc.vector.scalar_tensor_tensor(out=gates[:], in0=rank[:], scalar=1.5, in1=probs[:],
                                                                op0=ALU.is_lt, op1=ALU.mult))
                            step(nc.vector.tensor_reduce(e_sum[:], gates[:], AX_X, ALU.add))
                            step(nc.vector.reciprocal(e_sum[:], e_sum[:]))
                            step(nc.vector.scalar_tensor_tensor(
                                out=gates[:], in0=gates[:], scalar=0.5,
                                in1=e_sum[:].unsqueeze(2).to_broadcast([P, TC, 8]), op0=ALU.mult, op1=ALU.mult))

                            def square(e, s):
                                k = e * SLABS + s
                                dve.wait_ge(tanh_done, i * NE * SLABS + k + 1)
                                t = ring[:, k % RING]
                                nc.vector.tensor_tensor(t, t, t, ALU.mult).then_inc(basis_ready, 1)

                            def accumulate(e, kan):
                                n = 2 * e + kan
                                dve.wait_ge(eo_turned, i * 2 * NE + n + 1)
                                for c in range(TC):
                                    g = (NE if kan else 0) + e
                                    last = nc.vector.scalar_tensor_tensor(
                                        out=acc[:, c], in0=ps_ht[:, c], scalar=gates[:, c, g:g + 1],
                                        in1=acc[:, c], op0=ALU.mult, op1=ALU.add)
                                last.then_inc(acc_done, 1)
                                dve.wait_ge(acc_done, i * 2 * NE + n + 1)

                            for e in range(NE):
                                for s in range(L0):
                                    square(e, s)
                                if e:
                                    accumulate(e - 1, 1)
                                dve.wait_ge(z_var_done, i * NE + e + 1)
                                nc.vector.tensor_scalar(z_var[:], ps_var, 1.0 / F2, EPS, ALU.mult,
                                                        ALU.add).then_inc(z_var_ready, 1)
                                dve.wait_ge(z_rstd_ready, i * NE + e + 1)
                                nc.vector.tensor_tensor(diag[:], ident[:].unsqueeze(1).to_broadcast([P, TC, P]),
                                                        z_rstd[:].unsqueeze(2).to_broadcast([P, TC, P]),
                                                        ALU.mult).then_inc(diag_ready, 1)
                                dve.wait_ge(bc_done, i * NE + e + 1)
                                dve.wait_ge(zc_ready, i * 2 * NE + 2 * e + 2)
                                for m in range(2):
                                    nc.vector.tensor_tensor(zc[:, m], zc[:, m], ps_bc, ALU.mult).then_inc(n1_ready, 1)
                                for s in range(L0, SLABS):
                                    square(e, s)
                                    if s == L0 + 9:
                                        accumulate(e, 0)
                            accumulate(NE - 1, 1)
                            assert done[0] == DVE_STEPS, done

                    @block.scalar
                    def _(act):
                        with act.Fori(0, NT) as i:
                            act.wait_ge(norm_turned, i * 2 + 1)
                            nc.scalar.activation(a_t[:], ps_h, ACT.Copy).then_inc(a_t_ready, 1)
                            act.wait_ge(norm_turned, i * 2 + 2)
                            nc.scalar.activation(n_t[:], ps_o, ACT.Copy).then_inc(n_t_ready, 1)
                            act.wait_ge(shifted, i + 1)
                            nc.scalar.activation(probs[:], probs[:], ACT.Exp).then_inc(exp_done, 1)
                            act.wait_ge(n_t_ready, i + 1)

                            def tanh(e, s):
                                k = e * SLABS + s
                                act.wait_ge(slab_used, i * NE * SLABS + k + 1)
                                if s < L0:
                                    src, sc, bi = n_t[:], scale0[:, e:e + 1], bias0[:, e, s:s + 1]
                                else:
                                    m, g = divmod(s - L0, NG)
                                    if g == 0:
                                        act.wait_ge(n1_ready, i * 2 * NE + 2 * e + m + 1)
                                    q = 2 * e + m
                                    src, sc, bi = zc[:, m], scale1[:, q:q + 1], bias1[:, q, g:g + 1]
                                nc.scalar.activation(ring[:, k % RING], src, ACT.Tanh, bias=bi,
                                                     scale=sc).then_inc(tanh_done, 1)

                            def gelu(e, j):
                                n = i * 4 * NE + 4 * e + j
                                act.wait_ge(hid_done, n + 1)
                                act.wait_ge(hid_used, n + 1)
                                nc.scalar.activation(hid[:, j % 2], ps_h, ACT.Gelu,
                                                     bias=col("mlp_b1", 4 * e + j)).then_inc(gelu_done, 1)

                            def z_square(e, m):
                                if m == 0:
                                    act.wait_ge(z_var_done, i * NE + e)
                                nc.scalar.activation(z_sq[:, m], ps_z[:, m], ACT.Square, bias=z_bias[:, e, m:m + 1],
                                                     scale=-1.0).then_inc(z_sq_ready, 1)

                            def z_copy(e, m):
                                nc.scalar.activation(zc[:, m], ps_z[:, m], ACT.Identity, bias=z_bias[:, e, m:m + 1],
                                                     scale=-1.0).then_inc(zc_ready, 1)

                            for e in range(NE):
                                for s in range(LOOK if e else 0, L0):
                                    tanh(e, s)
                                act.wait_ge(slab_used, i * NE * SLABS + e * SLABS + L0 + RING)
                                z_square(e, 0)
                                z_square(e, 1)
                                gelu(e, 0)
                                z_copy(e, 0)
                                gelu(e, 1)
                                z_copy(e, 1)
                                gelu(e, 2)
                                gelu(e, 3)
                                act.wait_ge(hid_used, i * 4 * NE + 4 * e + 4 + 2)
                                act.wait_ge(eo_turned, i * 2 * NE + 2 * e)
                                nc.scalar.activation(eo[:], ps_o, ACT.Identity,
                                                     bias=col("mlp_b2", e)).then_inc(eo_ready, 1)
                                for s in range(L0, SLABS):
                                    tanh(e, s)
                                if e + 1 < NE:
                                    for s in range(LOOK):
                                        tanh(e + 1, s)
                                act.wait_ge(slab_used, i * NE * SLABS + (e + 1) * SLABS + RING)
                                act.wait_ge(eo_turned, i * 2 * NE + 2 * e + 1)
                                nc.scalar.activation(eo[:], ps_o, ACT.Identity, bias=o_bias[:, e:e + 1],
                                                     scale=-1.0).then_inc(eo_ready, 1)

                    @block.tensor
                    def _(pe):
                        pe.sem_inc(slab_used, RING)
                        pe.sem_inc(hid_used, 2)
                        with pe.Fori(0, NT) as i:
                            pe.wait_ge(norm_ready, i * 2 + 1)
                            pe.wait_ge(acc_done, i * 2 * NE)
                            for c in range(TC):
                                last = nc.tensor.transpose(ps_ht[:, c], a_tok[:, c], ident[:])
                            last.then_inc(norm_turned, 1)
                            pe.wait_ge(norm_ready, i * 2 + 2)
                            pe.wait_ge(eo_ready, i * 2 * NE)
                            for c in range(TC):
                                last = nc.tensor.transpose(ps_ot[:, c], n_tok[:, c], ident[:])
                            last.then_inc(norm_turned, 1)
                            pe.wait_ge(a_t_ready, i + 1)
                            for c in range(TC):
                                last = nc.tensor.matmul(ps_logit[:, c], a_t[:, c * P:(c + 1) * P],
                                                        col("gate", 0, 8), start=True, stop=True)
                            last.then_inc(logits_done, 1)
                            pe.wait_ge(shifted, i + 1)
                            pe.wait_ge(n_t_ready, i + 1)

                            def slab(e, s):
                                k = e * SLABS + s
                                pe.wait_ge(basis_ready, i * NE * SLABS + k + 1)
                                for m in range(2 if s < L0 else 1):
                                    for b in range(2):
                                        rhs = ring[:, k % RING, b * BANK:(b + 1) * BANK]
                                        if s < L0:
                                            last = nc.tensor.matmul(psum[:, 2 * m + b], w0[:, e, s, m * P:(m + 1) * P],
                                                                    rhs, start=(s == 0), stop=(s == L0 - 1))
                                        else:
                                            q, g = divmod(s - L0, NG)
                                            last = nc.tensor.matmul(psum[:, 6 + b], w1[:, e, q, g, :], rhs,
                                                                    start=(s == L0), stop=(s == SLABS - 1))
                                last.then_inc(slab_used, 1)

                            def mlp_up(e, j):
                                if j:
                                    pe.wait_ge(gelu_done, i * 4 * NE + 4 * e + j)
                                else:
                                    pe.wait_ge(acc_done, i * 2 * NE + 2 * e)
                                for b in range(2):
                                    last = nc.tensor.matmul(psum[:, 4 + b], mw1[:, e, j * P:(j + 1) * P],
                                                            a_t[:, b * BANK:(b + 1) * BANK], start=True, stop=True)
                                last.then_inc(hid_done, 1)

                            def mlp_down(e, j):
                                pe.wait_ge(gelu_done, i * 4 * NE + 4 * e + j + 1)
                                if j == 0:
                                    pe.wait_ge(eo_ready, i * 2 * NE + 2 * e)
                                for b in range(2):
                                    last = nc.tensor.matmul(psum[:, 6 + b], mw2[:, e, j, :],
                                                            hid[:, j % 2, b * BANK:(b + 1) * BANK],
                                                            start=(j == 0), stop=(j == 3))
                                last.then_inc(hid_used, 1)

                            def turn_out(e, kan):
                                n = 2 * e + kan
                                pe.wait_ge(eo_ready, i * 2 * NE + n + 1)
                                pe.wait_ge(acc_done, i * 2 * NE + n)
                                for c in range(TC):
                                    last = nc.tensor.transpose(ps_ht[:, c], eo[:, c * P:(c + 1) * P], ident[:])
                                last.then_inc(eo_turned, 1)

                            for e in range(NE):
                                pe.wait_ge(zc_ready, i * 2 * NE + 2 * e)
                                pe.wait_ge(n1_ready, i * 2 * NE + 2 * e)
                                for s in range(L0):
                                    slab(e, s)
                                if e:
                                    turn_out(e - 1, 1)
                                mlp_up(e, 0)
                                mlp_up(e, 1)
                                mlp_down(e, 0)
                                mlp_up(e, 2)
                                mlp_down(e, 1)
                                mlp_up(e, 3)
                                pe.wait_ge(z_sum_ready, i * NE + e + 1)
                                pe.wait_ge(zc_ready, i * 2 * NE + 2 * e + 2)
                                for c in range(TC):
                                    last = nc.tensor.matmul(psum[:, 0, c:c + 1], z_sq[:, 0, c * P:(c + 1) * P],
                                                            ones[:, 0:1], start=True, stop=True)
                                last.then_inc(z_var_done, 1)
                                mlp_down(e, 2)
                                mlp_down(e, 3)
                                pe.wait_ge(diag_ready, i * NE + e + 1)
                                for b in range(2):
                                    last = nc.tensor.matmul(
                                        psum[:, 2 + b], ones[:],
                                        diag[:, 4 * b:4 * b + 4].rearrange("p c t -> p (c t)"),
                                        start=True, stop=True)
                                last.then_inc(bc_done, 1)
                                pe.wait_ge(eo_ready, i * 2 * NE + 2 * e + 1)
                                for s in range(L0, SLABS):
                                    slab(e, s)
                                    if s == L0 + 3:
                                        turn_out(e, 0)
                            turn_out(NE - 1, 1)

        def retention():
            tmp = ExitStack()
            with tmp:
                def many(name, shape):
                    return [sb(f"{name}_{s}", shape, tmp) for s in range(SLOTS)]

                wq = sb("wq", [P, NL, P], tmp)
                wk = sb("wk", [P, NL, P], tmp)
                wv = sb("wv", [P, NL, P], tmp)
                wg = sb("wg", [P, NL, P], tmp)
                wo = sb("wo", [P, NL, P], tmp)
                wq_rot = sb("wq_rot", [P, NL, P], tmp)
                wk_rot = sb("wk_rot", [P, NL, P], tmp)
                fw1 = sb("fw1", [P, NL, FM], tmp)
                fw2 = sb("fw2", [P, NL, 4, P], tmp)
                b2_rows = sb("b2_rows", [P, NL, P], tmp)
                cos_q = sb("cos_q", [P, S], tmp)
                sin_q = sb("sin_q", [P, S], tmp)
                cos_k = sb("cos_k", [P, S], tmp)
                sin_k = sb("sin_k", [P, S], tmp)
                decay_q = sb("decay_q", [P, P], tmp)
                decay_k = sb("decay_k", [P, P], tmp)
                decay_qk = sb("decay_qk", [P, NH, P], tmp)
                same_head = sb("same_head", [P, P], tmp)

                u = many("u", [P, NC, P])
                row = many("row", [P, NC, P])
                col_in = many("col_in", [P, S])
                q = many("q", [P, S])
                qd = many("qd", [P, S])
                k = many("k", [P, S])
                part = many("part", [P, S])
                v = many("v", [P, NC, P])
                kd = many("kd", [P, NC, P])
                gate = many("gate", [P, S])
                big = many("big", [P, 4, S])
                state = many("state", [P, NC, P])
                stats = many("r_stats", [P, NC, 6])
                mean_var = many("r_mean_var", [P, NC, 2])
                var_eps = many("r_var_eps", [P, NC * NH])
                rstd = many("r_rstd", [P, NC * NH])
                mean = many("r_mean", [P, NC * NH])
                k_head = [b[:, 0:2].rearrange("p a (h t) -> p (a h) t", t=P) for b in big]
                scores = [b[:, 2:4].rearrange("p a (h t) -> p (a h) t", t=P) for b in big]

                def bank(s, n):
                    return psum[:, 4 * s + n]

                def bank_c(s, n):
                    return psum[:, 4 * s + n].rearrange("p (c f) -> p c f", f=P)

                def sems(name):
                    return [sem(f"{name}_{s}") for s in range(SLOTS)]

                r_in = sem("r_in")
                rot_done = sem("rot_done")
                r_step = sem("r_step")
                x_got = sems("x_got")
                x_put = sems("x_put")
                u_ready = sems("u_ready")
                var_asked = sems("r_var_asked")
                rstd_given = sems("r_rstd_given")
                n1_row = sems("n1_row")
                n1_turned = sems("n1_turned")
                n1_col = sems("n1_col")
                q_done = sems("q_done")
                k_done = sems("k_done")
                q_ready = sems("q_ready")
                k_ready = sems("k_ready")
                qd_ready = sems("qd_ready")
                g_done = sems("g_done")
                v_done = sems("v_done")
                kt_done = sems("kt_done")
                g_ready = sems("g_ready")
                v_ready = sems("v_ready")
                kd_ready = sems("kd_ready")
                kh_ready = sems("kh_ready")
                sc_done = sems("sc_done")
                sc_ready = sems("sc_ready")
                kv_done = sems("kv_done")
                state_ready = sems("state_ready")
                y_done = sems("y_done")
                y_row = sems("y_row")
                y_turned = sems("y_turned")
                y_col = sems("y_col")
                gy_ready = sems("gy_ready")
                wo_done = sems("wo_done")
                u2_ready = sems("u2_ready")
                ub_ready = sems("ub_ready")
                n2_row = sems("n2_row")
                n2_turned = sems("n2_turned")
                n2_col = sems("n2_col")
                h_done = sems("h_done")
                h_ready = sems("h_ready")
                w2_done = sems("w2_done")
                ITER = NB // SLOTS
                R_STEPS = SLOTS * (2 + NL * 13)

                with nc.Block() as block:
                    @block.sync
                    def _(sp):
                        n = 0
                        for dst, name in ((wq, "wq"), (wk, "wk"), (wv, "wv"), (wg, "wg"), (wo, "wo"), (fw1, "fw1"),
                                          (fw2, "fw2"), (b2_rows, "b2_rows"), (cos_q, "cos_q"), (sin_q, "sin_q"),
                                          (cos_k, "cos_k"), (sin_k, "sin_k"), (decay_q, "decay_q"),
                                          (decay_k, "decay_k"), (decay_qk, "decay_qk"), (same_head, "same_head")):
                            sp.dma_start(dst[:], A[name]).then_inc(r_in, 16)
                            n += 1
                        assert n == 16
                        sp.wait_ge(r_in, 16 * n)

                    @block.gpsimd
                    def _(pool):
                        pool.wait_ge(r_in, 256)
                        with pool.Fori(0, ITER) as i:
                            def power(s, n):
                                pool.wait_ge(var_asked[s], i * 7 + n)
                                m = NC * NH if n in (3, 6) else NC
                                nc.gpsimd.tensor_tensor(rstd[s][:, 0:m], var_eps[s][:, 0:m], neg_half[:, 0:m],
                                                        ALU.pow).then_inc(rstd_given[s], 1)

                            for s in range(SLOTS):
                                pool.wait_ge(n2_turned[s], i * NL)
                                hold(pool)
                                nc.gpsimd.tensor_copy(row[s][:], x_all[:, bass.ds(i * SLOTS * NC + s * NC, NC), :]
                                                      ).then_inc(x_got[s], 1)
                            for s in range(SLOTS):
                                power(s, 1)
                            for l in range(NL):
                                n = i * NL + l + 1
                                for s in range(SLOTS):
                                    power(s, 2 + 3 * l)
                                for s in range(SLOTS):
                                    pool.wait_ge(q_ready[s], n)
                                    nc.gpsimd.tensor_tensor(
                                        qd[s][:].rearrange("p (c t) -> p c t", t=P),
                                        q[s][:].rearrange("p (c t) -> p c t", t=P),
                                        decay_q[:].unsqueeze(1).to_broadcast([P, NC, P]),
                                        ALU.mult).then_inc(qd_ready[s], 1)
                                for c in range(NC):
                                    for s in range(SLOTS):
                                        if c == 0:
                                            pool.wait_ge(k_ready[s], n)
                                            pool.wait_ge(w2_done[s], n - 1)
                                        else:
                                            pool.wait_ge(sc_done[s], (i * NL + l) * NC + c)
                                        nc.gpsimd.tensor_tensor(
                                            k_head[s], k[s][:, c * P:(c + 1) * P].unsqueeze(1).to_broadcast([P, NH, P]),
                                            col("head_mask", 0, NH).unsqueeze(2).to_broadcast([P, NH, P]),
                                            ALU.mult).then_inc(kh_ready[s], 1)
                                for s in range(SLOTS):
                                    power(s, 3 + 3 * l)
                                for s in range(SLOTS):
                                    pool.wait_ge(u2_ready[s], n)
                                    power(s, 4 + 3 * l)
                                    nc.gpsimd.tensor_tensor(part[s][:].rearrange("p (c f) -> p c f", f=P), u[s][:],
                                                            b2_rows[:, l].unsqueeze(1).to_broadcast([P, NC, P]),
                                                            ALU.add).then_inc(ub_ready[s], 1)
                            for s in range(SLOTS):
                                pool.wait_ge(u_ready[s], (i + 1) * (NL + 1))
                                hold(pool)
                                xs = x_all[:, bass.ds(i * SLOTS * NC + s * NC, NC), :]
                                nc.gpsimd.tensor_tensor(xs, xs, u[s][:], ALU.add).then_inc(x_put[s], 1)
                            for s in range(SLOTS):
                                pool.wait_ge(x_put[s], i + 1)

                    @block.vector
                    def _(dve):
                        dve.wait_ge(r_in, 256)
                        for w, w_rot in ((wq, wq_rot), (wk, wk_rot)):
                            pairs = w[:].rearrange("p l (n two) -> p l n two", two=2)
                            rot = w_rot[:].rearrange("p l (n two) -> p l n two", two=2)
                            nc.vector.tensor_scalar(rot[:, :, :, 0], pairs[:, :, :, 1], -1.0, None,
                                                    ALU.mult).then_inc(rot_done, 1)
                            nc.vector.tensor_copy(rot[:, :, :, 1], pairs[:, :, :, 0]).then_inc(rot_done, 1)
                        with dve.Fori(0, ITER) as i:
                            done = [0]

                            def step(ins):
                                done[0] += 1
                                ins.then_inc(r_step, 1)
                                dve.wait_ge(r_step, i * R_STEPS + done[0])

                            def normalise(s, dst, src, n, ready, value):
                                for c in range(NC):
                                    last = nc.vector.bn_stats(stats[s][:, c], src[:, c])
                                step(last)
                                hold(dve)
                                for c in range(NC):
                                    last = nc.vector.bn_aggr(mean_var[s][:, c], stats[s][:, c])
                                step(last)
                                nc.vector.tensor_scalar(var_eps[s][:, 0:NC], mean_var[s][:, :, 1], EPS, None,
                                                        ALU.add).then_inc(var_asked[s], 1)

                                def rest():
                                    dve.wait_ge(rstd_given[s], i * 7 + n)
                                    for c in range(NC):
                                        last = nc.vector.tensor_scalar(dst[:, c], src[:, c], mean_var[s][:, c, 0:1],
                                                                       rstd[s][:, c:c + 1], ALU.subtract, ALU.mult)
                                    last.then_inc(ready, 1)
                                    dve.wait_ge(ready, value)
                                return rest

                            def both(f):
                                rests = [f(s) for s in range(SLOTS)]
                                for r in rests:
                                    r()

                            def first(s):
                                dve.wait_ge(x_got[s], i + 1)
                                dve.wait_ge(x_put[s], i)
                                return normalise(s, u[s], row[s], 1, u_ready[s], i * (NL + 1) + 1)

                            both(first)
                            for l in range(NL):
                                n = i * NL + l + 1
                                both(lambda s: normalise(s, row[s], u[s], 2 + 3 * l, n1_row[s], n))
                                for s in range(SLOTS):
                                    dve.wait_ge(q_done[s], n)
                                    nc.vector.tensor_tensor(part[s][:], bank(s, 1), cos_q[:], ALU.mult)
                                    step(nc.vector.tensor_tensor(q[s][:], bank(s, 2), sin_q[:], ALU.mult))
                                    nc.vector.tensor_tensor(q[s][:], q[s][:], part[s][:], ALU.add
                                                            ).then_inc(q_ready[s], 1)
                                    dve.wait_ge(q_ready[s], n)
                                    dve.wait_ge(k_done[s], n)
                                    nc.vector.tensor_tensor(part[s][:], bank(s, 3), cos_k[:], ALU.mult)
                                    step(nc.vector.tensor_tensor(k[s][:], bank(s, 0), sin_k[:], ALU.mult))
                                    nc.vector.tensor_tensor(k[s][:], k[s][:], part[s][:], ALU.add
                                                            ).then_inc(k_ready[s], 1)
                                for s in range(SLOTS):
                                    dve.wait_ge(kt_done[s], n)
                                    nc.vector.tensor_tensor(kd[s][:], bank_c(s, 3),
                                                            decay_k[:].unsqueeze(1).to_broadcast([P, NC, P]),
                                                            ALU.mult).then_inc(kd_ready[s], 1)

                                def decay(s, c):
                                    at = (i * NL + l) * NC + c
                                    dve.wait_ge(sc_done[s], at + 1)
                                    dve.wait_ge(y_done[s], at)
                                    nc.vector.tensor_tensor(
                                        scores[s], psum[:, 4 * s:4 * s + 2].rearrange("p a (h t) -> p (a h) t", t=P),
                                        decay_qk[:], ALU.mult).then_inc(sc_ready[s], 1)

                                for s in range(SLOTS):
                                    decay(s, 0)
                                for s in range(SLOTS):
                                    dve.wait_ge(kv_done[s], n)
                                    step(nc.vector.tensor_tensor(state[s][:, 1:4], bank_c(s, 2)[:, 0:3],
                                                                 same_head[:].unsqueeze(1).to_broadcast([P, 3, P]),
                                                                 ALU.mult))
                                    step(nc.vector.scalar_tensor_tensor(
                                        out=state[s][:, 2], in0=state[s][:, 1], scalar=col("decay_chunk"),
                                        in1=state[s][:, 2], op0=ALU.mult, op1=ALU.add))
                                    nc.vector.scalar_tensor_tensor(
                                        out=state[s][:, 3], in0=state[s][:, 2], scalar=col("decay_chunk"),
                                        in1=state[s][:, 3], op0=ALU.mult, op1=ALU.add).then_inc(state_ready[s], 1)
                                for c in range(1, NC):
                                    for s in range(SLOTS):
                                        decay(s, c)

                                def group_norm(s):
                                    dve.wait_ge(y_done[s], n * NC)
                                    y = bank(s, 3).rearrange("p (g f) -> p g f", f=HD)
                                    yc = row[s][:].rearrange("p c (h f) -> p (c h) f", f=HD)
                                    sq = part[s][:].rearrange("p (g f) -> p g f", f=HD)
                                    step(nc.vector.tensor_reduce(mean[s][:], y, AX_X, ALU.add))
                                    step(nc.vector.tensor_scalar(mean[s][:], mean[s][:], 1.0 / HD, None, ALU.mult))
                                    step(nc.vector.tensor_tensor(
                                        yc, y, mean[s][:].unsqueeze(2).to_broadcast([P, NC * NH, HD]), ALU.subtract))
                                    step(nc.vector.tensor_tensor(sq, yc, yc, ALU.mult))
                                    step(nc.vector.tensor_reduce(var_eps[s][:], sq, AX_X, ALU.add))
                                    nc.vector.tensor_scalar(var_eps[s][:], var_eps[s][:], 1.0 / HD, EPS, ALU.mult,
                                                            ALU.add).then_inc(var_asked[s], 1)

                                    def rest():
                                        dve.wait_ge(rstd_given[s], i * 7 + 3 + 3 * l)
                                        nc.vector.tensor_tensor(
                                            yc, yc, rstd[s][:].unsqueeze(2).to_broadcast([P, NC * NH, HD]),
                                            ALU.mult).then_inc(y_row[s], 1)
                                    return rest

                                both(group_norm)
                                for s in range(SLOTS):
                                    dve.wait_ge(y_col[s], n)
                                    dve.wait_ge(g_ready[s], n)
                                    nc.vector.tensor_tensor(col_in[s][:], col_in[s][:], gate[s][:], ALU.mult
                                                            ).then_inc(gy_ready[s], 1)

                                def second(s):
                                    dve.wait_ge(wo_done[s], n)
                                    nc.vector.tensor_tensor(u[s][:], bank_c(s, 1), u[s][:], ALU.add
                                                            ).then_inc(u2_ready[s], 1)
                                    dve.wait_ge(u2_ready[s], n)
                                    dve.wait_ge(y_turned[s], n)
                                    return normalise(s, row[s], u[s], 4 + 3 * l, n2_row[s], n)

                                both(second)
                                for s in range(SLOTS):
                                    dve.wait_ge(w2_done[s], n)
                                    dve.wait_ge(ub_ready[s], n)
                                    nc.vector.tensor_tensor(u[s][:], bank_c(s, 3),
                                                            part[s][:].rearrange("p (c f) -> p c f", f=P), ALU.add
                                                            ).then_inc(u_ready[s], 1)
                                    dve.wait_ge(u_ready[s], i * (NL + 1) + l + 2)
                            assert done[0] == R_STEPS, done

                    @block.scalar
                    def _(act):
                        act.wait_ge(r_in, 256)
                        with act.Fori(0, ITER) as i:
                            for l in range(NL):
                                n = i * NL + l + 1
                                for s in range(SLOTS):
                                    act.wait_ge(n1_turned[s], n)
                                    nc.scalar.activation(col_in[s][:], bank(s, 0), ACT.Identity, bias=col("ln1_b", l),
                                                         scale=col("ln1_w", l)).then_inc(n1_col[s], 1)
                                for s in range(SLOTS):
                                    act.wait_ge(g_done[s], n)
                                    nc.scalar.activation(gate[s][:], bank(s, 1), ACT.Silu).then_inc(g_ready[s], 1)
                                    act.wait_ge(v_done[s], n)
                                    nc.scalar.activation(v[s][:], bank_c(s, 2), ACT.Copy).then_inc(v_ready[s], 1)
                                for s in range(SLOTS):
                                    act.wait_ge(y_turned[s], n)
                                    nc.scalar.activation(col_in[s][:], bank(s, 0), ACT.Identity, bias=col("gn_b", l),
                                                         scale=col("gn_w", l)).then_inc(y_col[s], 1)
                                for s in range(SLOTS):
                                    act.wait_ge(n2_turned[s], n)
                                    nc.scalar.activation(col_in[s][:], bank(s, 2), ACT.Identity, bias=col("ln2_b", l),
                                                         scale=col("ln2_w", l)).then_inc(n2_col[s], 1)
                                for j in range(4):
                                    for s in range(SLOTS):
                                        act.wait_ge(h_done[s], (i * NL + l) * 4 + j + 1)
                                        nc.scalar.activation(big[s][:, j], bank(s, j % 3), ACT.Silu,
                                                             bias=col("ffn_b1", 4 * l + j)).then_inc(h_ready[s], 1)

                    @block.tensor
                    def _(pe):
                        pe.wait_ge(r_in, 256)
                        pe.wait_ge(rot_done, 4)
                        with pe.Fori(0, ITER) as i:
                            def turn(dst, src, done_sem):
                                for c in range(NC):
                                    last = nc.tensor.transpose(dst[:, c], src[:, c], ident[:])
                                last.then_inc(done_sem, 1)

                            def product(dst, w, rhs):
                                return nc.tensor.matmul(dst, w, rhs, start=True, stop=True)

                            for l in range(NL):
                                n = i * NL + l + 1
                                at = (i * NL + l) * NC
                                for s in range(SLOTS):
                                    pe.wait_ge(n1_row[s], n)
                                    pe.wait_ge(h_ready[s], at)
                                    turn(bank_c(s, 0), row[s], n1_turned[s])
                                for s in range(SLOTS):
                                    pe.wait_ge(n1_col[s], n)
                                    product(bank(s, 1), wq[:, l], col_in[s][:])
                                    product(bank(s, 2), wq_rot[:, l], col_in[s][:]).then_inc(q_done[s], 1)
                                    pe.wait_ge(u_ready[s], i * (NL + 1) + l + 1)
                                    product(bank(s, 3), wk[:, l], col_in[s][:])
                                    product(bank(s, 0), wk_rot[:, l], col_in[s][:]).then_inc(k_done[s], 1)
                                for s in range(SLOTS):
                                    pe.wait_ge(q_ready[s], n)
                                    product(bank(s, 1), wg[:, l], col_in[s][:]).then_inc(g_done[s], 1)
                                    for c in range(NC):
                                        last = product(bank_c(s, 2)[:, c], col_in[s][:, c * P:(c + 1) * P], wv[:, l])
                                    last.then_inc(v_done[s], 1)
                                    pe.wait_ge(k_ready[s], n)
                                    turn(bank_c(s, 3), k[s][:].rearrange("p (c t) -> p c t", t=P), kt_done[s])

                                def score(s, c):
                                    pe.wait_ge(kh_ready[s], at + c + 1)
                                    if c == 0:
                                        pe.wait_ge(g_ready[s], n)
                                    else:
                                        pe.wait_ge(sc_ready[s], at + c)
                                    for h in range(NH):
                                        last = product(bank_c(s, h // 4)[:, h % 4], k_head[s][:, h],
                                                       q[s][:, c * P:(c + 1) * P])
                                    last.then_inc(sc_done[s], 1)

                                def output(s, c):
                                    pe.wait_ge(sc_ready[s], at + c + 1)
                                    if c == 0:
                                        pe.wait_ge(kd_ready[s], n)
                                    if c == 1:
                                        pe.wait_ge(state_ready[s], n)
                                        pe.wait_ge(qd_ready[s], n)
                                    dst = bank_c(s, 3)[:, c]
                                    if c:
                                        nc.tensor.matmul(dst, qd[s][:, c * P:(c + 1) * P], state[s][:, c],
                                                         start=True, stop=False, skip_group_check=True)
                                    for h in range(NH):
                                        last = nc.tensor.matmul(dst[:, h * HD:(h + 1) * HD], scores[s][:, h],
                                                                v[s][:, c, h * HD:(h + 1) * HD],
                                                                start=(c == 0 and h == 0), stop=(h == NH - 1),
                                                                skip_group_check=True)
                                    last.then_inc(y_done[s], 1)

                                for s in range(SLOTS):
                                    score(s, 0)
                                for s in range(SLOTS):
                                    pe.wait_ge(v_ready[s], n)
                                    pe.wait_ge(kd_ready[s], n)
                                    for c in range(NC - 1):
                                        last = product(bank_c(s, 2)[:, c], kd[s][:, c], v[s][:, c])
                                    last.then_inc(kv_done[s], 1)
                                for c in range(1, NC):
                                    for s in range(SLOTS):
                                        score(s, c)
                                    for s in range(SLOTS):
                                        output(s, c - 1)
                                for s in range(SLOTS):
                                    output(s, NC - 1)
                                for s in range(SLOTS):
                                    pe.wait_ge(y_row[s], n)
                                    turn(bank_c(s, 0), row[s], y_turned[s])
                                for s in range(SLOTS):
                                    pe.wait_ge(gy_ready[s], n)
                                    for c in range(NC):
                                        last = product(bank_c(s, 1)[:, c], col_in[s][:, c * P:(c + 1) * P], wo[:, l])
                                    last.then_inc(wo_done[s], 1)
                                for s in range(SLOTS):
                                    pe.wait_ge(n2_row[s], n)
                                    turn(bank_c(s, 2), row[s], n2_turned[s])
                                for j in range(4):
                                    for s in range(SLOTS):
                                        if j == 0:
                                            pe.wait_ge(n2_col[s], n)
                                        if j == 3:
                                            pe.wait_ge(h_ready[s], at + 1)
                                        product(bank(s, j % 3), fw1[:, l, j * P:(j + 1) * P],
                                                col_in[s][:]).then_inc(h_done[s], 1)
                                for s in range(SLOTS):
                                    for c in range(NC):
                                        for j in range(4):
                                            if c == 0:
                                                pe.wait_ge(h_ready[s], at + j + 1)
                                            last = nc.tensor.matmul(bank_c(s, 3)[:, c],
                                                                    big[s][:, j, c * P:(c + 1) * P], fw2[:, l, j],
                                                                    start=(j == 0), stop=(j == 3))
                                    last.then_inc(w2_done[s], 1)

        stages = A["stages"]
        if stages >= 1:
            feed_forward("a")
        if stages >= 2:
            retention()
        if stages >= 3:
            feed_forward("b")

        x_out = sem("x_out")
        with nc.Block() as block:
            @block.sync
            def _(sp):
                sp.dma_start(A["out"], x_all[:]).then_inc(x_out, 16)
                sp.wait_ge(x_out, 16)


def constants():
    half = HD // 2
    scale_vec = (np.arange(0, HD, 2) + 0.4 * HD) / (1.4 * HD)
    scale = scale_vec[None, :] ** (np.arange(S, dtype=np.float64) / 64)[:, None]
    ang = np.arange(S, dtype=np.float64)[:, None] / 10000.0 ** (np.arange(half, dtype=np.float64) / half)[None, :]
    sin, cos = np.sin(ang), np.cos(ang)
    gammas = 1.0 - np.exp(np.linspace(np.log(1.0 / 32), np.log(1.0 / 64), NH))
    head = np.arange(P) // HD
    t = np.arange(P)

    def by_feature(m):
        return np.ascontiguousarray(np.tile(np.repeat(m, 2, axis=-1).T, (NH, 1)).astype(np.float32))

    diff = t[None, :] - t[:, None]
    decay = np.where(diff[None] >= 0, gammas[:, None, None] ** np.maximum(diff, 0)[None], 0.0)
    return {
        "ident": np.eye(P, dtype=np.float32),
        "tril": np.ascontiguousarray(np.broadcast_to(np.tril(np.ones((8, 8), np.float32), -1), (P, 8, 8))),
        "cos_q": by_feature(cos * scale), "sin_q": by_feature(sin * scale),
        "cos_k": by_feature(cos / scale), "sin_k": by_feature(sin / scale),
        "decay_q": (gammas[head][:, None] ** t[None, :]).astype(np.float32),
        "decay_k": (gammas[head][None, :] ** (P - t)[:, None]).astype(np.float32),
        "decay_qk": np.ascontiguousarray(decay.transpose(1, 0, 2).astype(np.float32)),
        "same_head": (head[:, None] == head[None, :]).astype(np.float32),
        "neg_half_grid": np.ascontiguousarray(np.broadcast_to(NEG_HALF_GRID, (P, NG))),
        "head_mask": (head[:, None] == np.arange(NH)[None, :]).astype(np.float32),
        "decay_chunk": (gammas[head] ** P).astype(np.float32)[:, None],
    }


STAGES = 3


def kernel(**inputs):
    import concourse.bacc as _bacc
    from concourse.bass_utils import run_bass_kernel_spmd as _run

    a = {k.replace("L0_attn_", "").replace("L0_ffn_", "f_"): np.asarray(v) for k, v in inputs.items()}
    con = constants()
    vectors = {
        "gate": a["f_gate_W"], "kan_g0": a["f_kan_ln_g0"].T, "kan_b0": a["f_kan_ln_b0"].T,
        "kan_g1": a["f_kan_ln_g1"].reshape(2 * NE, P).T, "kan_b1": a["f_kan_ln_b1"].reshape(2 * NE, P).T,
        "mlp_b1": a["f_mlp_b1"].reshape(4 * NE, P).T, "mlp_b2": a["f_mlp_b2"].T,
        "ln1_w": a["ln1_w"].T, "ln1_b": a["ln1_b"].T, "ln2_w": a["ln2_w"].T, "ln2_b": a["ln2_b"].T,
        "gn_w": a["gn_w"].T, "gn_b": a["gn_b"].T, "ffn_b1": a["ffn_b1"].reshape(4 * NL, P).T,
        "neg_half_grid": con.pop("neg_half_grid"), "head_mask": con.pop("head_mask"),
        "decay_chunk": con.pop("decay_chunk"),
    }
    arrays = {
        "x": a["X"].reshape(NB * NC, P, P).transpose(1, 0, 2),
        "cols": np.concatenate([vectors[k] for k in COLS], axis=1),
        "kan_rows": np.concatenate([a["f_kan_sl_b0"], a["f_kan_sl_b1"]], axis=1)[None],
        "w0": a["f_kan_sl_W0"].reshape(NE, P, NG, F2).transpose(1, 0, 2, 3),
        "w1": a["f_kan_sl_W1"].reshape(NE, 2, P, NG, P).transpose(2, 0, 1, 3, 4),
        "mw1": a["f_mlp_W1"].transpose(1, 0, 2),
        "mw2": a["f_mlp_W2"].reshape(NE, 4, P, P).transpose(2, 0, 1, 3),
        "wq": a["WQ"].transpose(2, 0, 1, 3).reshape(P, NL, P),
        "wk": a["WK"].transpose(2, 0, 1, 3).reshape(P, NL, P),
        "wv": a["WV"].transpose(2, 0, 1, 3).reshape(P, NL, P),
        "wg": a["WG"].transpose(1, 0, 2),
        "wo": a["WO"].transpose(1, 0, 2),
        "fw1": a["ffn_w1"].transpose(1, 0, 2),
        "fw2": a["ffn_w2"].reshape(NL, 4, P, P).transpose(2, 0, 1, 3),
        "b2_rows": np.broadcast_to(a["ffn_b2"][None], (P, NL, P)),
        **con,
    }
    nc = _bacc.Bacc("TRN2", target_bir_lowering=False, num_devices=1)
    arrays = {f"in_{k}": np.ascontiguousarray(v) for k, v in arrays.items()}
    args = {k[3:]: nc.dram_tensor(k, v.shape, F32, kind="ExternalInput").ap() for k, v in arrays.items()}
    args["out"] = nc.dram_tensor("out", (P, NB * NC, P), F32, kind="ExternalOutput").ap()
    args["stages"] = STAGES
    build(nc, args)
    r = _run(nc, [arrays], core_ids=[0])
    got = r.results[0]["out"]
    return np.ascontiguousarray(got.transpose(1, 0, 2)).reshape(NB, S, P)
```

```python
from contextlib import ExitStack

import concourse.bass as bass
import numpy as np
from concourse import mybir

F32 = mybir.dt.float32
F16 = mybir.dt.float16
ACT = mybir.ActivationFunctionType
ALU = mybir.AluOpType
AX_X = mybir.AxisListType.X

P = 128
EPS = 1e-5
NE = 4
NG = 8
FM = 512
F2 = 256
T = 1024
TC = T // P
NT = 4
BANK = 512
RT = 6
RB = 4
L0 = NG
L1 = 2 * NG
SLABS = L0 + L1
TILE_SLABS = NE * SLABS
W_SCALE = 2.0 ** 8
A_SCALE = 2.0 ** 8
H_SCALE = 2.0 ** 6
T_SCALE = 2.0 ** 6
BASIS_UNIT = 1.0 / (T_SCALE * T_SCALE * W_SCALE)
WHOLE = "000" + 5 * "110" + "111111"
OPENING = "-" * 10 + "0" * L0 + "-" * 6
CLOSING = "---" + "1" * L1
PHASE_Q = [L0 + SLABS * e for e in range(NE)]
TURN = 9
UP, GELU, HIDDEN, DOWN = (14, 16, 19, 21), (18, 20, 0, 1), (20, 22, 0, 1), (20, 21, 23, 23)
Z_OUT, Z_SUM, VAR, Z_VAR, DIAG, BROADCAST, N1 = 23, 23, 20, 23, 0, 22, 2
OUTPUTS, TURN_KAN, ADD_KAN, TURN_MLP, ADD_MLP = 2, 3, 7, 6, 10
TURN_A, A_PARTS = 9, 13
EXPS, CHOOSE, GIVE, STORE = (0, 3), (0, 4), (0, 8), (0, 8)
COPY_X, STATS_A, NORM_A, STATS_N, NORM_N = (0, 12), (1, 4), (1, 8), (1, 11), (1, 15)
TURN_N, N_TURN_OUT, N_COPY = (2, 10), (2, 13), (2, 19)
OFF_ACT = (6, 15)
HIGH_ON_POOL = (5, 10, 15)
NL = 2
NH = 8
HD = P // NH
S = 512
NC = S // P
NB = 8
SLOTS = 2
NEG_HALF_GRID = -0.5 * np.linspace(-1.2, 0.2, NG).astype(np.float32)



def on_act(q):
    return (q - L0) % SLABS not in OFF_ACT


def on_dve(q):
    return not on_act(q)


def high_on_pool(q):
    return (q - L0) % SLABS in HIGH_ON_POOL


def high_on_dve(q):
    return not high_on_pool(q)


def count(kind, q):
    return sum(kind(r) for r in range(q))


def steps(order, e, start=0, stop=None):
    q, done = PHASE_Q[e] + (SLABS - L0 if order == OPENING else 0), [0, 0]
    for p, layer in enumerate(order):
        slab = None
        if layer != "-":
            layer = int(layer)
            slab = (q, layer, done[layer])
            q += 1
            done[layer] += 1
        if p >= start and (stop is None or p < stop):
            yield p, slab


def last_l0(order, e):
    return [slab[0] for _, slab in steps(order, e) if slab and slab[1] == 0][-1]


COLS = {}
_at = 0
for _name, _n in (("gate", 8), ("kan_g0", NE), ("kan_b0", NE), ("kan_g1", 2 * NE), ("kan_b1", 2 * NE),
                  ("mlp_b1", 4 * NE), ("mlp_b2", NE), ("ln1_w", NL), ("ln1_b", NL), ("ln2_w", NL), ("ln2_b", NL),
                  ("gn_w", NL), ("gn_b", NL), ("ffn_b1", 4 * NL), ("neg_half_grid", NG), ("head_mask", NH),
                  ("decay_chunk", 1)):
    COLS[_name] = (_at, _at + _n)
    _at += _n
NCOLS = _at


def build(nc, A):
    ctx = ExitStack()
    with ctx:
        def sb(name, shape, stack=ctx, dtype=F32):
            return stack.enter_context(nc.sbuf_tensor(name, shape, dtype))

        def sem(name):
            return ctx.enter_context(nc.semaphore(name))

        small_in = sem("small_in")

        x_all = sb("x_all", [P, NB * NC, P])
        cols = sb("cols", [P, NCOLS])
        ident = sb("ident", [P, P])
        ones = sb("ones", [P, P])
        neg_half = sb("neg_half", [P, 64])
        idle = sb("idle", [P, 96])
        idle_word = iter(range(32, 96))
        tril = sb("tril", [P, 8, 8])
        w0_h, w0_l = (sb(f"w0_{part}", [P, NE, NG, F2], dtype=F16) for part in "hl")
        w1_h, w1_l = (sb(f"w1_{part}", [P, NE, 2, NG, P], dtype=F16) for part in "hl")
        mw1_h, mw1_l = (sb(f"mw1_{part}", [P, NE * FM], dtype=F16)[:] for part in "hl")
        mw2_h, mw2_l = (sb(f"mw2_{part}", [P, NE * 4 * P], dtype=F16)[:] for part in "hl")
        gate_h, gate_l = (sb(f"gate_{part}", [P, 8], dtype=F16) for part in "hl")
        z_bias = sb("z_bias", [P, NE, 2])
        o_bias = sb("o_bias", [P, NE])
        scale0 = sb("scale0", [P, NE])
        bias0 = sb("bias0", [P, NE, NG])
        scale1 = sb("scale1", [P, 2 * NE])
        bias1 = sb("bias1", [P, 2 * NE, NG])
        psum = ctx.enter_context(nc.psum_tensor("psum", [P, 8, BANK], F32))

        def hold(eng, k=None):
            k = next(idle_word) if k is None else k % 32
            if eng is nc.vector:
                nc.vector.memset(idle[:, k:k + 1], 0.0)
            else:
                nc.gpsimd.tensor_tensor(idle[:, k:k + 1], neg_half[:, 0:1], neg_half[:, 1:2], ALU.add)

        def col(name, i=0, n=1):
            a = COLS[name][0] + i
            return cols[:, a:a + n]

        with ExitStack() as tmp:
            kan_rows = sb("kan_rows", [1, NE, F2 + P], tmp)
            row_mean = sb("row_mean", [P, NE, NG], tmp)
            bias_mean = sb("bias_mean", [1, NE], tmp)
            w0_raw = sb("w0_raw", [P, 2, NG * F2], tmp)
            w1_raw = sb("w1_raw", [P, 2, 2 * NG * P], tmp)
            mw1_raw = sb("mw1_raw", [P, NE * FM], tmp)
            mw2_raw = sb("mw2_raw", [P, NE * 4 * P], tmp)
            x_in = sem("x_in")
            w0_in = [sem(f"w0_in{e}") for e in range(NE)]
            w1_in = [sem(f"w1_in{e}") for e in range(NE)]
            mlp_in = [sem("mw1_in"), sem("mw2_in")]
            prep_step = sem("prep_step")
            rows_centred = sem("rows_centred")
            w0_centred = sem("w0_centred")
            w0_high = sem("w0_high")
            w0_low = sem("w0_low")
            w0_summed = sem("w0_summed")
            w1_high = sem("w1_high")
            w1_low = sem("w1_low")
            w1_summed = sem("w1_summed")
            other_high = sem("other_high")
            other_low = sem("other_low")
            prep_done = sem("prep_done")
            others = ((mw1_h, mw1_l, mw1_raw), (mw2_h, mw2_l, mw2_raw))

            def flat(w):
                return w.rearrange("p a b -> p (a b)")

            with nc.Block() as block:
                @block.sync
                def _(sp):
                    for dst, src in ((cols[:], A["cols"]), (ident[:], A["ident"]), (tril[:], A["tril"]),
                                     (kan_rows[:], A["kan_rows"])):
                        sp.dma_start(dst, src).then_inc(small_in, 16)
                    for e in range(NE):
                        if e >= 2:
                            sp.wait_ge(w0_low, e - 1)
                            sp.wait_ge(w0_high, e - 1)
                            sp.wait_ge(w0_summed, e - 1)
                            sp.wait_ge(w1_low, e - 1)
                            sp.wait_ge(w1_high, e - 1)
                            sp.wait_ge(w1_summed, e - 1)
                        sp.dma_start(w0_raw[:, e % 2], flat(A["w0"][:, e])).then_inc(w0_in[e], 16)
                        sp.dma_start(w1_raw[:, e % 2], A["w1"][:, e].rearrange("p m g o -> p (m g o)")
                                     ).then_inc(w1_in[e], 16)
                        if e == 1:
                            sp.dma_start(mw1_raw[:], flat(A["mw1"])).then_inc(mlp_in[0], 16)
                            sp.dma_start(mw2_raw[:], A["mw2"].rearrange("p e j o -> p (e j o)")
                                         ).then_inc(mlp_in[1], 16)
                            sp.dma_start(x_all[:], A["x"]).then_inc(x_in, 16)
                    sp.wait_ge(x_in, 16)

                @block.vector
                def _(dve):
                    done = [0]

                    def step(ins):
                        done[0] += 1
                        ins.then_inc(prep_step, 1)
                        dve.wait_ge(prep_step, done[0])

                    def low(dst, raw, high, scale=W_SCALE):
                        return nc.vector.scalar_tensor_tensor(out=dst, in0=raw, scalar=scale, in1=high,
                                                              op0=ALU.mult, op1=ALU.subtract)

                    nc.vector.memset(ones[:], 1.0).then_inc(prep_done, 1)
                    nc.vector.memset(neg_half[:], -0.5).then_inc(prep_done, 1)
                    dve.wait_ge(small_in, 64)
                    nc.vector.tensor_scalar(scale0[:], col("kan_g0", 0, NE), 0.5, None, ALU.mult).then_inc(prep_done, 1)
                    nc.vector.tensor_scalar(scale1[:], col("kan_g1", 0, 2 * NE), 0.5, None,
                                            ALU.mult).then_inc(prep_done, 1)
                    nc.vector.scalar_tensor_tensor(
                        out=bias0[:], in0=col("kan_b0", 0, NE).unsqueeze(2).to_broadcast([P, NE, NG]), scalar=0.5,
                        in1=col("neg_half_grid", 0, NG).unsqueeze(1).to_broadcast([P, NE, NG]),
                        op0=ALU.mult, op1=ALU.add).then_inc(prep_done, 1)
                    nc.vector.scalar_tensor_tensor(
                        out=bias1[:], in0=col("kan_b1", 0, 2 * NE).unsqueeze(2).to_broadcast([P, 2 * NE, NG]),
                        scalar=0.5, in1=col("neg_half_grid", 0, NG).unsqueeze(1).to_broadcast([P, 2 * NE, NG]),
                        op0=ALU.mult, op1=ALU.add).then_inc(prep_done, 1)
                    rows = kan_rows[:, :, 0:F2]
                    step(nc.vector.tensor_reduce(bias_mean[:], rows, AX_X, ALU.add))
                    step(nc.vector.tensor_scalar(bias_mean[:], bias_mean[:], 1.0 / F2, None, ALU.mult))
                    nc.vector.tensor_tensor(rows, rows, bias_mean[:].unsqueeze(2).to_broadcast([1, NE, F2]),
                                            ALU.subtract).then_inc(rows_centred, 1)
                    for e in range(NE):
                        w = w0_raw[:, e % 2].rearrange("p (g o) -> p g o", o=F2)
                        dve.wait_ge(w0_in[e], 16)
                        step(nc.vector.tensor_reduce(row_mean[:, e], w, AX_X, ALU.add))
                        step(nc.vector.tensor_scalar(row_mean[:, e], row_mean[:, e], 1.0 / F2, None, ALU.mult))
                        nc.vector.tensor_tensor(w, w, row_mean[:, e].unsqueeze(2).to_broadcast([P, NG, F2]),
                                                ALU.subtract).then_inc(w0_centred, 1)
                        dve.wait_ge(w1_high, e + 1)
                        low(w1_l[:, e].rearrange("p m g o -> p (m g o)"), w1_raw[:, e % 2],
                            w1_h[:, e].rearrange("p m g o -> p (m g o)")).then_inc(w1_low, 1)
                        dve.wait_ge(w0_centred, e + 1)
                        dve.wait_ge(w0_high, e + 1)
                        low(flat(w0_l[:, e]), w0_raw[:, e % 2], flat(w0_h[:, e])).then_inc(w0_low, 1)
                    dve.wait_ge(other_high, 1)
                    low(gate_l[:], col("gate", 0, 8), gate_h[:]).then_inc(other_low, 1)
                    for n, (high, lower, raw) in enumerate(others):
                        dve.wait_ge(other_high, n + 2)
                        low(lower, raw[:], high).then_inc(other_low, 1)
                    dve.wait_ge(w1_summed, NE)
                    nc.vector.tensor_copy(z_bias[:], psum[:, 0, 0:2 * NE].rearrange("p (e m) -> p e m", m=2)
                                          ).then_inc(prep_done, 1)
                    nc.vector.tensor_copy(o_bias[:], psum[:, 0, 2 * NE:3 * NE]).then_inc(prep_done, 1)
                    dve.wait_ge(prep_done, 8)

                @block.scalar
                def _(act):
                    act.wait_ge(small_in, 64)
                    nc.scalar.activation(gate_h[:], col("gate", 0, 8), ACT.Copy, scale=W_SCALE).then_inc(other_high, 1)
                    for e in range(NE):
                        act.wait_ge(w1_in[e], 16)
                        nc.scalar.activation(w1_h[:, e].rearrange("p m g o -> p (m g o)"), w1_raw[:, e % 2], ACT.Copy,
                                             scale=W_SCALE).then_inc(w1_high, 1)
                        act.wait_ge(w0_centred, e + 1)
                        nc.scalar.activation(flat(w0_h[:, e]), w0_raw[:, e % 2], ACT.Copy,
                                             scale=W_SCALE).then_inc(w0_high, 1)
                    for n, (high, lower, raw) in enumerate(others):
                        act.wait_ge(mlp_in[n], 16)
                        nc.scalar.activation(high, raw[:], ACT.Copy, scale=W_SCALE).then_inc(other_high, 1)

                @block.tensor
                def _(pe):
                    pe.wait_ge(prep_done, 1)
                    pe.wait_ge(rows_centred, 1)
                    for e in range(NE):
                        w = w0_raw[:, e % 2].rearrange("p (g o) -> p g o", o=F2)
                        pe.wait_ge(w0_centred, e + 1)
                        for m in range(2):
                            out = psum[:, 0, 2 * e + m:2 * e + m + 1]
                            for g in range(NG):
                                nc.tensor.matmul(out, w[:, g, m * P:(m + 1) * P], ones[:, 0:1],
                                                 start=(g == 0), stop=False)
                            last = nc.tensor.matmul(out, kan_rows[:, e, m * P:(m + 1) * P], ones[0:1, 0:1],
                                                    start=False, stop=True)
                        last.then_inc(w0_summed, 1)
                        pe.wait_ge(w1_in[e], 16)
                        out = psum[:, 0, 2 * NE + e:2 * NE + e + 1]
                        w = w1_raw[:, e % 2].rearrange("p (m o) -> p m o", o=P)
                        for m in range(2 * NG):
                            nc.tensor.matmul(out, w[:, m], ones[:, 0:1], start=(m == 0), stop=False)
                        last = nc.tensor.matmul(out, kan_rows[:, e, F2:F2 + P], ones[0:1, 0:1],
                                                start=False, stop=True)
                        last.then_inc(w1_summed, 1)

        x_copied = sem("x_copied")
        x_stored = sem("x_stored")
        dve_step = sem("dve_step")
        gate_step = sem("gate_step")
        var_asked = sem("var_asked")
        rstd_given = sem("rstd_given")
        norm_ready = sem("norm_ready")
        a_turned = sem("a_turned")
        n_turned = sem("n_turned")
        a_h_ready = sem("a_h_ready")
        a_l_ready = sem("a_l_ready")
        n_t_ready = sem("n_t_ready")
        logits_done = sem("logits_done")
        shifted = sem("shifted")
        exp_done = sem("exp_done")
        gates_ready = sem("gates_ready")
        tanh_done = sem("tanh_done")
        act_squared = sem("act_squared")
        dve_squared = sem("dve_squared")
        pool_high = sem("pool_high")
        dve_high = sem("dve_high")
        basis_ready = sem("basis_ready")
        slab_used = sem("slab_used")
        hid_done = sem("hid_done")
        gelu_done = sem("gelu_done")
        hid_h_ready = sem("hid_h_ready")
        hid_ready = sem("hid_ready")
        hid_used = sem("hid_used")
        z_sq_ready = sem("z_sq_ready")
        zc_ready = sem("zc_ready")
        z_sum_ready = sem("z_sum_ready")
        z_var_done = sem("z_var_done")
        z_var_ready = sem("z_var_ready")
        z_rstd_ready = sem("z_rstd_ready")
        diag_ready = sem("diag_ready")
        bc_done = sem("bc_done")
        n1_ready = sem("n1_ready")
        mlp_out_ready = sem("mlp_out_ready")
        kan_out_ready = sem("kan_out_ready")
        mlp_turned = sem("mlp_turned")
        kan_turned = sem("kan_turned")
        n_next_ready = sem("n_next_ready")
        acc_done = sem("acc_done")

        def feed_forward(tag, t0):
            tmp = ExitStack()
            with tmp:
                acc = sb(f"acc_{tag}", [P, TC, P], tmp)
                a_tok = sb(f"a_tok_{tag}", [P, TC, P], tmp)
                n_tok = sb(f"n_tok_{tag}", [P, TC, P], tmp)
                a_h = sb(f"a_h_{tag}", [P, T], tmp, F16)
                a_l = sb(f"a_l_{tag}", [P, T], tmp, F16)
                n_t = sb(f"n_t_{tag}", [P, T], tmp)
                stats = sb(f"stats_{tag}", [P, TC, 6], tmp)
                mean_var = sb(f"mean_var_{tag}", [P, TC, 2], tmp)
                var_eps = sb(f"var_eps_{tag}", [P, TC], tmp)
                rstd = sb(f"rstd_{tag}", [P, TC], tmp)
                z_var = sb(f"z_var_{tag}", [P, TC], tmp)
                z_rstd = sb(f"z_rstd_{tag}", [P, TC], tmp)
                top = sb(f"top_{tag}", [P, TC], tmp)
                e_sum = sb(f"e_sum_{tag}", [P, TC], tmp)
                probs = sb(f"probs_{tag}", [P, TC, 8], tmp)
                above = sb(f"above_{tag}", [P, TC, 8, 8], tmp)
                equal = sb(f"equal_{tag}", [P, TC, 8, 8], tmp)
                rank = sb(f"rank_{tag}", [P, TC, 8], tmp)
                next_gates = sb(f"next_gates_{tag}", [P, TC, 8], tmp)
                gates = sb(f"gates_{tag}", [P, TC, 8], tmp)
                tbuf = sb(f"tbuf_{tag}", [P, RT, T], tmp)
                basis_h = sb(f"basis_h_{tag}", [P, RB, T], tmp, F16)
                basis_l = sb(f"basis_l_{tag}", [P, RB, T], tmp, F16)
                hid = sb(f"hid_{tag}", [P, 2, T], tmp)
                hid_h = sb(f"hid_h_{tag}", [P, 2, T], tmp, F16)
                hid_l = sb(f"hid_l_{tag}", [P, 2, T], tmp, F16)
                zc = sb(f"zc_{tag}", [P, 2, T], tmp)
                z_sq = sb(f"z_sq_{tag}", [P, 2, T], tmp)
                diag = z_sq[:, 0].rearrange("p (c t) -> p c t", t=P)
                eo_mlp = sb(f"eo_mlp_{tag}", [P, T], tmp)
                eo_kan = sb(f"eo_kan_{tag}", [P, T], tmp)

                ps_z = psum[:, 0:4].rearrange("p (m b) t -> p m (b t)", m=2)
                ps_mlp = psum[:, 0:2].rearrange("p b t -> p (b t)")
                ps_h = psum[:, 4:6].rearrange("p b t -> p (b t)")
                ps_kan = psum[:, 6:8].rearrange("p b t -> p (b t)")
                ps_turned = psum[:, 4:6].rearrange("p b (c f) -> p (b c) f", f=P)
                ps_bc = psum[:, 2:4].rearrange("p b t -> p (b t)")
                ps_var = psum[:, 2, 0:TC]
                ps_logit = psum[:, 3, 0:8 * TC].rearrange("p (c e) -> p c e", e=8)

                GATE_STEPS = 15
                TILE_ACT = count(on_act, TILE_SLABS)
                TILE_DVE = count(on_dve, TILE_SLABS)
                TILE_HIGH_POOL = count(high_on_pool, TILE_SLABS)
                TILE_HIGH_DVE = count(high_on_dve, TILE_SLABS)

                def passes(engine, phase, finish):
                    phase(t0 - 1, NE - 1, OPENING)
                    phase(t0, 0, WHOLE, 0, TURN, first=True)
                    with engine.Fori(t0, t0 + NT - 1) as i:
                        phase(i, 0, WHOLE, TURN)
                        for e in range(1, NE):
                            phase(i, e, WHOLE)
                        phase(i + 1, 0, WHOLE, 0, TURN)
                    i = t0 + NT - 1
                    phase(i, 0, WHOLE, TURN, last=True)
                    for e in range(1, NE - 1):
                        phase(i, e, WHOLE, last=True)
                    phase(i, NE - 1, CLOSING, last=True)
                    finish(i)

                with nc.Block() as block:
                    @block.gpsimd
                    def _(pool):
                        if t0 == 0:
                            pool.sem_inc(x_stored, 1)

                        def copy_x(i):
                            src = x_all[:, 0:TC] if i is None else x_all[:, bass.ds((i - t0) * TC, TC), :]
                            nc.gpsimd.tensor_copy(a_tok[:], src).then_inc(x_copied, 1)

                        def power(i, n):
                            pool.wait_ge(var_asked, i * 2 + n)
                            nc.gpsimd.tensor_tensor(rstd[:], var_eps[:], neg_half[:, 0:TC],
                                                    ALU.pow).then_inc(rstd_given, 1)

                        def store(i):
                            pool.wait_ge(acc_done, (i + 1) * 2 * NE + 1)
                            hold(pool)
                            xs = x_all[:, bass.ds((i - t0) * TC, TC), :]
                            nc.gpsimd.tensor_tensor(xs, xs, acc[:], ALU.add).then_inc(x_stored, 1)

                        def phase(i, e, order, start=0, stop=None, first=False, last=False):
                            w = i * NE + e + 1
                            for p, slab in steps(order, e, start, stop):
                                if slab and high_on_pool(slab[0]):
                                    q = slab[0]
                                    if on_act(q):
                                        pool.wait_ge(act_squared, i * TILE_ACT + count(on_act, q) + 1)
                                    else:
                                        pool.wait_ge(dve_squared, i * TILE_DVE + count(on_dve, q) + 1)
                                    pool.wait_ge(slab_used, i * TILE_SLABS + q + 1)
                                    hold(pool, q)
                                    nc.gpsimd.tensor_copy(basis_h[:, q % RB], tbuf[:, q % RT]).then_inc(pool_high, 1)
                                if p == Z_SUM and order != CLOSING:
                                    pool.wait_ge(z_sq_ready, 2 * w + 2)
                                    nc.gpsimd.tensor_tensor(z_sq[:, 0], z_sq[:, 0], z_sq[:, 1],
                                                            ALU.add).then_inc(z_sum_ready, 1)
                                    pool.wait_ge(z_var_ready, w + 1)
                                    nc.gpsimd.tensor_tensor(z_rstd[:], z_var[:], neg_half[:, 0:TC],
                                                            ALU.pow).then_inc(z_rstd_ready, 1)
                                if (e, p) == STORE and not first:
                                    store(i - 1)
                                if (e, p) == COPY_X and not last:
                                    pool.wait_ge(a_turned, i + 1)
                                    hold(pool)
                                    copy_x(i + 1)
                                if (e, p) == STATS_A and not last:
                                    power(i + 1, 1)
                                if (e, p) == STATS_N and not last:
                                    power(i + 1, 2)

                        copy_x(None)
                        power(t0, 1)
                        power(t0, 2)
                        passes(pool, phase, store)
                        pool.wait_ge(x_stored, t0 + NT + 1)

                    @block.vector
                    def _(dve):
                        if t0 == 0:
                            dve.sem_inc(basis_ready, RT)
                            dve.sem_inc(hid_ready, 2)
                            dve.sem_inc(n1_ready, 1)
                            dve.sem_inc(acc_done, 1)

                        class Preparation:

                            def __init__(self, i, steps=0):
                                self.i, self.steps = i, steps

                            def step(self, ins):
                                self.steps += 1
                                ins.then_inc(gate_step, 1)
                                dve.wait_ge(gate_step, self.i * GATE_STEPS + self.steps)

                            def row_stats(self, n):
                                if n == 1:
                                    dve.wait_ge(x_copied, self.i + 1)
                                    hold(dve)
                                for c in range(TC):
                                    last = nc.vector.bn_stats(stats[:, c], a_tok[:, c])
                                self.step(last)
                                hold(dve)
                                for c in range(TC):
                                    last = nc.vector.bn_aggr(mean_var[:, c], stats[:, c])
                                self.step(last)
                                nc.vector.tensor_scalar(var_eps[:], mean_var[:, :, 1], EPS, None,
                                                        ALU.add).then_inc(var_asked, 1)

                            def row_norm(self, n):
                                dve.wait_ge(rstd_given, self.i * 2 + n)
                                dst = a_tok if n == 1 else n_tok
                                for c in range(TC):
                                    last = nc.vector.tensor_scalar(dst[:, c], a_tok[:, c], mean_var[:, c, 0:1],
                                                                   rstd[:, c:c + 1], ALU.subtract, ALU.mult)
                                last.then_inc(norm_ready, 1)
                                if n == 1:
                                    dve.wait_ge(norm_ready, self.i * 2 + 1)

                            def a_low(self):
                                dve.wait_ge(a_h_ready, self.i + 1)
                                nc.vector.scalar_tensor_tensor(out=a_l[:], in0=ps_h, scalar=A_SCALE, in1=a_h[:],
                                                               op0=ALU.mult, op1=ALU.subtract).then_inc(a_l_ready, 1)

                            def logits(self):
                                dve.wait_ge(logits_done, self.i + 1)
                                self.step(nc.vector.tensor_reduce(top[:], ps_logit, AX_X, ALU.max))
                                nc.vector.tensor_tensor(probs[:], ps_logit,
                                                        top[:].unsqueeze(2).to_broadcast([P, TC, 8]),
                                                        ALU.subtract).then_inc(shifted, 1)

                            def choose(self):
                                dve.wait_ge(exp_done, self.i + 1)
                                step = self.step
                                step(nc.vector.tensor_reduce(e_sum[:], probs[:], AX_X, ALU.add))
                                step(nc.vector.reciprocal(e_sum[:], e_sum[:]))
                                step(nc.vector.tensor_tensor(probs[:], probs[:],
                                                             e_sum[:].unsqueeze(2).to_broadcast([P, TC, 8]),
                                                             ALU.mult))
                                pj = probs[:].unsqueeze(2).to_broadcast([P, TC, 8, 8])
                                pi = probs[:].unsqueeze(3).to_broadcast([P, TC, 8, 8])
                                nc.vector.tensor_tensor(above[:], pj, pi, ALU.is_gt)
                                step(nc.vector.tensor_tensor(equal[:], pj, pi, ALU.is_equal))
                                step(nc.vector.tensor_tensor(equal[:], equal[:],
                                                             tril[:].unsqueeze(1).to_broadcast([P, TC, 8, 8]),
                                                             ALU.mult))
                                step(nc.vector.tensor_tensor(above[:], above[:], equal[:], ALU.add))
                                step(nc.vector.tensor_reduce(rank[:], above[:], AX_X, ALU.add))
                                step(nc.vector.scalar_tensor_tensor(out=next_gates[:], in0=rank[:], scalar=1.5,
                                                                    in1=probs[:], op0=ALU.is_lt, op1=ALU.mult))
                                step(nc.vector.tensor_reduce(e_sum[:], next_gates[:], AX_X, ALU.add))
                                step(nc.vector.reciprocal(e_sum[:], e_sum[:]))
                                assert self.steps == GATE_STEPS, self.steps

                            def give(self):
                                nc.vector.scalar_tensor_tensor(
                                    out=gates[:], in0=next_gates[:], scalar=0.5,
                                    in1=e_sum[:].unsqueeze(2).to_broadcast([P, TC, 8]), op0=ALU.mult,
                                    op1=ALU.mult).then_inc(gates_ready, 1)
                                dve.wait_ge(gates_ready, self.i + 1)

                        def square(i, q):
                            dve.wait_ge(tanh_done, i * TILE_SLABS + q + 1)
                            t = tbuf[:, q % RT]
                            nc.vector.scalar_tensor_tensor(out=t, in0=t, scalar=T_SCALE * T_SCALE, in1=t,
                                                           op0=ALU.mult, op1=ALU.mult).then_inc(dve_squared, 1)

                        def high(i, q):
                            if high_on_pool(q):
                                return
                            if on_act(q):
                                dve.wait_ge(act_squared, i * TILE_ACT + count(on_act, q) + 1)
                            else:
                                dve.wait_ge(dve_squared, i * TILE_DVE + count(on_dve, q) + 1)
                            dve.wait_ge(slab_used, i * TILE_SLABS + q + 1)
                            nc.vector.tensor_copy(basis_h[:, q % RB], tbuf[:, q % RT]).then_inc(dve_high, 1)

                        def low(i, q):
                            if high_on_pool(q):
                                dve.wait_ge(pool_high, i * TILE_HIGH_POOL + count(high_on_pool, q) + 1)
                            else:
                                dve.wait_ge(dve_high, i * TILE_HIGH_DVE + count(high_on_dve, q) + 1)
                            nc.vector.tensor_tensor(basis_l[:, q % RB], tbuf[:, q % RT], basis_h[:, q % RB],
                                                    ALU.subtract).then_inc(basis_ready, 1)

                        def drain(i, q):
                            high(i, q)
                            low(i, q - 1)
                            low(i, q)

                        def add_output(n, e, kan, wait_turned):
                            dve.wait_ge(*wait_turned)
                            for c in range(TC):
                                at = (NE if kan else 0) + e
                                g = gates[:, c, at:at + 1]
                                if e == 0 and not kan:
                                    last = nc.vector.tensor_scalar(acc[:, c], ps_turned[:, c], g, None, ALU.mult)
                                else:
                                    last = nc.vector.scalar_tensor_tensor(
                                        out=acc[:, c], in0=ps_turned[:, c], scalar=g, in1=acc[:, c],
                                        op0=ALU.mult, op1=ALU.add)
                            last.then_inc(acc_done, 1)
                            dve.wait_ge(acc_done, n + 2)

                        def hidden(w, j):
                            n = 4 * w + j
                            dve.wait_ge(gelu_done, n + 2)
                            dve.wait_ge(hid_used, n + 1)
                            nc.vector.tensor_scalar(hid_h[:, j % 2], hid[:, j % 2], H_SCALE, None,
                                                    ALU.mult).then_inc(hid_h_ready, 1)
                            dve.wait_ge(hid_h_ready, n + 1)
                            nc.vector.scalar_tensor_tensor(out=hid_l[:, j % 2], in0=hid[:, j % 2],
                                                           scalar=H_SCALE, in1=hid_h[:, j % 2],
                                                           op0=ALU.mult, op1=ALU.subtract).then_inc(hid_ready, 1)

                        def phase(i, e, order, start=0, stop=None, first=False, last=False):
                            n = i * NE + e
                            w = n + 1
                            if order == CLOSING:
                                drain(i, PHASE_Q[e] - 1)
                            since = {OPENING: NE * SLABS, CLOSING: PHASE_Q[e]}.get(order, PHASE_Q[0] if first else 0)
                            for p, slab in steps(order, e, start, stop):
                                if slab:
                                    q = slab[0]
                                    if on_dve(q):
                                        square(i, q)
                                    if q - 1 >= since:
                                        high(i, q - 1)
                                    if q - 2 >= since:
                                        low(i, q - 2)
                                    if order == OPENING and q == NE * SLABS + L0 - 1:
                                        drain(i, q)
                                if order != CLOSING:
                                    if p == HIDDEN[0]:
                                        hidden(w, 0)
                                    if p == HIDDEN[1]:
                                        hidden(w, 1)
                                    if p == Z_VAR:
                                        dve.wait_ge(z_var_done, w + 2)
                                        nc.vector.tensor_scalar(z_var[:], ps_var, 1.0 / F2, EPS, ALU.mult,
                                                                ALU.add).then_inc(z_var_ready, 1)
                                if order == OPENING:
                                    if p == A_PARTS:
                                        Preparation(i + 1).a_low()
                                    if p == Z_VAR:
                                        Preparation(i + 1, steps=4).logits()
                                    continue
                                if p == DIAG:
                                    dve.wait_ge(z_rstd_ready, n + 1)
                                    nc.vector.tensor_tensor(diag, ident[:].unsqueeze(1).to_broadcast([P, TC, P]),
                                                            z_rstd[:].unsqueeze(2).to_broadcast([P, TC, P]),
                                                            ALU.mult).then_inc(diag_ready, 1)
                                if p == HIDDEN[2]:
                                    hidden(n, 2)
                                if p == HIDDEN[3]:
                                    hidden(n, 3)
                                if p == N1:
                                    dve.wait_ge(bc_done, n + 1)
                                    dve.wait_ge(zc_ready, 2 * n + 3)
                                    for m in range(2):
                                        nc.vector.tensor_tensor(zc[:, m], zc[:, m], ps_bc,
                                                                ALU.mult).then_inc(n1_ready, 1)
                                if (e, p) == CHOOSE:
                                    Preparation(i, steps=5).choose()
                                if p == ADD_KAN and not first:
                                    add_output(2 * n - 1, (e - 1) % NE, True, (kan_turned, n + 1))
                                if (e, p) == GIVE:
                                    Preparation(i).give()
                                if p == ADD_MLP:
                                    if e == 0:
                                        dve.wait_ge(x_stored, i + 1)
                                    add_output(2 * n, e, False, (mlp_turned, n + 2))
                                if not last:
                                    following = Preparation(i + 1)
                                    if (e, p) == STATS_A:
                                        following.row_stats(1)
                                    if (e, p) == NORM_A:
                                        following.row_norm(1)
                                    if (e, p) == STATS_N:
                                        following.steps = 2
                                        following.row_stats(2)
                                    if (e, p) == NORM_N:
                                        following.row_norm(2)
                                    if (e, p) == (NE - 1, A_PARTS):
                                        following.a_low()
                                    if (e, p) == (NE - 1, Z_VAR):
                                        following.steps = 4
                                        following.logits()

                        def finish(i):
                            drain(i, NE * SLABS - 1)
                            add_output((i + 1) * 2 * NE - 1, NE - 1, True, (kan_turned, (i + 1) * NE + 1))

                        begin = Preparation(t0)
                        begin.row_stats(1)
                        begin.row_norm(1)
                        begin.row_stats(2)
                        begin.row_norm(2)
                        passes(dve, phase, finish)

                    @block.scalar
                    def _(act):
                        if t0 == 0:
                            act.sem_inc(gelu_done, 1)
                            act.sem_inc(zc_ready, 1)

                        def n_turn_out(i):
                            act.wait_ge(n_turned, i + 1)
                            nc.scalar.activation(n_tok[:].rearrange("p c t -> p (c t)"), ps_h,
                                                 ACT.Copy).then_inc(n_next_ready, 1)

                        def n_copy(i):
                            act.wait_ge(n_next_ready, i + 1)
                            nc.scalar.activation(n_t[:], n_tok[:].rearrange("p c t -> p (c t)"),
                                                 ACT.Copy).then_inc(n_t_ready, 1)
                            act.wait_ge(n_t_ready, i + 1)

                        def tanh(i, q, layer, e, s):
                            act.wait_ge(basis_ready, i * TILE_SLABS + q + 1)
                            if layer == 0:
                                src, sc, bi = n_t[:], scale0[:, e:e + 1], bias0[:, e, s:s + 1]
                            else:
                                m, g = divmod(s, NG)
                                if g == 0:
                                    act.wait_ge(n1_ready, i * 2 * NE + 2 * e + m + 2)
                                src, sc, bi = zc[:, m], scale1[:, 2 * e + m:2 * e + m + 1], bias1[:, 2 * e + m, g:g + 1]
                            nc.scalar.activation(tbuf[:, q % RT], src, ACT.Tanh, bias=bi, scale=sc
                                                 ).then_inc(tanh_done, 1)

                        def square(i, q):
                            if on_act(q):
                                act.wait_ge(tanh_done, i * TILE_SLABS + q + 1)
                                t = tbuf[:, q % RT]
                                nc.scalar.activation(t, t, ACT.Square, scale=T_SCALE).then_inc(act_squared, 1)

                        def gelu(w, e, j):
                            act.wait_ge(hid_done, 4 * w + j + 1)
                            act.wait_ge(hid_ready, 4 * w + j + 1)
                            nc.scalar.activation(hid[:, j % 2], ps_h, ACT.Gelu, bias=col("mlp_b1", 4 * e + j),
                                                 scale=1.0 / (A_SCALE * W_SCALE)).then_inc(gelu_done, 1)

                        def z_square(e, m):
                            nc.scalar.activation(z_sq[:, m], ps_z[:, m], ACT.Square, bias=z_bias[:, e, m:m + 1],
                                                 scale=-BASIS_UNIT).then_inc(z_sq_ready, 1)

                        def z_copy(e, m):
                            nc.scalar.activation(zc[:, m], ps_z[:, m], ACT.Identity, bias=z_bias[:, e, m:m + 1],
                                                 scale=-BASIS_UNIT).then_inc(zc_ready, 1)

                        def kan_out(n, e, used):
                            act.wait_ge(slab_used, used)
                            act.wait_ge(kan_turned, n + 1)
                            nc.scalar.activation(eo_kan[:], ps_kan, ACT.Identity, bias=o_bias[:, e:e + 1],
                                                 scale=-BASIS_UNIT).then_inc(kan_out_ready, 1)

                        def phase(i, e, order, start=0, stop=None, first=False, last=False):
                            n = i * NE + e
                            w, ew = n + 1, (e + 1) % NE
                            if order == CLOSING:
                                square(i, PHASE_Q[e] - 1)
                            since = {OPENING: NE * SLABS, CLOSING: PHASE_Q[e]}.get(order, PHASE_Q[0] if first else 0)
                            for p, slab in steps(order, e, start, stop):
                                if slab:
                                    q, layer, s = slab
                                    tanh(i, q, layer, e if layer else ew, s)
                                    if q - 1 >= since:
                                        square(i, q - 1)
                                    if order == OPENING and q == NE * SLABS + L0 - 1:
                                        square(i, q)
                                if order != CLOSING:
                                    if p == GELU[0]:
                                        gelu(w, ew, 0)
                                    if p == GELU[1]:
                                        gelu(w, ew, 1)
                                    if p == Z_OUT:
                                        act.wait_ge(slab_used, i * TILE_SLABS + last_l0(order, e) + 1 + RB)
                                        if order != OPENING or t0:
                                            act.wait_ge(bc_done, w)
                                        z_square(ew, 0)
                                        z_square(ew, 1)
                                        if order != OPENING:
                                            act.wait_ge(tanh_done, i * TILE_SLABS + PHASE_Q[e] + SLABS)
                                        z_copy(ew, 0)
                                        z_copy(ew, 1)
                                if p == A_PARTS and (order == OPENING or e == NE - 1 and not last):
                                    act.wait_ge(a_turned, i + 2)
                                    nc.scalar.activation(a_h[:], ps_h, ACT.Copy, scale=A_SCALE).then_inc(a_h_ready, 1)
                                if order == OPENING:
                                    continue
                                if p == GELU[2]:
                                    gelu(n, e, 2)
                                if p == GELU[3]:
                                    gelu(n, e, 3)
                                if p == OUTPUTS:
                                    act.wait_ge(hid_used, 4 * n + 4 + 2)
                                    act.wait_ge(mlp_turned, n + 1)
                                    nc.scalar.activation(eo_mlp[:], ps_mlp, ACT.Identity, bias=col("mlp_b2", e),
                                                         scale=1.0 / (H_SCALE * W_SCALE)).then_inc(mlp_out_ready, 1)
                                    if not first:
                                        kan_out(n - 1, (e - 1) % NE, i * TILE_SLABS + PHASE_Q[e] + RB)
                                if (e, p) == EXPS:
                                    act.wait_ge(shifted, i + 1)
                                    nc.scalar.activation(probs[:], probs[:], ACT.Exp,
                                                         scale=1.0 / (A_SCALE * W_SCALE)).then_inc(exp_done, 1)
                                if (e, p) == N_TURN_OUT and not last:
                                    n_turn_out(i + 1)
                                if (e, p) == N_COPY and not last:
                                    act.wait_ge(tanh_done, i * TILE_SLABS + last_l0(order, e) + 1)
                                    n_copy(i + 1)

                        def finish(i):
                            square(i, NE * SLABS - 1)
                            kan_out((i + 1) * NE - 1, NE - 1, (i + 1) * TILE_SLABS + RB)

                        n_turn_out(t0)
                        n_copy(t0)
                        passes(act, phase, finish)

                    @block.tensor
                    def _(pe):
                        if t0 == 0:
                            pe.sem_inc(slab_used, RB)
                            pe.sem_inc(hid_used, 2)
                            pe.sem_inc(z_var_done, 1)
                            pe.sem_inc(mlp_turned, 1)
                            pe.sem_inc(kan_turned, 1)

                        def split_product(outs, w_h, w_l, x_h, x_l, start, stop):
                            for n, (w, x) in enumerate(((w_h, x_h), (w_h, x_l), (w_l, x_h))):
                                for b, out in enumerate(outs):
                                    last = nc.tensor.matmul(out, w, x(b), start=(start and n == 0),
                                                            stop=(stop and n == 2))
                            return last

                        def half(buf):
                            return lambda b: buf[:, b * BANK:(b + 1) * BANK]

                        def turn(src):
                            for c in range(TC):
                                last = nc.tensor.transpose(ps_turned[:, c], src(c), ident[:])
                            return last

                        def turn_a(i):
                            pe.wait_ge(norm_ready, i * 2 + 1)
                            turn(lambda c: a_tok[:, c]).then_inc(a_turned, 1)

                        def turn_n(i):
                            pe.wait_ge(norm_ready, i * 2 + 2)
                            turn(lambda c: n_tok[:, c]).then_inc(n_turned, 1)

                        def gate_logits(i):
                            for c in range(TC):
                                at = slice(c * P, (c + 1) * P)
                                nc.tensor.matmul(ps_logit[:, c], a_h[:, at], gate_h[:], start=True, stop=False)
                                nc.tensor.matmul(ps_logit[:, c], a_h[:, at], gate_l[:], start=False, stop=False)
                                last = nc.tensor.matmul(ps_logit[:, c], a_l[:, at], gate_h[:], start=False, stop=True)
                            last.then_inc(logits_done, 1)

                        def multiply_slab(i, q, layer, e, s):
                            pe.wait_ge(basis_ready, i * TILE_SLABS + q + 1 + RT)
                            x_h, x_l = half(basis_h[:, q % RB]), half(basis_l[:, q % RB])
                            if layer == 0:
                                for m in range(2):
                                    at = slice(m * P, (m + 1) * P)
                                    done = split_product([psum[:, 2 * m], psum[:, 2 * m + 1]], w0_h[:, e, s, at],
                                                         w0_l[:, e, s, at], x_h, x_l, s == 0, s == L0 - 1)
                            else:
                                m, g = divmod(s, NG)
                                done = split_product([psum[:, 6], psum[:, 7]], w1_h[:, e, m, g], w1_l[:, e, m, g],
                                                     x_h, x_l, s == 0, s == L1 - 1)
                            done.then_inc(slab_used, 1)

                        def mlp_up(w, e, j):
                            if j:
                                pe.wait_ge(gelu_done, 4 * w + j + 1)
                            at = slice(e * FM + j * P, e * FM + (j + 1) * P)
                            split_product([psum[:, 4], psum[:, 5]], mw1_h[:, at], mw1_l[:, at], half(a_h),
                                          half(a_l), True, True).then_inc(hid_done, 1)

                        def mlp_down(w, e, j):
                            pe.wait_ge(hid_ready, 4 * w + j + 1 + 2)
                            at = slice((4 * e + j) * P, (4 * e + j + 1) * P)
                            split_product([psum[:, 0], psum[:, 1]], mw2_h[:, at], mw2_l[:, at],
                                          half(hid_h[:, j % 2]), half(hid_l[:, j % 2]), j == 0, j == 3
                                          ).then_inc(hid_used, 1)

                        def turn_kan(n):
                            pe.wait_ge(kan_out_ready, n + 1)
                            pe.wait_ge(acc_done, 2 * n + 2)
                            turn(lambda c: eo_kan[:, c * P:(c + 1) * P]).then_inc(kan_turned, 1)

                        def broadcast(n):
                            pe.wait_ge(diag_ready, n + 1)
                            for b in range(2):
                                done = nc.tensor.matmul(
                                    psum[:, 2 + b], ones[:], diag[:, 4 * b:4 * b + 4].rearrange("p c t -> p (c t)"),
                                    start=True, stop=True)
                            done.then_inc(bc_done, 1)

                        def phase(i, e, order, start=0, stop=None, first=False, last=False):
                            n = i * NE + e
                            w, ew = n + 1, (e + 1) % NE
                            for p, slab in steps(order, e, start, stop):
                                if slab:
                                    q, layer, s = slab
                                    if (layer, s) == (0, 0) and order != OPENING:
                                        pe.wait_ge(n1_ready, 2 * n + 3)
                                        pe.wait_ge(mlp_out_ready, n + 1)
                                    if (layer, s) == (1, 0) and not first:
                                        pe.wait_ge(kan_out_ready, n)
                                    multiply_slab(i, q, layer, e if layer else ew, s)
                                if p == TURN_A and (order == OPENING or e == NE - 1 and not last):
                                    if order != OPENING:
                                        pe.wait_ge(acc_done, 2 * n + 2)
                                    turn_a(i + 1)
                                if order != CLOSING:
                                    if p == UP[0]:
                                        if order == OPENING or e == NE - 1:
                                            pe.wait_ge(a_l_ready, i + 2)
                                        else:
                                            pe.wait_ge(acc_done, 2 * n + 2)
                                        if e == N_TURN_OUT[0] and not last:
                                            pe.wait_ge(n_next_ready, i + 2)
                                        mlp_up(w, ew, 0)
                                    if p == UP[1]:
                                        mlp_up(w, ew, 1)
                                    if p == UP[2]:
                                        mlp_up(w, ew, 2)
                                    if p == VAR:
                                        pe.wait_ge(z_sum_ready, w + 1)
                                        pe.wait_ge(zc_ready, 2 * w + 3)
                                        for c in range(TC):
                                            done = nc.tensor.matmul(
                                                ps_var[:, c:c + 1], z_sq[:, 0, c * P:(c + 1) * P], ones[:, 0:1],
                                                start=True, stop=True)
                                        done.then_inc(z_var_done, 1)
                                        if order == OPENING or e == NE - 1:
                                            gate_logits(i + 1)
                                    if p == DOWN[0]:
                                        pe.wait_ge(zc_ready, 2 * w + 2)
                                        mlp_down(w, ew, 0)
                                    if p == UP[3]:
                                        mlp_up(w, ew, 3)
                                    if p == DOWN[1]:
                                        mlp_down(w, ew, 1)
                                    if p == BROADCAST:
                                        if order == OPENING or e == NE - 1:
                                            pe.wait_ge(shifted, i + 2)
                                        broadcast(w)
                                    if p == DOWN[2]:
                                        mlp_down(w, ew, 2)
                                    if p == DOWN[3]:
                                        mlp_down(w, ew, 3)
                                if order == OPENING:
                                    continue
                                if p == TURN_KAN and not first:
                                    pe.wait_ge(gelu_done, 4 * n + 5)
                                    turn_kan(n - 1)
                                if p == TURN_MLP:
                                    pe.wait_ge(mlp_out_ready, n + 1)
                                    pe.wait_ge(acc_done, 2 * n + 1)
                                    turn(lambda c: eo_mlp[:, c * P:(c + 1) * P]).then_inc(mlp_turned, 1)
                                if (e, p) == TURN_N and not last:
                                    pe.wait_ge(acc_done, 2 * n + 2)
                                    turn_n(i + 1)

                        def finish(i):
                            turn_kan((i + 1) * NE - 1)

                        turn_n(t0)
                        pe.wait_ge(n_next_ready, t0 + 1)
                        passes(pe, phase, finish)

        def retention():
            tmp = ExitStack()
            with tmp:
                def many(name, shape):
                    return [sb(f"{name}_{s}", shape, tmp) for s in range(SLOTS)]

                wq = sb("wq", [P, NL, P], tmp)
                wk = sb("wk", [P, NL, P], tmp)
                wv = sb("wv", [P, NL, P], tmp)
                wg = sb("wg", [P, NL, P], tmp)
                wo = sb("wo", [P, NL, P], tmp)
                wq_rot = sb("wq_rot", [P, NL, P], tmp)
                wk_rot = sb("wk_rot", [P, NL, P], tmp)
                fw1 = sb("fw1", [P, NL, FM], tmp)
                fw2 = sb("fw2", [P, NL, 4, P], tmp)
                b2_rows = sb("b2_rows", [P, NL, P], tmp)
                cos_q = sb("cos_q", [P, S], tmp)
                sin_q = sb("sin_q", [P, S], tmp)
                cos_k = sb("cos_k", [P, S], tmp)
                sin_k = sb("sin_k", [P, S], tmp)
                decay_q = sb("decay_q", [P, P], tmp)
                decay_k = sb("decay_k", [P, P], tmp)
                decay_qk = sb("decay_qk", [P, NH, P], tmp)
                same_head = sb("same_head", [P, P], tmp)

                u = many("u", [P, NC, P])
                row = many("row", [P, NC, P])
                col_in = many("col_in", [P, S])
                q = many("q", [P, S])
                qd = many("qd", [P, S])
                k = many("k", [P, S])
                part = many("part", [P, S])
                v = many("v", [P, NC, P])
                kd = many("kd", [P, NC, P])
                gate = many("gate", [P, S])
                big = many("big", [P, 4, S])
                state = many("state", [P, NC, P])
                stats = many("r_stats", [P, NC, 6])
                mean_var = many("r_mean_var", [P, NC, 2])
                var_eps = many("r_var_eps", [P, NC * NH])
                rstd = many("r_rstd", [P, NC * NH])
                mean = many("r_mean", [P, NC * NH])
                k_head = [b[:, 0:2].rearrange("p a (h t) -> p (a h) t", t=P) for b in big]
                scores = [b[:, 2:4].rearrange("p a (h t) -> p (a h) t", t=P) for b in big]

                def bank(s, n):
                    return psum[:, 4 * s + n]

                def bank_c(s, n):
                    return psum[:, 4 * s + n].rearrange("p (c f) -> p c f", f=P)

                def sems(name):
                    return [sem(f"{name}_{s}") for s in range(SLOTS)]

                r_in = sem("r_in")
                rot_done = sem("rot_done")
                r_step = sem("r_step")
                x_got = sems("x_got")
                x_put = sems("x_put")
                u_ready = sems("u_ready")
                var_asked = sems("r_var_asked")
                rstd_given = sems("r_rstd_given")
                n1_row = sems("n1_row")
                n1_turned = sems("n1_turned")
                n1_col = sems("n1_col")
                q_done = sems("q_done")
                k_done = sems("k_done")
                q_ready = sems("q_ready")
                k_ready = sems("k_ready")
                qd_ready = sems("qd_ready")
                g_done = sems("g_done")
                v_done = sems("v_done")
                kt_done = sems("kt_done")
                g_ready = sems("g_ready")
                v_ready = sems("v_ready")
                kd_ready = sems("kd_ready")
                kh_ready = sems("kh_ready")
                sc_done = sems("sc_done")
                sc_ready = sems("sc_ready")
                kv_done = sems("kv_done")
                state_ready = sems("state_ready")
                y_done = sems("y_done")
                y_row = sems("y_row")
                y_turned = sems("y_turned")
                y_col = sems("y_col")
                gy_ready = sems("gy_ready")
                wo_done = sems("wo_done")
                u2_ready = sems("u2_ready")
                ub_ready = sems("ub_ready")
                n2_row = sems("n2_row")
                n2_turned = sems("n2_turned")
                n2_col = sems("n2_col")
                h_done = sems("h_done")
                h_ready = sems("h_ready")
                w2_done = sems("w2_done")
                ITER = NB // SLOTS
                R_STEPS = SLOTS * (2 + NL * 13)

                with nc.Block() as block:
                    @block.sync
                    def _(sp):
                        n = 0
                        for dst, name in ((wq, "wq"), (wk, "wk"), (wv, "wv"), (wg, "wg"), (wo, "wo"), (fw1, "fw1"),
                                          (fw2, "fw2"), (b2_rows, "b2_rows"), (cos_q, "cos_q"), (sin_q, "sin_q"),
                                          (cos_k, "cos_k"), (sin_k, "sin_k"), (decay_q, "decay_q"),
                                          (decay_k, "decay_k"), (decay_qk, "decay_qk"), (same_head, "same_head")):
                            sp.dma_start(dst[:], A[name]).then_inc(r_in, 16)
                            n += 1
                        assert n == 16
                        sp.wait_ge(r_in, 16 * n)

                    @block.gpsimd
                    def _(pool):
                        pool.wait_ge(r_in, 256)
                        with pool.Fori(0, ITER) as i:
                            def power(s, n):
                                pool.wait_ge(var_asked[s], i * 7 + n)
                                m = NC * NH if n in (3, 6) else NC
                                nc.gpsimd.tensor_tensor(rstd[s][:, 0:m], var_eps[s][:, 0:m], neg_half[:, 0:m],
                                                        ALU.pow).then_inc(rstd_given[s], 1)

                            for s in range(SLOTS):
                                pool.wait_ge(n2_turned[s], i * NL)
                                hold(pool)
                                nc.gpsimd.tensor_copy(row[s][:], x_all[:, bass.ds(i * SLOTS * NC + s * NC, NC), :]
                                                      ).then_inc(x_got[s], 1)
                            for s in range(SLOTS):
                                power(s, 1)
                            for l in range(NL):
                                n = i * NL + l + 1
                                for s in range(SLOTS):
                                    power(s, 2 + 3 * l)
                                for s in range(SLOTS):
                                    pool.wait_ge(q_ready[s], n)
                                    nc.gpsimd.tensor_tensor(
                                        qd[s][:].rearrange("p (c t) -> p c t", t=P),
                                        q[s][:].rearrange("p (c t) -> p c t", t=P),
                                        decay_q[:].unsqueeze(1).to_broadcast([P, NC, P]),
                                        ALU.mult).then_inc(qd_ready[s], 1)
                                for c in range(NC):
                                    for s in range(SLOTS):
                                        if c == 0:
                                            pool.wait_ge(k_ready[s], n)
                                            pool.wait_ge(w2_done[s], n - 1)
                                        else:
                                            pool.wait_ge(sc_done[s], (i * NL + l) * NC + c)
                                        nc.gpsimd.tensor_tensor(
                                            k_head[s], k[s][:, c * P:(c + 1) * P].unsqueeze(1).to_broadcast([P, NH, P]),
                                            col("head_mask", 0, NH).unsqueeze(2).to_broadcast([P, NH, P]),
                                            ALU.mult).then_inc(kh_ready[s], 1)
                                for s in range(SLOTS):
                                    power(s, 3 + 3 * l)
                                for s in range(SLOTS):
                                    pool.wait_ge(u2_ready[s], n)
                                    power(s, 4 + 3 * l)
                                    nc.gpsimd.tensor_tensor(part[s][:].rearrange("p (c f) -> p c f", f=P), u[s][:],
                                                            b2_rows[:, l].unsqueeze(1).to_broadcast([P, NC, P]),
                                                            ALU.add).then_inc(ub_ready[s], 1)
                            for s in range(SLOTS):
                                pool.wait_ge(u_ready[s], (i + 1) * (NL + 1))
                                hold(pool)
                                xs = x_all[:, bass.ds(i * SLOTS * NC + s * NC, NC), :]
                                nc.gpsimd.tensor_tensor(xs, xs, u[s][:], ALU.add).then_inc(x_put[s], 1)
                            for s in range(SLOTS):
                                pool.wait_ge(x_put[s], i + 1)

                    @block.vector
                    def _(dve):
                        dve.wait_ge(r_in, 256)
                        for w, w_rot in ((wq, wq_rot), (wk, wk_rot)):
                            pairs = w[:].rearrange("p l (n two) -> p l n two", two=2)
                            rot = w_rot[:].rearrange("p l (n two) -> p l n two", two=2)
                            nc.vector.tensor_scalar(rot[:, :, :, 0], pairs[:, :, :, 1], -1.0, None,
                                                    ALU.mult).then_inc(rot_done, 1)
                            nc.vector.tensor_copy(rot[:, :, :, 1], pairs[:, :, :, 0]).then_inc(rot_done, 1)
                        with dve.Fori(0, ITER) as i:
                            done = [0]

                            def step(ins):
                                done[0] += 1
                                ins.then_inc(r_step, 1)
                                dve.wait_ge(r_step, i * R_STEPS + done[0])

                            def normalise(s, dst, src, n, ready, value):
                                for c in range(NC):
                                    last = nc.vector.bn_stats(stats[s][:, c], src[:, c])
                                step(last)
                                hold(dve)
                                for c in range(NC):
                                    last = nc.vector.bn_aggr(mean_var[s][:, c], stats[s][:, c])
                                step(last)
                                nc.vector.tensor_scalar(var_eps[s][:, 0:NC], mean_var[s][:, :, 1], EPS, None,
                                                        ALU.add).then_inc(var_asked[s], 1)

                                def rest():
                                    dve.wait_ge(rstd_given[s], i * 7 + n)
                                    for c in range(NC):
                                        last = nc.vector.tensor_scalar(dst[:, c], src[:, c], mean_var[s][:, c, 0:1],
                                                                       rstd[s][:, c:c + 1], ALU.subtract, ALU.mult)
                                    last.then_inc(ready, 1)
                                    dve.wait_ge(ready, value)
                                return rest

                            def both(f):
                                rests = [f(s) for s in range(SLOTS)]
                                for r in rests:
                                    r()

                            def first(s):
                                dve.wait_ge(x_got[s], i + 1)
                                dve.wait_ge(x_put[s], i)
                                return normalise(s, u[s], row[s], 1, u_ready[s], i * (NL + 1) + 1)

                            both(first)
                            for l in range(NL):
                                n = i * NL + l + 1
                                both(lambda s: normalise(s, row[s], u[s], 2 + 3 * l, n1_row[s], n))
                                for s in range(SLOTS):
                                    dve.wait_ge(q_done[s], n)
                                    nc.vector.tensor_tensor(part[s][:], bank(s, 1), cos_q[:], ALU.mult)
                                    step(nc.vector.tensor_tensor(q[s][:], bank(s, 2), sin_q[:], ALU.mult))
                                    nc.vector.tensor_tensor(q[s][:], q[s][:], part[s][:], ALU.add
                                                            ).then_inc(q_ready[s], 1)
                                    dve.wait_ge(q_ready[s], n)
                                    dve.wait_ge(k_done[s], n)
                                    nc.vector.tensor_tensor(part[s][:], bank(s, 3), cos_k[:], ALU.mult)
                                    step(nc.vector.tensor_tensor(k[s][:], bank(s, 0), sin_k[:], ALU.mult))
                                    nc.vector.tensor_tensor(k[s][:], k[s][:], part[s][:], ALU.add
                                                            ).then_inc(k_ready[s], 1)
                                for s in range(SLOTS):
                                    dve.wait_ge(kt_done[s], n)
                                    nc.vector.tensor_tensor(kd[s][:], bank_c(s, 3),
                                                            decay_k[:].unsqueeze(1).to_broadcast([P, NC, P]),
                                                            ALU.mult).then_inc(kd_ready[s], 1)

                                def decay(s, c):
                                    at = (i * NL + l) * NC + c
                                    dve.wait_ge(sc_done[s], at + 1)
                                    dve.wait_ge(y_done[s], at)
                                    nc.vector.tensor_tensor(
                                        scores[s], psum[:, 4 * s:4 * s + 2].rearrange("p a (h t) -> p (a h) t", t=P),
                                        decay_qk[:], ALU.mult).then_inc(sc_ready[s], 1)

                                for s in range(SLOTS):
                                    decay(s, 0)
                                for s in range(SLOTS):
                                    dve.wait_ge(kv_done[s], n)
                                    step(nc.vector.tensor_tensor(state[s][:, 1:4], bank_c(s, 2)[:, 0:3],
                                                                 same_head[:].unsqueeze(1).to_broadcast([P, 3, P]),
                                                                 ALU.mult))
                                    step(nc.vector.scalar_tensor_tensor(
                                        out=state[s][:, 2], in0=state[s][:, 1], scalar=col("decay_chunk"),
                                        in1=state[s][:, 2], op0=ALU.mult, op1=ALU.add))
                                    nc.vector.scalar_tensor_tensor(
                                        out=state[s][:, 3], in0=state[s][:, 2], scalar=col("decay_chunk"),
                                        in1=state[s][:, 3], op0=ALU.mult, op1=ALU.add).then_inc(state_ready[s], 1)
                                for c in range(1, NC):
                                    for s in range(SLOTS):
                                        decay(s, c)

                                def group_norm(s):
                                    dve.wait_ge(y_done[s], n * NC)
                                    y = bank(s, 3).rearrange("p (g f) -> p g f", f=HD)
                                    yc = row[s][:].rearrange("p c (h f) -> p (c h) f", f=HD)
                                    sq = part[s][:].rearrange("p (g f) -> p g f", f=HD)
                                    step(nc.vector.tensor_reduce(mean[s][:], y, AX_X, ALU.add))
                                    step(nc.vector.tensor_scalar(mean[s][:], mean[s][:], 1.0 / HD, None, ALU.mult))
                                    step(nc.vector.tensor_tensor(
                                        yc, y, mean[s][:].unsqueeze(2).to_broadcast([P, NC * NH, HD]), ALU.subtract))
                                    step(nc.vector.tensor_tensor(sq, yc, yc, ALU.mult))
                                    step(nc.vector.tensor_reduce(var_eps[s][:], sq, AX_X, ALU.add))
                                    nc.vector.tensor_scalar(var_eps[s][:], var_eps[s][:], 1.0 / HD, EPS, ALU.mult,
                                                            ALU.add).then_inc(var_asked[s], 1)

                                    def rest():
                                        dve.wait_ge(rstd_given[s], i * 7 + 3 + 3 * l)
                                        nc.vector.tensor_tensor(
                                            yc, yc, rstd[s][:].unsqueeze(2).to_broadcast([P, NC * NH, HD]),
                                            ALU.mult).then_inc(y_row[s], 1)
                                    return rest

                                both(group_norm)
                                for s in range(SLOTS):
                                    dve.wait_ge(y_col[s], n)
                                    dve.wait_ge(g_ready[s], n)
                                    nc.vector.tensor_tensor(col_in[s][:], col_in[s][:], gate[s][:], ALU.mult
                                                            ).then_inc(gy_ready[s], 1)

                                def second(s):
                                    dve.wait_ge(wo_done[s], n)
                                    nc.vector.tensor_tensor(u[s][:], bank_c(s, 1), u[s][:], ALU.add
                                                            ).then_inc(u2_ready[s], 1)
                                    dve.wait_ge(u2_ready[s], n)
                                    dve.wait_ge(y_turned[s], n)
                                    return normalise(s, row[s], u[s], 4 + 3 * l, n2_row[s], n)

                                both(second)
                                for s in range(SLOTS):
                                    dve.wait_ge(w2_done[s], n)
                                    dve.wait_ge(ub_ready[s], n)
                                    nc.vector.tensor_tensor(u[s][:], bank_c(s, 3),
                                                            part[s][:].rearrange("p (c f) -> p c f", f=P), ALU.add
                                                            ).then_inc(u_ready[s], 1)
                                    dve.wait_ge(u_ready[s], i * (NL + 1) + l + 2)
                            assert done[0] == R_STEPS, done

                    @block.scalar
                    def _(act):
                        act.wait_ge(r_in, 256)
                        with act.Fori(0, ITER) as i:
                            for l in range(NL):
                                n = i * NL + l + 1
                                for s in range(SLOTS):
                                    act.wait_ge(n1_turned[s], n)
                                    nc.scalar.activation(col_in[s][:], bank(s, 0), ACT.Identity, bias=col("ln1_b", l),
                                                         scale=col("ln1_w", l)).then_inc(n1_col[s], 1)
                                for s in range(SLOTS):
                                    act.wait_ge(g_done[s], n)
                                    nc.scalar.activation(gate[s][:], bank(s, 1), ACT.Silu).then_inc(g_ready[s], 1)
                                    act.wait_ge(v_done[s], n)
                                    nc.scalar.activation(v[s][:], bank_c(s, 2), ACT.Copy).then_inc(v_ready[s], 1)
                                for s in range(SLOTS):
                                    act.wait_ge(y_turned[s], n)
                                    nc.scalar.activation(col_in[s][:], bank(s, 0), ACT.Identity, bias=col("gn_b", l),
                                                         scale=col("gn_w", l)).then_inc(y_col[s], 1)
                                for s in range(SLOTS):
                                    act.wait_ge(n2_turned[s], n)
                                    nc.scalar.activation(col_in[s][:], bank(s, 2), ACT.Identity, bias=col("ln2_b", l),
                                                         scale=col("ln2_w", l)).then_inc(n2_col[s], 1)
                                for j in range(4):
                                    for s in range(SLOTS):
                                        act.wait_ge(h_done[s], (i * NL + l) * 4 + j + 1)
                                        nc.scalar.activation(big[s][:, j], bank(s, j % 3), ACT.Silu,
                                                             bias=col("ffn_b1", 4 * l + j)).then_inc(h_ready[s], 1)

                    @block.tensor
                    def _(pe):
                        pe.wait_ge(r_in, 256)
                        pe.wait_ge(rot_done, 4)
                        with pe.Fori(0, ITER) as i:
                            def turn(dst, src, done_sem):
                                for c in range(NC):
                                    last = nc.tensor.transpose(dst[:, c], src[:, c], ident[:])
                                last.then_inc(done_sem, 1)

                            def product(dst, w, rhs):
                                return nc.tensor.matmul(dst, w, rhs, start=True, stop=True)

                            for l in range(NL):
                                n = i * NL + l + 1
                                at = (i * NL + l) * NC
                                for s in range(SLOTS):
                                    pe.wait_ge(n1_row[s], n)
                                    pe.wait_ge(h_ready[s], at)
                                    turn(bank_c(s, 0), row[s], n1_turned[s])
                                for s in range(SLOTS):
                                    pe.wait_ge(n1_col[s], n)
                                    product(bank(s, 1), wq[:, l], col_in[s][:])
                                    product(bank(s, 2), wq_rot[:, l], col_in[s][:]).then_inc(q_done[s], 1)
                                    pe.wait_ge(u_ready[s], i * (NL + 1) + l + 1)
                                    product(bank(s, 3), wk[:, l], col_in[s][:])
                                    product(bank(s, 0), wk_rot[:, l], col_in[s][:]).then_inc(k_done[s], 1)
                                for s in range(SLOTS):
                                    pe.wait_ge(q_ready[s], n)
                                    product(bank(s, 1), wg[:, l], col_in[s][:]).then_inc(g_done[s], 1)
                                    for c in range(NC):
                                        last = product(bank_c(s, 2)[:, c], col_in[s][:, c * P:(c + 1) * P], wv[:, l])
                                    last.then_inc(v_done[s], 1)
                                    pe.wait_ge(k_ready[s], n)
                                    turn(bank_c(s, 3), k[s][:].rearrange("p (c t) -> p c t", t=P), kt_done[s])

                                def score(s, c):
                                    pe.wait_ge(kh_ready[s], at + c + 1)
                                    if c == 0:
                                        pe.wait_ge(g_ready[s], n)
                                    else:
                                        pe.wait_ge(sc_ready[s], at + c)
                                    for h in range(NH):
                                        last = product(bank_c(s, h // 4)[:, h % 4], k_head[s][:, h],
                                                       q[s][:, c * P:(c + 1) * P])
                                    last.then_inc(sc_done[s], 1)

                                def output(s, c):
                                    pe.wait_ge(sc_ready[s], at + c + 1)
                                    if c == 0:
                                        pe.wait_ge(kd_ready[s], n)
                                    if c == 1:
                                        pe.wait_ge(state_ready[s], n)
                                        pe.wait_ge(qd_ready[s], n)
                                    dst = bank_c(s, 3)[:, c]
                                    if c:
                                        nc.tensor.matmul(dst, qd[s][:, c * P:(c + 1) * P], state[s][:, c],
                                                         start=True, stop=False, skip_group_check=True)
                                    for h in range(NH):
                                        last = nc.tensor.matmul(dst[:, h * HD:(h + 1) * HD], scores[s][:, h],
                                                                v[s][:, c, h * HD:(h + 1) * HD],
                                                                start=(c == 0 and h == 0), stop=(h == NH - 1),
                                                                skip_group_check=True)
                                    last.then_inc(y_done[s], 1)

                                for s in range(SLOTS):
                                    score(s, 0)
                                for s in range(SLOTS):
                                    pe.wait_ge(v_ready[s], n)
                                    pe.wait_ge(kd_ready[s], n)
                                    for c in range(NC - 1):
                                        last = product(bank_c(s, 2)[:, c], kd[s][:, c], v[s][:, c])
                                    last.then_inc(kv_done[s], 1)
                                for c in range(1, NC):
                                    for s in range(SLOTS):
                                        score(s, c)
                                    for s in range(SLOTS):
                                        output(s, c - 1)
                                for s in range(SLOTS):
                                    output(s, NC - 1)
                                for s in range(SLOTS):
                                    pe.wait_ge(y_row[s], n)
                                    turn(bank_c(s, 0), row[s], y_turned[s])
                                for s in range(SLOTS):
                                    pe.wait_ge(gy_ready[s], n)
                                    for c in range(NC):
                                        last = product(bank_c(s, 1)[:, c], col_in[s][:, c * P:(c + 1) * P], wo[:, l])
                                    last.then_inc(wo_done[s], 1)
                                for s in range(SLOTS):
                                    pe.wait_ge(n2_row[s], n)
                                    turn(bank_c(s, 2), row[s], n2_turned[s])
                                for j in range(4):
                                    for s in range(SLOTS):
                                        if j == 0:
                                            pe.wait_ge(n2_col[s], n)
                                        if j == 3:
                                            pe.wait_ge(h_ready[s], at + 1)
                                        product(bank(s, j % 3), fw1[:, l, j * P:(j + 1) * P],
                                                col_in[s][:]).then_inc(h_done[s], 1)
                                for s in range(SLOTS):
                                    for c in range(NC):
                                        for j in range(4):
                                            if c == 0:
                                                pe.wait_ge(h_ready[s], at + j + 1)
                                            last = nc.tensor.matmul(bank_c(s, 3)[:, c],
                                                                    big[s][:, j, c * P:(c + 1) * P], fw2[:, l, j],
                                                                    start=(j == 0), stop=(j == 3))
                                    last.then_inc(w2_done[s], 1)

        stages = A["stages"]
        if stages >= 1:
            feed_forward("a", 0)
        if stages >= 2:
            retention()
        if stages >= 3:
            feed_forward("b", NT)

        x_out = sem("x_out")
        with nc.Block() as block:
            @block.sync
            def _(sp):
                sp.dma_start(A["out"], x_all[:]).then_inc(x_out, 16)
                sp.wait_ge(x_out, 16)


def constants():
    half = HD // 2
    scale_vec = (np.arange(0, HD, 2) + 0.4 * HD) / (1.4 * HD)
    scale = scale_vec[None, :] ** (np.arange(S, dtype=np.float64) / 64)[:, None]
    ang = np.arange(S, dtype=np.float64)[:, None] / 10000.0 ** (np.arange(half, dtype=np.float64) / half)[None, :]
    sin, cos = np.sin(ang), np.cos(ang)
    gammas = 1.0 - np.exp(np.linspace(np.log(1.0 / 32), np.log(1.0 / 64), NH))
    head = np.arange(P) // HD
    t = np.arange(P)

    def by_feature(m):
        return np.ascontiguousarray(np.tile(np.repeat(m, 2, axis=-1).T, (NH, 1)).astype(np.float32))

    diff = t[None, :] - t[:, None]
    decay = np.where(diff[None] >= 0, gammas[:, None, None] ** np.maximum(diff, 0)[None], 0.0)
    return {
        "ident": np.eye(P, dtype=np.float32),
        "tril": np.ascontiguousarray(np.broadcast_to(np.tril(np.ones((8, 8), np.float32), -1), (P, 8, 8))),
        "cos_q": by_feature(cos * scale), "sin_q": by_feature(sin * scale),
        "cos_k": by_feature(cos / scale), "sin_k": by_feature(sin / scale),
        "decay_q": (gammas[head][:, None] ** t[None, :]).astype(np.float32),
        "decay_k": (gammas[head][None, :] ** (P - t)[:, None]).astype(np.float32),
        "decay_qk": np.ascontiguousarray(decay.transpose(1, 0, 2).astype(np.float32)),
        "same_head": (head[:, None] == head[None, :]).astype(np.float32),
        "neg_half_grid": np.ascontiguousarray(np.broadcast_to(NEG_HALF_GRID, (P, NG))),
        "head_mask": (head[:, None] == np.arange(NH)[None, :]).astype(np.float32),
        "decay_chunk": (gammas[head] ** P).astype(np.float32)[:, None],
    }


STAGES = 3


def kernel(**inputs):
    import concourse.bacc as _bacc
    from concourse.bass_utils import run_bass_kernel_spmd as _run

    a = {k.replace("L0_attn_", "").replace("L0_ffn_", "f_"): np.asarray(v) for k, v in inputs.items()}
    con = constants()
    vectors = {
        "gate": a["f_gate_W"], "kan_g0": a["f_kan_ln_g0"].T, "kan_b0": a["f_kan_ln_b0"].T,
        "kan_g1": a["f_kan_ln_g1"].reshape(2 * NE, P).T, "kan_b1": a["f_kan_ln_b1"].reshape(2 * NE, P).T,
        "mlp_b1": a["f_mlp_b1"].reshape(4 * NE, P).T, "mlp_b2": a["f_mlp_b2"].T,
        "ln1_w": a["ln1_w"].T, "ln1_b": a["ln1_b"].T, "ln2_w": a["ln2_w"].T, "ln2_b": a["ln2_b"].T,
        "gn_w": a["gn_w"].T, "gn_b": a["gn_b"].T, "ffn_b1": a["ffn_b1"].reshape(4 * NL, P).T,
        "neg_half_grid": con.pop("neg_half_grid"), "head_mask": con.pop("head_mask"),
        "decay_chunk": con.pop("decay_chunk"),
    }
    arrays = {
        "x": a["X"].reshape(NB * NC, P, P).transpose(1, 0, 2),
        "cols": np.concatenate([vectors[k] for k in COLS], axis=1),
        "kan_rows": np.concatenate([a["f_kan_sl_b0"], a["f_kan_sl_b1"]], axis=1)[None],
        "w0": a["f_kan_sl_W0"].reshape(NE, P, NG, F2).transpose(1, 0, 2, 3),
        "w1": a["f_kan_sl_W1"].reshape(NE, 2, P, NG, P).transpose(2, 0, 1, 3, 4),
        "mw1": a["f_mlp_W1"].transpose(1, 0, 2),
        "mw2": a["f_mlp_W2"].reshape(NE, 4, P, P).transpose(2, 0, 1, 3),
        "wq": a["WQ"].transpose(2, 0, 1, 3).reshape(P, NL, P),
        "wk": a["WK"].transpose(2, 0, 1, 3).reshape(P, NL, P),
        "wv": a["WV"].transpose(2, 0, 1, 3).reshape(P, NL, P),
        "wg": a["WG"].transpose(1, 0, 2),
        "wo": a["WO"].transpose(1, 0, 2),
        "fw1": a["ffn_w1"].transpose(1, 0, 2),
        "fw2": a["ffn_w2"].reshape(NL, 4, P, P).transpose(2, 0, 1, 3),
        "b2_rows": np.broadcast_to(a["ffn_b2"][None], (P, NL, P)),
        **con,
    }
    nc = _bacc.Bacc("TRN2", target_bir_lowering=False, num_devices=1)
    arrays = {f"in_{k}": np.ascontiguousarray(v) for k, v in arrays.items()}
    args = {k[3:]: nc.dram_tensor(k, v.shape, F32, kind="ExternalInput").ap() for k, v in arrays.items()}
    args["out"] = nc.dram_tensor("out", (P, NB * NC, P), F32, kind="ExternalOutput").ap()
    args["stages"] = STAGES
    build(nc, args)
    r = _run(nc, [arrays], core_ids=[0])
    got = r.results[0]["out"]
    return np.ascontiguousarray(got.transpose(1, 0, 2)).reshape(NB, S, P)
```

```python
from contextlib import ExitStack

import concourse.bass as bass
import numpy as np
from concourse import mybir

F32 = mybir.dt.float32
F16 = mybir.dt.float16
ACT = mybir.ActivationFunctionType
ALU = mybir.AluOpType
AX_X = mybir.AxisListType.X

P = 128
EPS = 1e-5
NE = 4
NG = 8
FM = 512
F2 = 256
T = 1024
TC = T // P
NT = 4
BANK = 512
RT = 6
RB = 6
L0 = NG
L1 = 2 * NG
SLABS = L0 + L1
TILE_SLABS = NE * SLABS
W_SCALE = 2.0 ** 8
A_SCALE = 2.0 ** 8
H_SCALE = 2.0 ** 6
T_SCALE = 2.0 ** 6
BASIS_UNIT = 1.0 / (T_SCALE * T_SCALE * W_SCALE)
WHOLE = "000001101011011111111111"
OPENING = "-" * 5 + "0" * L0 + "-" * 11
CLOSING = "-" * 5 + "1" * L1
PHASE_Q = [L0 + SLABS * e for e in range(NE)]
TURN = 11
UP, GELU, HIDDEN, DOWN = (10, 12, 18, 18), (17, 19, 22, 23), (19, 19, 23, 23), (17, 18, 20, 20)
Z_OUT, Z_OUT_1, Z_SUM, VAR, Z_VAR, BROADCAST, N1 = 19, 23, 15, 17, 20, 20, 1
MLP_OUT, KAN_OUT, TURN_KAN, ADD_KAN, TURN_MLP, ADD_MLP = 2, 3, 1, 6, 5, 12
TURN_A, A_PARTS = 8, 14
EXPS, CHOOSE, GIVE, STORE = (0, 4), (0, 4), (0, 10), (0, 10)
COPY_X, STATS_A, NORM_A, STATS_N, NORM_N = (0, 12), (1, 4), (1, 9), (1, 13), (1, 16)
TURN_N, N_TURN_OUT = (2, 9), (2, 16)
SQUARE_AT_ONCE = (2, 3, 18, 21, 22, 23)
OFF_ACT = (1, 5, 10, 16, 17)
LOW_ON_POOL = (1, 3, 5, 7, 9, 11, 13, 15, 21, 23)
NL = 2
NH = 8
HD = P // NH
S = 512
NC = S // P
NB = 8
SLOTS = 2
NEG_HALF_GRID = -0.5 * np.linspace(-1.2, 0.2, NG).astype(np.float32)


def on_act(q):
    return (q - L0) % SLABS not in OFF_ACT


def on_dve(q):
    return not on_act(q)


def low_on_pool(q):
    return (q - L0) % SLABS in LOW_ON_POOL


def low_on_dve(q):
    return not low_on_pool(q)


def count(kind, q):
    return sum(kind(r) for r in range(q)) - sum(kind(r) for r in range(q, 0))


def steps(order, e, start=0, stop=None):
    q, done = PHASE_Q[e] + (SLABS - L0 if order == OPENING else 0), [0, 0]
    for p, layer in enumerate(order):
        slab = None
        if layer != "-":
            layer = int(layer)
            slab = (q, layer, done[layer])
            q += 1
            done[layer] += 1
        if p >= start and (stop is None or p < stop):
            yield p, slab


def last_l0(order, e):
    return [slab[0] for _, slab in steps(order, e) if slab and slab[1] == 0][-1]


def half_l1(order, e):
    return [slab[0] for _, slab in steps(order, e) if slab and slab[1] == 1][NG - 1]


COLS = {}
_at = 0
for _name, _n in (("gate", 8), ("kan_g0", NE), ("kan_b0", NE), ("kan_g1", 2 * NE), ("kan_b1", 2 * NE),
                  ("mlp_b1", 4 * NE), ("mlp_b2", NE), ("ln1_w", NL), ("ln1_b", NL), ("ln2_w", NL), ("ln2_b", NL),
                  ("gn_w", NL), ("gn_b", NL), ("ffn_b1", 4 * NL), ("neg_half_grid", NG), ("head_mask", NH),
                  ("decay_chunk", 1)):
    COLS[_name] = (_at, _at + _n)
    _at += _n
NCOLS = _at


def build(nc, A):
    ctx = ExitStack()
    with ctx:
        def sb(name, shape, stack=ctx, dtype=F32):
            return stack.enter_context(nc.sbuf_tensor(name, shape, dtype))

        def sem(name):
            return ctx.enter_context(nc.semaphore(name))

        small_in = sem("small_in")

        x_all = sb("x_all", [P, NB * NC, P])
        cols = sb("cols", [P, NCOLS])
        ident = sb("ident", [P, P])
        ones = sb("ones", [P, P])
        neg_half = sb("neg_half", [P, 64])
        idle = sb("idle", [P, 96])
        idle_word = iter(range(32, 96))
        tril = sb("tril", [P, 8, 8])
        w0_h, w0_l = (sb(f"w0_{part}", [P, NE, NG, F2], dtype=F16) for part in "hl")
        w1_h, w1_l = (sb(f"w1_{part}", [P, NE, 2, NG, P], dtype=F16) for part in "hl")
        mw1_h, mw1_l = (sb(f"mw1_{part}", [P, NE * FM], dtype=F16)[:] for part in "hl")
        mw2_h, mw2_l = (sb(f"mw2_{part}", [P, NE * 4 * P], dtype=F16)[:] for part in "hl")
        gate_h, gate_l = (sb(f"gate_{part}", [P, 8], dtype=F16) for part in "hl")
        z_bias = sb("z_bias", [P, NE, 2])
        o_bias = sb("o_bias", [P, NE])
        scale0 = sb("scale0", [P, NE])
        bias0 = sb("bias0", [P, NE, NG])
        scale1 = sb("scale1", [P, 2 * NE])
        bias1 = sb("bias1", [P, 2 * NE, NG])
        psum = ctx.enter_context(nc.psum_tensor("psum", [P, 8, BANK], F32))

        def hold(eng, k=None):
            k = next(idle_word) if k is None else k % 32
            if eng is nc.vector:
                nc.vector.memset(idle[:, k:k + 1], 0.0)
            else:
                nc.gpsimd.tensor_tensor(idle[:, k:k + 1], neg_half[:, 0:1], neg_half[:, 1:2], ALU.add)

        def col(name, i=0, n=1):
            a = COLS[name][0] + i
            return cols[:, a:a + n]

        with ExitStack() as tmp:
            kan_rows = sb("kan_rows", [1, NE, F2 + P], tmp)
            row_mean = sb("row_mean", [P, NE, NG], tmp)
            bias_mean = sb("bias_mean", [1, NE], tmp)
            w0_raw = sb("w0_raw", [P, 2, NG * F2], tmp)
            w1_raw = sb("w1_raw", [P, 2, 2 * NG * P], tmp)
            mw1_raw = sb("mw1_raw", [P, NE * FM], tmp)
            mw2_raw = sb("mw2_raw", [P, NE * 4 * P], tmp)
            x_in = sem("x_in")
            w0_in = [sem(f"w0_in{e}") for e in range(NE)]
            w1_in = [sem(f"w1_in{e}") for e in range(NE)]
            mlp_in = [sem("mw1_in"), sem("mw2_in")]
            prep_step = sem("prep_step")
            rows_centred = sem("rows_centred")
            rows_summed = sem("rows_summed")
            rows_turned = sem("rows_turned")
            w0_centred = sem("w0_centred")
            w0_high = sem("w0_high")
            w0_low = sem("w0_low")
            w0_summed = sem("w0_summed")
            w1_high = sem("w1_high")
            w1_low = sem("w1_low")
            w1_summed = sem("w1_summed")
            other_high = sem("other_high")
            other_low = sem("other_low")
            prep_done = sem("prep_done")
            others = ((mw1_h, mw1_l, mw1_raw), (mw2_h, mw2_l, mw2_raw))

            def flat(w):
                return w.rearrange("p a b -> p (a b)")

            with nc.Block() as block:
                @block.sync
                def _(sp):
                    for dst, src in ((cols[:], A["cols"]), (ident[:], A["ident"]), (tril[:], A["tril"]),
                                     (kan_rows[:], A["kan_rows"])):
                        sp.dma_start(dst, src).then_inc(small_in, 16)
                    for e in range(NE):
                        if e >= 2:
                            sp.wait_ge(w0_low, e - 1)
                            sp.wait_ge(w0_high, e - 1)
                            sp.wait_ge(w0_summed, e - 1)
                            sp.wait_ge(w1_low, e - 1)
                            sp.wait_ge(w1_high, e - 1)
                            sp.wait_ge(w1_summed, e - 1)
                        sp.dma_start(w0_raw[:, e % 2], flat(A["w0"][:, e])).then_inc(w0_in[e], 16)
                        sp.dma_start(w1_raw[:, e % 2], A["w1"][:, e].rearrange("p m g o -> p (m g o)")
                                     ).then_inc(w1_in[e], 16)
                        if e == 1:
                            sp.dma_start(mw1_raw[:], flat(A["mw1"])).then_inc(mlp_in[0], 16)
                            sp.dma_start(mw2_raw[:], A["mw2"].rearrange("p e j o -> p (e j o)")
                                         ).then_inc(mlp_in[1], 16)
                            sp.dma_start(x_all[:], A["x"]).then_inc(x_in, 16)
                    sp.wait_ge(x_in, 16)

                @block.vector
                def _(dve):
                    done = [0]

                    def step(ins):
                        done[0] += 1
                        ins.then_inc(prep_step, 1)
                        dve.wait_ge(prep_step, done[0])

                    def low(dst, raw, high, scale=W_SCALE):
                        return nc.vector.scalar_tensor_tensor(out=dst, in0=raw, scalar=scale, in1=high,
                                                              op0=ALU.mult, op1=ALU.subtract)

                    nc.vector.memset(ones[:], 1.0).then_inc(prep_done, 1)
                    nc.vector.memset(neg_half[:], -0.5).then_inc(prep_done, 1)
                    dve.wait_ge(small_in, 64)
                    nc.vector.tensor_scalar(scale0[:], col("kan_g0", 0, NE), 0.5, None, ALU.mult).then_inc(prep_done, 1)
                    nc.vector.tensor_scalar(scale1[:], col("kan_g1", 0, 2 * NE), 0.5, None,
                                            ALU.mult).then_inc(prep_done, 1)
                    nc.vector.scalar_tensor_tensor(
                        out=bias0[:], in0=col("kan_b0", 0, NE).unsqueeze(2).to_broadcast([P, NE, NG]), scalar=0.5,
                        in1=col("neg_half_grid", 0, NG).unsqueeze(1).to_broadcast([P, NE, NG]),
                        op0=ALU.mult, op1=ALU.add).then_inc(prep_done, 1)
                    nc.vector.scalar_tensor_tensor(
                        out=bias1[:], in0=col("kan_b1", 0, 2 * NE).unsqueeze(2).to_broadcast([P, 2 * NE, NG]),
                        scalar=0.5, in1=col("neg_half_grid", 0, NG).unsqueeze(1).to_broadcast([P, 2 * NE, NG]),
                        op0=ALU.mult, op1=ALU.add).then_inc(prep_done, 1)
                    rows = kan_rows[:, :, 0:F2]
                    step(nc.vector.tensor_reduce(bias_mean[:], rows, AX_X, ALU.add))
                    step(nc.vector.tensor_scalar(bias_mean[:], bias_mean[:], 1.0 / F2, None, ALU.mult))
                    nc.vector.tensor_tensor(rows, rows, bias_mean[:].unsqueeze(2).to_broadcast([1, NE, F2]),
                                            ALU.subtract).then_inc(rows_centred, 1)
                    for e in range(NE):
                        if e == 2:
                            dve.wait_ge(other_high, 1)
                            low(gate_l[:], col("gate", 0, 8), gate_h[:]).then_inc(other_low, 1)
                            for n, (high, lower, raw) in enumerate(others):
                                dve.wait_ge(other_high, n + 2)
                                low(lower, raw[:], high).then_inc(other_low, 1)
                        w = w0_raw[:, e % 2].rearrange("p (g o) -> p g o", o=F2)
                        dve.wait_ge(w0_in[e], 16)
                        step(nc.vector.tensor_reduce(row_mean[:, e], w, AX_X, ALU.add))
                        step(nc.vector.tensor_scalar(row_mean[:, e], row_mean[:, e], 1.0 / F2, None, ALU.mult))
                        nc.vector.tensor_tensor(w, w, row_mean[:, e].unsqueeze(2).to_broadcast([P, NG, F2]),
                                                ALU.subtract).then_inc(w0_centred, 1)
                        dve.wait_ge(w1_high, e + 1)
                        low(w1_l[:, e].rearrange("p m g o -> p (m g o)"), w1_raw[:, e % 2],
                            w1_h[:, e].rearrange("p m g o -> p (m g o)")).then_inc(w1_low, 1)
                        dve.wait_ge(w0_centred, e + 1)
                        dve.wait_ge(w0_high, e + 1)
                        low(flat(w0_l[:, e]), w0_raw[:, e % 2], flat(w0_h[:, e])).then_inc(w0_low, 1)
                    dve.wait_ge(w0_summed, NE)
                    dve.wait_ge(w1_summed, NE)
                    dve.wait_ge(rows_centred, 1)
                    nc.vector.tensor_tensor(kan_rows[:], kan_rows[:], psum[0:1, 0:NE, 0:F2 + P],
                                            ALU.add).then_inc(rows_summed, 1)
                    dve.wait_ge(rows_turned, 1)
                    nc.vector.tensor_copy(z_bias[:], psum[:, NE, 0:2 * NE].rearrange("p (e m) -> p e m", m=2)
                                          ).then_inc(prep_done, 1)
                    nc.vector.tensor_copy(o_bias[:], psum[:, NE, 2 * NE:3 * NE]).then_inc(prep_done, 1)
                    dve.wait_ge(prep_done, 8)

                @block.scalar
                def _(act):
                    act.wait_ge(small_in, 64)
                    nc.scalar.activation(gate_h[:], col("gate", 0, 8), ACT.Copy, scale=W_SCALE).then_inc(other_high, 1)
                    for e in range(NE):
                        if e == 2:
                            for n, (high, lower, raw) in enumerate(others):
                                act.wait_ge(mlp_in[n], 16)
                                nc.scalar.activation(high, raw[:], ACT.Copy, scale=W_SCALE).then_inc(other_high, 1)
                        act.wait_ge(w1_in[e], 16)
                        nc.scalar.activation(w1_h[:, e].rearrange("p m g o -> p (m g o)"), w1_raw[:, e % 2], ACT.Copy,
                                             scale=W_SCALE).then_inc(w1_high, 1)
                        act.wait_ge(w0_centred, e + 1)
                        nc.scalar.activation(flat(w0_h[:, e]), w0_raw[:, e % 2], ACT.Copy,
                                             scale=W_SCALE).then_inc(w0_high, 1)

                @block.tensor
                def _(pe):
                    pe.wait_ge(prep_done, 1)
                    for e in range(NE):
                        w = w1_raw[:, e % 2].rearrange("p (m o) -> p m o", o=P)
                        pe.wait_ge(w1_in[e], 16)
                        for m in range(2 * NG):
                            last = nc.tensor.matmul(psum[0:1, e, F2:F2 + P], ones[:, 0:1], w[:, m],
                                                    start=(m == 0), stop=(m == 2 * NG - 1))
                        last.then_inc(w1_summed, 1)
                        w = w0_raw[:, e % 2].rearrange("p (g o) -> p g o", o=F2)
                        pe.wait_ge(w0_centred, e + 1)
                        for g in range(NG):
                            last = nc.tensor.matmul(psum[0:1, e, 0:F2], ones[:, 0:1], w[:, g],
                                                    start=(g == 0), stop=(g == NG - 1))
                        last.then_inc(w0_summed, 1)
                    pe.wait_ge(rows_summed, 1)
                    for m in range(3):
                        for e in range(NE):
                            at = 2 * e + m if m < 2 else 2 * NE + e
                            last = nc.tensor.matmul(psum[:, NE, at:at + 1], kan_rows[:, e, m * P:(m + 1) * P],
                                                    ones[0:1, 0:1], start=True, stop=True)
                    last.then_inc(rows_turned, 1)

        x_copied = sem("x_copied")
        x_stored = sem("x_stored")
        gate_step = sem("gate_step")
        var_asked = sem("var_asked")
        rstd_given = sem("rstd_given")
        norm_ready = sem("norm_ready")
        a_turned = sem("a_turned")
        n_turned = sem("n_turned")
        a_h_ready = sem("a_h_ready")
        a_l_ready = sem("a_l_ready")
        n_t_ready = sem("n_t_ready")
        logits_done = sem("logits_done")
        shifted = sem("shifted")
        exp_done = sem("exp_done")
        gates_ready = sem("gates_ready")
        tanh_done = sem("tanh_done")
        act_squared = sem("act_squared")
        dve_squared = sem("dve_squared")
        dve_high = sem("dve_high")
        pool_low = sem("pool_low")
        dve_low = sem("dve_low")
        slab_used = sem("slab_used")
        hid_done = sem("hid_done")
        gelu_done = sem("gelu_done")
        hid_h_ready = sem("hid_h_ready")
        hid_ready = sem("hid_ready")
        hid_used = sem("hid_used")
        z_sq_ready = sem("z_sq_ready")
        zc_ready = sem("zc_ready")
        z_sum_ready = sem("z_sum_ready")
        z_var_done = sem("z_var_done")
        z_var_ready = sem("z_var_ready")
        z_rstd_ready = sem("z_rstd_ready")
        diag_ready = sem("diag_ready")
        bc_done = sem("bc_done")
        n1_ready = sem("n1_ready")
        z_sq0_ready = sem("z_sq0_ready")
        gated = sem("gated")
        acc_added = sem("acc_added")
        mlp_out_ready = sem("mlp_out_ready")
        kan_out_ready = sem("kan_out_ready")
        mlp_turned = sem("mlp_turned")
        kan_turned = sem("kan_turned")

        def feed_forward(tag, t0):
            tmp = ExitStack()
            with tmp:
                acc = sb(f"acc_{tag}", [P, TC, P], tmp)
                a_tok = sb(f"a_tok_{tag}", [P, TC, P], tmp)
                n_tok = sb(f"n_tok_{tag}", [P, TC, P], tmp)
                a_h = sb(f"a_h_{tag}", [P, T], tmp, F16)
                a_l = sb(f"a_l_{tag}", [P, T], tmp, F16)
                n_t = sb(f"n_t_{tag}", [P, T], tmp)
                stats = sb(f"stats_{tag}", [P, TC, 6], tmp)
                mean_var = sb(f"mean_var_{tag}", [P, TC, 2], tmp)
                var_eps = sb(f"var_eps_{tag}", [P, TC], tmp)
                rstd = sb(f"rstd_{tag}", [P, TC], tmp)
                z_var = sb(f"z_var_{tag}", [P, TC], tmp)
                z_rstd = sb(f"z_rstd_{tag}", [P, TC], tmp)
                top = sb(f"top_{tag}", [P, TC], tmp)
                e_sum = sb(f"e_sum_{tag}", [P, TC], tmp)
                probs = sb(f"probs_{tag}", [P, TC, 8], tmp)
                above = sb(f"above_{tag}", [P, TC, 8, 8], tmp)
                equal = sb(f"equal_{tag}", [P, TC, 8, 8], tmp)
                rank = sb(f"rank_{tag}", [P, TC, 8], tmp)
                next_gates = sb(f"next_gates_{tag}", [P, TC, 8], tmp)
                gates = sb(f"gates_{tag}", [P, TC, 8], tmp)
                tbuf = sb(f"tbuf_{tag}", [P, RT, T], tmp)
                basis_h = sb(f"basis_h_{tag}", [P, RB, T], tmp, F16)
                basis_l = sb(f"basis_l_{tag}", [P, RB, T], tmp, F16)
                hid = sb(f"hid_{tag}", [P, 2, T], tmp)
                hid_h = sb(f"hid_h_{tag}", [P, 2, T], tmp, F16)
                hid_l = sb(f"hid_l_{tag}", [P, 2, T], tmp, F16)
                zc = sb(f"zc_{tag}", [P, 2, T], tmp)
                z_sq = sb(f"z_sq_{tag}", [P, 2, T], tmp)
                diag = z_sq[:, 0].rearrange("p (c t) -> p c t", t=P)
                eo_mlp = z_sq[:, 1]
                eo_kan = hid[:, 0]

                ps_z = psum[:, 0:4].rearrange("p (m b) t -> p m (b t)", m=2)
                ps_mlp = psum[:, 0:2].rearrange("p b t -> p (b t)")
                ps_h = psum[:, 4:6].rearrange("p b t -> p (b t)")
                ps_kan = psum[:, 6:8].rearrange("p b t -> p (b t)")
                ps_turned = psum[:, 4:6].rearrange("p b (c f) -> p (b c) f", f=P)
                ps_bc = psum[:, 2:4].rearrange("p b t -> p (b t)")
                ps_var = psum[:, 4, 0:TC]
                ps_logit = psum[:, 5, 0:8 * TC].rearrange("p (c e) -> p c e", e=8)

                GATE_STEPS = 15
                ADDED = 2 * NE - 1
                TILE_ACT = count(on_act, TILE_SLABS)
                TILE_DVE = count(on_dve, TILE_SLABS)

                def low_done(i, q):
                    kind, done = (low_on_pool, pool_low) if low_on_pool(q) else (low_on_dve, dve_low)
                    return done, i * count(kind, TILE_SLABS) + count(kind, q) - count(kind, -RT) + 1

                def passes(engine, phase, finish):
                    phase(t0 - 1, NE - 1, OPENING)
                    phase(t0, 0, WHOLE, 0, TURN, first=True)
                    with engine.Fori(t0, t0 + NT - 1) as i:
                        phase(i, 0, WHOLE, TURN)
                        for e in range(1, NE):
                            phase(i, e, WHOLE)
                        phase(i + 1, 0, WHOLE, 0, TURN)
                    i = t0 + NT - 1
                    phase(i, 0, WHOLE, TURN, last=True)
                    for e in range(1, NE - 1):
                        phase(i, e, WHOLE, last=True)
                    phase(i, NE - 1, CLOSING, last=True)
                    finish(i)

                with nc.Block() as block:
                    @block.gpsimd
                    def _(pool):
                        if t0 == 0:
                            pool.sem_inc(x_stored, 1)
                            pool.sem_inc(acc_added, 1)
                            pool.sem_inc(pool_low, -count(low_on_pool, -RT))

                        def copy_x(i):
                            nc.gpsimd.tensor_copy(a_tok[:], x_all[:, bass.ds((i - t0) * TC, TC), :]
                                                  ).then_inc(x_copied, 1)

                        def power(i, n):
                            pool.wait_ge(var_asked, i * 2 + n)
                            nc.gpsimd.tensor_tensor(rstd[:], var_eps[:], neg_half[:, 0:TC],
                                                    ALU.pow).then_inc(rstd_given, 1)

                        def diagonal(w):
                            pool.wait_ge(z_rstd_ready, w + 1)
                            nc.gpsimd.tensor_tensor(diag, ident[:].unsqueeze(1).to_broadcast([P, TC, P]),
                                                    z_rstd[:].unsqueeze(2).to_broadcast([P, TC, P]),
                                                    ALU.mult).then_inc(diag_ready, 1)

                        def add_output(i, m, eo):
                            pool.wait_ge(gated, i * 2 * NE + m + 2)
                            if m > 1:
                                pool.wait_ge(acc_added, i * ADDED + m)
                            nc.gpsimd.tensor_tensor(acc[:], acc[:], eo.rearrange("p (c t) -> p c t", t=P),
                                                    ALU.add).then_inc(acc_added, 1)

                        def store(i):
                            pool.wait_ge(acc_added, (i + 1) * ADDED + 1)
                            hold(pool)
                            xs = x_all[:, bass.ds((i - t0) * TC, TC), :]
                            nc.gpsimd.tensor_tensor(xs, xs, acc[:], ALU.add).then_inc(x_stored, 1)

                        def phase(i, e, order, start=0, stop=None, first=False, last=False):
                            w = i * NE + e + 1
                            for p, slab in steps(order, e, start, stop):
                                if slab and low_on_pool(slab[0]):
                                    q = slab[0]
                                    pool.wait_ge(dve_high, i * TILE_SLABS + q + 1)
                                    nc.gpsimd.tensor_tensor(basis_l[:, q % RB], tbuf[:, q % RT], basis_h[:, q % RB],
                                                            ALU.subtract).then_inc(pool_low, 1)
                                if p == Z_SUM and order != CLOSING:
                                    pool.wait_ge(zc_ready, 2 * w + 2)
                                    if order != OPENING or t0:
                                        pool.wait_ge(bc_done, w)
                                    nc.gpsimd.tensor_tensor(z_sq[:, 0], zc[:, 0], zc[:, 0],
                                                            ALU.mult).then_inc(z_sq0_ready, 1)
                                    pool.wait_ge(z_sq0_ready, w + 1)
                                    pool.wait_ge(z_sq_ready, w + 1)
                                    nc.gpsimd.tensor_tensor(z_sq[:, 0], z_sq[:, 0], z_sq[:, 1],
                                                            ALU.add).then_inc(z_sum_ready, 1)
                                    pool.wait_ge(z_var_ready, w + 1)
                                    nc.gpsimd.tensor_tensor(z_rstd[:], z_var[:], neg_half[:, 0:TC],
                                                            ALU.pow).then_inc(z_rstd_ready, 1)
                                    diagonal(w)
                                if order != OPENING and p == ADD_KAN and not first:
                                    if e == 0:
                                        add_output(i - 1, ADDED, eo_kan)
                                    else:
                                        add_output(i, 2 * e - 1, eo_kan)
                                if (e, p) == STORE and not first and order != OPENING:
                                    store(i - 1)
                                if order != OPENING and p == ADD_MLP and e:
                                    add_output(i, 2 * e, eo_mlp)
                                if (e, p) == COPY_X and not last:
                                    pool.wait_ge(a_turned, i + 1)
                                    hold(pool)
                                    copy_x(i + 1)
                                if (e, p) == STATS_A and not last:
                                    power(i + 1, 1)
                                if (e, p) == STATS_N and not last:
                                    power(i + 1, 2)

                        power(t0, 1)
                        power(t0, 2)

                        def finish(i):
                            add_output(i, ADDED, eo_kan)
                            store(i)

                        passes(pool, phase, finish)
                        pool.wait_ge(x_stored, t0 + NT + 1)

                    @block.vector
                    def _(dve):
                        if t0 == 0:
                            dve.sem_inc(dve_low, -count(low_on_dve, -RT))
                            dve.sem_inc(hid_ready, 2)
                            dve.sem_inc(n1_ready, 1)
                            dve.sem_inc(gated, 1)

                        class Preparation:

                            def __init__(self, i, steps=0):
                                self.i, self.steps = i, steps

                            def step(self, ins):
                                self.steps += 1
                                ins.then_inc(gate_step, 1)
                                dve.wait_ge(gate_step, self.i * GATE_STEPS + self.steps)

                            def row_stats(self, n):
                                if n == 1:
                                    dve.wait_ge(x_copied, self.i + 1)
                                    hold(dve)
                                for c in range(TC):
                                    last = nc.vector.bn_stats(stats[:, c], a_tok[:, c])
                                self.step(last)
                                hold(dve)
                                for c in range(TC):
                                    last = nc.vector.bn_aggr(mean_var[:, c], stats[:, c])
                                self.step(last)
                                nc.vector.tensor_scalar(var_eps[:], mean_var[:, :, 1], EPS, None,
                                                        ALU.add).then_inc(var_asked, 1)

                            def row_norm(self, n):
                                dve.wait_ge(rstd_given, self.i * 2 + n)
                                dst = a_tok if n == 1 else n_tok
                                for c in range(TC):
                                    last = nc.vector.tensor_scalar(dst[:, c], a_tok[:, c], mean_var[:, c, 0:1],
                                                                   rstd[:, c:c + 1], ALU.subtract, ALU.mult)
                                last.then_inc(norm_ready, 1)
                                if n == 1:
                                    dve.wait_ge(norm_ready, self.i * 2 + 1)

                            def a_low(self):
                                dve.wait_ge(a_h_ready, self.i + 1)
                                nc.vector.scalar_tensor_tensor(out=a_l[:], in0=ps_h, scalar=A_SCALE, in1=a_h[:],
                                                               op0=ALU.mult, op1=ALU.subtract).then_inc(a_l_ready, 1)

                            def logits(self):
                                dve.wait_ge(logits_done, self.i + 1)
                                self.step(nc.vector.tensor_reduce(top[:], ps_logit, AX_X, ALU.max))
                                nc.vector.tensor_tensor(probs[:], ps_logit,
                                                        top[:].unsqueeze(2).to_broadcast([P, TC, 8]),
                                                        ALU.subtract).then_inc(shifted, 1)

                            def choose(self):
                                dve.wait_ge(exp_done, self.i + 1)
                                step = self.step
                                step(nc.vector.tensor_reduce(e_sum[:], probs[:], AX_X, ALU.add))
                                step(nc.vector.reciprocal(e_sum[:], e_sum[:]))
                                step(nc.vector.tensor_tensor(probs[:], probs[:],
                                                             e_sum[:].unsqueeze(2).to_broadcast([P, TC, 8]),
                                                             ALU.mult))
                                pj = probs[:].unsqueeze(2).to_broadcast([P, TC, 8, 8])
                                pi = probs[:].unsqueeze(3).to_broadcast([P, TC, 8, 8])
                                nc.vector.tensor_tensor(above[:], pj, pi, ALU.is_gt)
                                step(nc.vector.tensor_tensor(equal[:], pj, pi, ALU.is_equal))
                                step(nc.vector.tensor_tensor(equal[:], equal[:],
                                                             tril[:].unsqueeze(1).to_broadcast([P, TC, 8, 8]),
                                                             ALU.mult))
                                step(nc.vector.tensor_tensor(above[:], above[:], equal[:], ALU.add))
                                step(nc.vector.tensor_reduce(rank[:], above[:], AX_X, ALU.add))
                                step(nc.vector.scalar_tensor_tensor(out=next_gates[:], in0=rank[:], scalar=1.5,
                                                                    in1=probs[:], op0=ALU.is_lt, op1=ALU.mult))
                                step(nc.vector.tensor_reduce(e_sum[:], next_gates[:], AX_X, ALU.add))
                                step(nc.vector.reciprocal(e_sum[:], e_sum[:]))
                                assert self.steps == GATE_STEPS, self.steps

                            def give(self):
                                nc.vector.scalar_tensor_tensor(
                                    out=gates[:], in0=next_gates[:], scalar=0.5,
                                    in1=e_sum[:].unsqueeze(2).to_broadcast([P, TC, 8]), op0=ALU.mult,
                                    op1=ALU.mult).then_inc(gates_ready, 1)
                                dve.wait_ge(gates_ready, self.i + 1)

                        def square(i, q):
                            dve.wait_ge(tanh_done, i * TILE_SLABS + q + 1)
                            t = tbuf[:, q % RT]
                            nc.vector.scalar_tensor_tensor(out=t, in0=t, scalar=T_SCALE * T_SCALE, in1=t,
                                                           op0=ALU.mult, op1=ALU.mult).then_inc(dve_squared, 1)

                        def high(i, q):
                            if on_act(q):
                                dve.wait_ge(act_squared, i * TILE_ACT + count(on_act, q) + 1)
                            else:
                                dve.wait_ge(dve_squared, i * TILE_DVE + count(on_dve, q) + 1)
                            dve.wait_ge(slab_used, i * TILE_SLABS + q + 1)
                            nc.vector.tensor_copy(basis_h[:, q % RB], tbuf[:, q % RT]).then_inc(dve_high, 1)

                        def low(i, q):
                            if low_on_pool(q):
                                return
                            dve.wait_ge(dve_high, i * TILE_SLABS + q + 1)
                            nc.vector.tensor_tensor(basis_l[:, q % RB], tbuf[:, q % RT], basis_h[:, q % RB],
                                                    ALU.subtract).then_inc(dve_low, 1)

                        def drain(i, q):
                            high(i, q)
                            low(i, q - 1)
                            low(i, q)

                        def gate_output(n, e, kan, turned):
                            dve.wait_ge(*turned)
                            at = (NE if kan else 0) + e
                            if e == 0 and not kan:
                                out = acc[:]
                            else:
                                out = (eo_kan if kan else eo_mlp).rearrange("p (c t) -> p c t", t=P)
                            nc.vector.tensor_tensor(out, ps_turned, gates[:, :, at:at + 1].to_broadcast([P, TC, P]),
                                                    ALU.mult).then_inc(gated, 1)
                            dve.wait_ge(gated, n + 2)

                        def hidden(w, j):
                            n = 4 * w + j
                            dve.wait_ge(gelu_done, n + 2)
                            dve.wait_ge(hid_used, n + 1)
                            nc.vector.tensor_scalar(hid_h[:, j % 2], hid[:, j % 2], H_SCALE, None,
                                                    ALU.mult).then_inc(hid_h_ready, 1)
                            dve.wait_ge(hid_h_ready, n + 1)
                            nc.vector.scalar_tensor_tensor(out=hid_l[:, j % 2], in0=hid[:, j % 2],
                                                           scalar=H_SCALE, in1=hid_h[:, j % 2],
                                                           op0=ALU.mult, op1=ALU.subtract).then_inc(hid_ready, 1)

                        def phase(i, e, order, start=0, stop=None, first=False, last=False):
                            n = i * NE + e
                            w = n + 1
                            if order == CLOSING:
                                drain(i, PHASE_Q[e] - 1)
                            since = {OPENING: NE * SLABS, CLOSING: PHASE_Q[e]}.get(order, PHASE_Q[0] if first else 0)
                            for p, slab in steps(order, e, start, stop):
                                if slab:
                                    q = slab[0]
                                    if on_dve(q):
                                        square(i, q)
                                    if q - 1 >= since:
                                        high(i, q - 1)
                                    if q - 2 >= since:
                                        low(i, q - 2)
                                    if order == OPENING and q == NE * SLABS + L0 - 1:
                                        drain(i, q)
                                if order != CLOSING:
                                    for j in range(4):
                                        if p == HIDDEN[j]:
                                            hidden(w, j)
                                    if p == Z_VAR:
                                        dve.wait_ge(z_var_done, w + 2)
                                        nc.vector.tensor_scalar(z_var[:], ps_var, 1.0 / F2, EPS, ALU.mult,
                                                                ALU.add).then_inc(z_var_ready, 1)
                                if order == OPENING:
                                    if p == A_PARTS:
                                        Preparation(i + 1).a_low()
                                    if p == Z_VAR:
                                        Preparation(i + 1, steps=4).logits()
                                    continue
                                if p == N1:
                                    dve.wait_ge(bc_done, n + 1)
                                    dve.wait_ge(zc_ready, 2 * n + 3)
                                    for m in range(2):
                                        nc.vector.tensor_tensor(zc[:, m], zc[:, m], ps_bc,
                                                                ALU.mult).then_inc(n1_ready, 1)
                                if (e, p) == CHOOSE:
                                    Preparation(i, steps=5).choose()
                                if p == ADD_KAN and not first:
                                    gate_output(2 * n - 1, (e - 1) % NE, True, (kan_turned, n + 1))
                                if (e, p) == GIVE:
                                    Preparation(i).give()
                                if p == ADD_MLP:
                                    if e == 0:
                                        dve.wait_ge(x_stored, i + 1)
                                    gate_output(2 * n, e, False, (mlp_turned, n + 2))
                                if not last:
                                    following = Preparation(i + 1)
                                    if (e, p) == STATS_A:
                                        following.row_stats(1)
                                    if (e, p) == NORM_A:
                                        following.row_norm(1)
                                    if (e, p) == STATS_N:
                                        following.steps = 2
                                        following.row_stats(2)
                                    if (e, p) == NORM_N:
                                        following.row_norm(2)
                                    if (e, p) == (NE - 1, A_PARTS):
                                        following.a_low()
                                    if (e, p) == (NE - 1, Z_VAR):
                                        following.steps = 4
                                        following.logits()

                        def finish(i):
                            drain(i, NE * SLABS - 1)
                            gate_output((i + 1) * 2 * NE - 1, NE - 1, True, (kan_turned, (i + 1) * NE + 1))

                        begin = Preparation(t0)
                        begin.row_stats(1)
                        begin.row_norm(1)
                        begin.row_stats(2)
                        begin.row_norm(2)
                        passes(dve, phase, finish)

                    @block.scalar
                    def _(act):
                        if t0 == 0:
                            act.sem_inc(gelu_done, 1)
                            act.sem_inc(zc_ready, 1)

                        def n_turn_out(i):
                            act.wait_ge(n_turned, i + 1)
                            nc.scalar.activation(n_t[:], ps_h, ACT.Copy).then_inc(n_t_ready, 1)
                            act.wait_ge(n_t_ready, i + 1)

                        def tanh(i, q, layer, e, s):
                            act.wait_ge(*low_done(i, q - RT))
                            if layer == 0:
                                src, sc, bi = n_t[:], scale0[:, e:e + 1], bias0[:, e, s:s + 1]
                            else:
                                m, g = divmod(s, NG)
                                if g == 0:
                                    act.wait_ge(n1_ready, i * 2 * NE + 2 * e + m + 2)
                                src, sc, bi = zc[:, m], scale1[:, 2 * e + m:2 * e + m + 1], bias1[:, 2 * e + m, g:g + 1]
                            nc.scalar.activation(tbuf[:, q % RT], src, ACT.Tanh, bias=bi, scale=sc
                                                 ).then_inc(tanh_done, 1)

                        def square(i, q):
                            if on_act(q):
                                act.wait_ge(tanh_done, i * TILE_SLABS + q + 1)
                                t = tbuf[:, q % RT]
                                nc.scalar.activation(t, t, ACT.Square, scale=T_SCALE).then_inc(act_squared, 1)

                        def gelu(w, e, j):
                            act.wait_ge(hid_done, 4 * w + j + 1)
                            act.wait_ge(hid_ready, 4 * w + j + 1)
                            nc.scalar.activation(hid[:, j % 2], ps_h, ACT.Gelu, bias=col("mlp_b1", 4 * e + j),
                                                 scale=1.0 / (A_SCALE * W_SCALE)).then_inc(gelu_done, 1)

                        def z_square(e, m):
                            nc.scalar.activation(z_sq[:, m], ps_z[:, m], ACT.Square, bias=z_bias[:, e, m:m + 1],
                                                 scale=-BASIS_UNIT).then_inc(z_sq_ready, 1)

                        def z_copy(e, m):
                            nc.scalar.activation(zc[:, m], ps_z[:, m], ACT.Identity, bias=z_bias[:, e, m:m + 1],
                                                 scale=-BASIS_UNIT).then_inc(zc_ready, 1)

                        def kan_out(n, e, used):
                            act.wait_ge(slab_used, used)
                            act.wait_ge(kan_turned, n + 1)
                            nc.scalar.activation(eo_kan, ps_kan, ACT.Identity, bias=o_bias[:, e:e + 1],
                                                 scale=-BASIS_UNIT).then_inc(kan_out_ready, 1)

                        def phase(i, e, order, start=0, stop=None, first=False, last=False):
                            n = i * NE + e
                            w, ew = n + 1, (e + 1) % NE
                            if order == CLOSING and SLABS - 1 not in SQUARE_AT_ONCE:
                                square(i, PHASE_Q[e] - 1)
                            since = {OPENING: NE * SLABS, CLOSING: PHASE_Q[e]}.get(order, PHASE_Q[0] if first else 0)
                            for p, slab in steps(order, e, start, stop):
                                if slab:
                                    q, layer, s = slab
                                    tanh(i, q, layer, e if layer else ew, s)
                                    if q - 1 >= since and (p - 1) % SLABS not in SQUARE_AT_ONCE:
                                        square(i, q - 1)
                                    if p in SQUARE_AT_ONCE or order == OPENING and q == last_l0(order, e):
                                        square(i, q)
                                if order != CLOSING:
                                    if p == GELU[0]:
                                        if order != OPENING and not first:
                                            act.wait_ge(acc_added, i * ADDED + 2 * e + 1)
                                        gelu(w, ew, 0)
                                    if p == Z_OUT:
                                        act.wait_ge(slab_used, i * TILE_SLABS + last_l0(order, e) + 1 + RB)
                                        if order != OPENING:
                                            act.wait_ge(tanh_done, i * TILE_SLABS + half_l1(order, e) + 1)
                                        z_copy(ew, 0)
                                        z_square(ew, 1)
                                    for j in range(1, 4):
                                        if p == GELU[j]:
                                            gelu(w, ew, j)
                                    if p == Z_OUT_1:
                                        if order != OPENING:
                                            act.wait_ge(tanh_done, i * TILE_SLABS + PHASE_Q[e] + SLABS)
                                        z_copy(ew, 1)
                                if p == A_PARTS and (order == OPENING or e == NE - 1 and not last):
                                    act.wait_ge(a_turned, i + 2)
                                    nc.scalar.activation(a_h[:], ps_h, ACT.Copy, scale=A_SCALE).then_inc(a_h_ready, 1)
                                if order == OPENING:
                                    continue
                                if p == MLP_OUT:
                                    act.wait_ge(hid_used, 4 * n + 4 + 2)
                                    act.wait_ge(mlp_turned, n + 1)
                                    nc.scalar.activation(eo_mlp, ps_mlp, ACT.Identity, bias=col("mlp_b2", e),
                                                         scale=1.0 / (H_SCALE * W_SCALE)).then_inc(mlp_out_ready, 1)
                                if p == KAN_OUT and not first:
                                    kan_out(n - 1, (e - 1) % NE, i * TILE_SLABS + PHASE_Q[e] + RB)
                                if (e, p) == EXPS:
                                    act.wait_ge(shifted, i + 1)
                                    nc.scalar.activation(probs[:], probs[:], ACT.Exp,
                                                         scale=1.0 / (A_SCALE * W_SCALE)).then_inc(exp_done, 1)
                                if (e, p) == N_TURN_OUT and not last:
                                    act.wait_ge(tanh_done, i * TILE_SLABS + last_l0(order, e) + 1)
                                    n_turn_out(i + 1)

                        def finish(i):
                            square(i, NE * SLABS - 1)
                            kan_out((i + 1) * NE - 1, NE - 1, (i + 1) * TILE_SLABS + RB)

                        nc.scalar.activation(a_tok[:], x_all[:, 0:TC], ACT.Copy).then_inc(x_copied, 1)
                        n_turn_out(t0)
                        passes(act, phase, finish)

                    @block.tensor
                    def _(pe):
                        if t0 == 0:
                            pe.sem_inc(slab_used, RB)
                            pe.sem_inc(hid_used, 2)
                            pe.sem_inc(z_var_done, 1)
                            pe.sem_inc(mlp_turned, 1)
                            pe.sem_inc(kan_turned, 1)

                        def split_product(outs, w_h, w_l, x_h, x_l, start, stop):
                            for n, (w, x) in enumerate(((w_h, x_h), (w_h, x_l), (w_l, x_h))):
                                for b, out in enumerate(outs):
                                    last = nc.tensor.matmul(out, w, x(b), start=(start and n == 0),
                                                            stop=(stop and n == 2))
                            return last

                        def half(buf):
                            return lambda b: buf[:, b * BANK:(b + 1) * BANK]

                        def turn(src):
                            for c in range(TC):
                                last = nc.tensor.transpose(ps_turned[:, c], src(c), ident[:])
                            return last

                        def turn_a(i):
                            pe.wait_ge(norm_ready, i * 2 + 1)
                            turn(lambda c: a_tok[:, c]).then_inc(a_turned, 1)

                        def turn_n(i):
                            pe.wait_ge(norm_ready, i * 2 + 2)
                            turn(lambda c: n_tok[:, c]).then_inc(n_turned, 1)

                        def gate_logits(i):
                            for c in range(TC):
                                at = slice(c * P, (c + 1) * P)
                                nc.tensor.matmul(ps_logit[:, c], a_h[:, at], gate_h[:], start=True, stop=False)
                                nc.tensor.matmul(ps_logit[:, c], a_h[:, at], gate_l[:], start=False, stop=False)
                                last = nc.tensor.matmul(ps_logit[:, c], a_l[:, at], gate_h[:], start=False, stop=True)
                            last.then_inc(logits_done, 1)

                        def multiply_slab(i, q, layer, e, s):
                            pe.wait_ge(*low_done(i, q))
                            x_h, x_l = half(basis_h[:, q % RB]), half(basis_l[:, q % RB])
                            if layer == 0:
                                for m in range(2):
                                    at = slice(m * P, (m + 1) * P)
                                    done = split_product([psum[:, 2 * m], psum[:, 2 * m + 1]], w0_h[:, e, s, at],
                                                         w0_l[:, e, s, at], x_h, x_l, s == 0, s == L0 - 1)
                            else:
                                m, g = divmod(s, NG)
                                done = split_product([psum[:, 6], psum[:, 7]], w1_h[:, e, m, g], w1_l[:, e, m, g],
                                                     x_h, x_l, s == 0, s == L1 - 1)
                            done.then_inc(slab_used, 1)

                        def mlp_up(w, e, j):
                            if j:
                                pe.wait_ge(gelu_done, 4 * w + j + 1)
                            at = slice(e * FM + j * P, e * FM + (j + 1) * P)
                            split_product([psum[:, 4], psum[:, 5]], mw1_h[:, at], mw1_l[:, at], half(a_h),
                                          half(a_l), True, True).then_inc(hid_done, 1)

                        def mlp_down(w, e, j):
                            pe.wait_ge(hid_ready, 4 * w + j + 1 + 2)
                            at = slice((4 * e + j) * P, (4 * e + j + 1) * P)
                            split_product([psum[:, 0], psum[:, 1]], mw2_h[:, at], mw2_l[:, at],
                                          half(hid_h[:, j % 2]), half(hid_l[:, j % 2]), j == 0, j == 3
                                          ).then_inc(hid_used, 1)

                        def turn_kan(n):
                            pe.wait_ge(kan_out_ready, n + 1)
                            pe.wait_ge(gated, 2 * n + 2)
                            turn(lambda c: eo_kan[:, c * P:(c + 1) * P]).then_inc(kan_turned, 1)

                        def broadcast(n):
                            pe.wait_ge(diag_ready, n + 1)
                            for b in range(2):
                                done = nc.tensor.matmul(
                                    psum[:, 2 + b], ones[:], diag[:, 4 * b:4 * b + 4].rearrange("p c t -> p (c t)"),
                                    start=True, stop=True)
                            done.then_inc(bc_done, 1)

                        def phase(i, e, order, start=0, stop=None, first=False, last=False):
                            n = i * NE + e
                            w, ew = n + 1, (e + 1) % NE
                            for p, slab in steps(order, e, start, stop):
                                if slab:
                                    q, layer, s = slab
                                    if (layer, s) == (0, 0) and order != OPENING:
                                        pe.wait_ge(n1_ready, 2 * n + 3)
                                        pe.wait_ge(mlp_out_ready, n + 1)
                                    if (layer, s) == (1, 0) and not first:
                                        pe.wait_ge(kan_out_ready, n)
                                    multiply_slab(i, q, layer, e if layer else ew, s)
                                if p == TURN_A and (order == OPENING or e == NE - 1 and not last):
                                    if order != OPENING:
                                        pe.wait_ge(gated, 2 * n + 2)
                                    turn_a(i + 1)
                                if order != CLOSING:
                                    if p == UP[0]:
                                        if order == OPENING or e == NE - 1:
                                            pe.wait_ge(a_l_ready, i + 2)
                                        else:
                                            pe.wait_ge(gated, 2 * n + 2)
                                        if e == N_TURN_OUT[0] and not last:
                                            pe.wait_ge(n_t_ready, i + 2)
                                        mlp_up(w, ew, 0)
                                    for j in range(1, 4):
                                        if p == UP[j]:
                                            if UP[j] > VAR:
                                                pe.wait_ge(z_var_ready, w + 1)
                                                if order == OPENING or e == NE - 1:
                                                    pe.wait_ge(shifted, i + 2)
                                            mlp_up(w, ew, j)
                                    if p == VAR:
                                        pe.wait_ge(gelu_done, 4 * w + 1 + sum(up <= VAR for up in UP))
                                        pe.wait_ge(z_sum_ready, w + 1)
                                        for c in range(TC):
                                            done = nc.tensor.matmul(
                                                ps_var[:, c:c + 1], z_sq[:, 0, c * P:(c + 1) * P], ones[:, 0:1],
                                                start=True, stop=True)
                                        done.then_inc(z_var_done, 1)
                                        if order == OPENING or e == NE - 1:
                                            gate_logits(i + 1)
                                    if p == DOWN[0]:
                                        pe.wait_ge(zc_ready, 2 * w + 2)
                                        mlp_down(w, ew, 0)
                                    if p == DOWN[1]:
                                        mlp_down(w, ew, 1)
                                    if p == DOWN[2]:
                                        mlp_down(w, ew, 2)
                                    if p == BROADCAST:
                                        pe.wait_ge(zc_ready, 2 * w + 3)
                                        broadcast(w)
                                    if p == DOWN[3]:
                                        mlp_down(w, ew, 3)
                                if order == OPENING:
                                    continue
                                if p == TURN_KAN and not first:
                                    pe.wait_ge(z_var_ready, n + 1)
                                    if e == 0:
                                        pe.wait_ge(shifted, i + 1)
                                    turn_kan(n - 1)
                                if p == TURN_MLP:
                                    pe.wait_ge(mlp_out_ready, n + 1)
                                    if first:
                                        pe.wait_ge(shifted, i + 1)
                                    pe.wait_ge(gated, 2 * n + 1)
                                    turn(lambda c: eo_mlp[:, c * P:(c + 1) * P]).then_inc(mlp_turned, 1)
                                if (e, p) == TURN_N and not last:
                                    pe.wait_ge(gated, 2 * n + 2)
                                    turn_n(i + 1)

                        def finish(i):
                            turn_kan((i + 1) * NE - 1)

                        turn_n(t0)
                        pe.wait_ge(n_t_ready, t0 + 1)
                        passes(pe, phase, finish)

        def retention():
            tmp = ExitStack()
            with tmp:
                def many(name, shape):
                    return [sb(f"{name}_{s}", shape, tmp) for s in range(SLOTS)]

                wq = sb("wq", [P, NL, P], tmp)
                wk = sb("wk", [P, NL, P], tmp)
                wv = sb("wv", [P, NL, P], tmp)
                wg = sb("wg", [P, NL, P], tmp)
                wo = sb("wo", [P, NL, P], tmp)
                wq_rot = sb("wq_rot", [P, NL, P], tmp)
                wk_rot = sb("wk_rot", [P, NL, P], tmp)
                fw1 = sb("fw1", [P, NL, FM], tmp)
                fw2 = sb("fw2", [P, NL, 4, P], tmp)
                b2_rows = sb("b2_rows", [P, NL, P], tmp)
                cos_q = sb("cos_q", [P, S], tmp)
                sin_q = sb("sin_q", [P, S], tmp)
                cos_k = sb("cos_k", [P, S], tmp)
                sin_k = sb("sin_k", [P, S], tmp)
                decay_q = sb("decay_q", [P, P], tmp)
                decay_k = sb("decay_k", [P, P], tmp)
                decay_qk = sb("decay_qk", [P, NH, P], tmp)
                same_head = sb("same_head", [P, P], tmp)

                u = many("u", [P, NC, P])
                row = many("row", [P, NC, P])
                col_in = many("col_in", [P, S])
                q = many("q", [P, S])
                qd = many("qd", [P, S])
                k = many("k", [P, S])
                part = many("part", [P, S])
                v = many("v", [P, NC, P])
                kd = many("kd", [P, NC, P])
                gate = many("gate", [P, S])
                big = many("big", [P, 4, S])
                state = many("state", [P, NC, P])
                stats = many("r_stats", [P, NC, 6])
                mean_var = many("r_mean_var", [P, NC, 2])
                var_eps = many("r_var_eps", [P, NC * NH])
                rstd = many("r_rstd", [P, NC * NH])
                mean = many("r_mean", [P, NC * NH])
                odd = many("odd", [P, 4, S])
                k_head, scores = ([[b[:, at:at + 2].rearrange("p a (h t) -> p (a h) t", t=P) for b in pair]
                                   for pair in zip(big, odd)] for at in (0, 2))

                def bank(s, n):
                    return psum[:, 4 * s + n]

                def bank_c(s, n):
                    return psum[:, 4 * s + n].rearrange("p (c f) -> p c f", f=P)

                def sems(name):
                    return [sem(f"{name}_{s}") for s in range(SLOTS)]

                qk_in = sem("qk_in")
                r_in = sem("r_in")
                rot_done = sem("rot_done")
                r_step = sem("r_step")
                x_got = sems("x_got")
                x_put = sems("x_put")
                u_ready = sems("u_ready")
                var_asked = sems("r_var_asked")
                rstd_given = sems("r_rstd_given")
                n1_row = sems("n1_row")
                n1_turned = sems("n1_turned")
                n1_col = sems("n1_col")
                q_done = sems("q_done")
                k_done = sems("k_done")
                q_ready = sems("q_ready")
                k_ready = sems("k_ready")
                qd_ready = sems("qd_ready")
                g_done = sems("g_done")
                v_done = sems("v_done")
                kt_done = sems("kt_done")
                g_ready = sems("g_ready")
                v_ready = sems("v_ready")
                kd_ready = sems("kd_ready")
                kh_ready = sems("kh_ready")
                sc_done = sems("sc_done")
                sc_ready = sems("sc_ready")
                kv_done = sems("kv_done")
                state_ready = sems("state_ready")
                y_done = sems("y_done")
                y_inv = sems("y_inv")
                y_rstd = sems("y_rstd")
                y_row = sems("y_row")
                y_turned = sems("y_turned")
                y_col = sems("y_col")
                gy_ready = sems("gy_ready")
                wo_done = sems("wo_done")
                u2_ready = sems("u2_ready")
                ub_ready = sems("ub_ready")
                n2_row = sems("n2_row")
                n2_turned = sems("n2_turned")
                n2_col = sems("n2_col")
                h_done = sems("h_done")
                h_ready = sems("h_ready")
                w2_done = sems("w2_done")
                ITER = NB // SLOTS
                R_ARRAYS = 14
                R_STEPS = SLOTS * (2 + NL * 14)
                VARS = 1 + 2 * NL

                with nc.Block() as block:
                    @block.sync
                    def _(sp):
                        for dst, name in ((wq, "wq"), (wk, "wk")):
                            sp.dma_start(dst[:], A[name]).then_inc(qk_in, 16)
                        others = ((cos_q, "cos_q"), (sin_q, "sin_q"), (cos_k, "cos_k"), (sin_k, "sin_k"),
                                  (decay_q, "decay_q"), (wg, "wg"), (wv, "wv"), (decay_k, "decay_k"),
                                  (decay_qk, "decay_qk"), (same_head, "same_head"), (wo, "wo"), (fw1, "fw1"),
                                  (fw2, "fw2"), (b2_rows, "b2_rows"))
                        assert len(others) == R_ARRAYS
                        for dst, name in others:
                            sp.dma_start(dst[:], A[name]).then_inc(r_in, 16)
                        sp.wait_ge(qk_in, 32)
                        sp.wait_ge(r_in, 16 * R_ARRAYS)

                    @block.gpsimd
                    def _(pool):
                        for s in range(SLOTS):
                            pool.sem_inc(x_put[s], 1)
                        with pool.Fori(0, ITER) as i:
                            def power(s, n):
                                pool.wait_ge(var_asked[s], i * VARS + n)
                                nc.gpsimd.tensor_tensor(rstd[s][:, 0:NC], var_eps[s][:, 0:NC], neg_half[:, 0:NC],
                                                        ALU.pow).then_inc(rstd_given[s], 1)

                            for s in range(SLOTS):
                                pool.wait_ge(n2_turned[s], i * NL + 1)
                                hold(pool)
                                nc.gpsimd.tensor_copy(row[s][:], x_all[:, bass.ds(i * SLOTS * NC + s * NC, NC), :]
                                                      ).then_inc(x_got[s], 1)
                            for s in range(SLOTS):
                                power(s, 1)
                            for l in range(NL):
                                n = i * NL + l + 1
                                for s in range(SLOTS):
                                    power(s, 2 + 2 * l)
                                pool.wait_ge(r_in, 16 * R_ARRAYS)
                                for s in range(SLOTS):
                                    pool.wait_ge(q_ready[s], n)
                                    nc.gpsimd.tensor_tensor(
                                        qd[s][:].rearrange("p (c t) -> p c t", t=P),
                                        q[s][:].rearrange("p (c t) -> p c t", t=P),
                                        decay_q[:].unsqueeze(1).to_broadcast([P, NC, P]),
                                        ALU.mult).then_inc(qd_ready[s], 1)
                                for c in range(NC):
                                    for s in range(SLOTS):
                                        if c == 0:
                                            pool.wait_ge(k_ready[s], n)
                                            pool.wait_ge(w2_done[s], n)
                                        elif c > 1:
                                            pool.wait_ge(sc_done[s], (i * NL + l) * NC + c - 1)
                                        nc.gpsimd.tensor_tensor(
                                            k_head[s][c % 2],
                                            k[s][:, c * P:(c + 1) * P].unsqueeze(1).to_broadcast([P, NH, P]),
                                            col("head_mask", 0, NH).unsqueeze(2).to_broadcast([P, NH, P]),
                                            ALU.mult).then_inc(kh_ready[s], 1)
                                for s in range(SLOTS):
                                    pool.wait_ge(u2_ready[s], n)
                                    power(s, 3 + 2 * l)
                                    nc.gpsimd.tensor_tensor(part[s][:].rearrange("p (c f) -> p c f", f=P), u[s][:],
                                                            b2_rows[:, l].unsqueeze(1).to_broadcast([P, NC, P]),
                                                            ALU.add).then_inc(ub_ready[s], 1)
                            for s in range(SLOTS):
                                pool.wait_ge(u_ready[s], (i + 1) * (NL + 1))
                                hold(pool)
                                xs = x_all[:, bass.ds(i * SLOTS * NC + s * NC, NC), :]
                                nc.gpsimd.tensor_tensor(xs, xs, u[s][:], ALU.add).then_inc(x_put[s], 1)
                            for s in range(SLOTS):
                                pool.wait_ge(x_put[s], i + 2)

                    @block.vector
                    def _(dve):
                        dve.wait_ge(qk_in, 32)
                        for w, w_rot in ((wq, wq_rot), (wk, wk_rot)):
                            pairs = w[:].rearrange("p l (n two) -> p l n two", two=2)
                            rot = w_rot[:].rearrange("p l (n two) -> p l n two", two=2)
                            nc.vector.tensor_scalar(rot[:, :, :, 0], pairs[:, :, :, 1], -1.0, None,
                                                    ALU.mult).then_inc(rot_done, 1)
                            nc.vector.tensor_copy(rot[:, :, :, 1], pairs[:, :, :, 0]).then_inc(rot_done, 1)
                        with dve.Fori(0, ITER) as i:
                            done = [0]

                            def step(ins):
                                done[0] += 1
                                ins.then_inc(r_step, 1)
                                dve.wait_ge(r_step, i * R_STEPS + done[0])

                            def normalise(s, dst, src, n, ready, value):
                                for c in range(NC):
                                    last = nc.vector.bn_stats(stats[s][:, c], src[:, c])
                                step(last)
                                hold(dve)
                                for c in range(NC):
                                    last = nc.vector.bn_aggr(mean_var[s][:, c], stats[s][:, c])
                                step(last)
                                nc.vector.tensor_scalar(var_eps[s][:, 0:NC], mean_var[s][:, :, 1], EPS, None,
                                                        ALU.add).then_inc(var_asked[s], 1)

                                def rest():
                                    dve.wait_ge(rstd_given[s], i * VARS + n)
                                    for c in range(NC):
                                        last = nc.vector.tensor_scalar(dst[:, c], src[:, c], mean_var[s][:, c, 0:1],
                                                                       rstd[s][:, c:c + 1], ALU.subtract, ALU.mult)
                                    last.then_inc(ready, 1)
                                    dve.wait_ge(ready, value)
                                return rest

                            def both(f):
                                rests = [f(s) for s in range(SLOTS)]
                                for r in rests:
                                    r()

                            def first(s):
                                dve.wait_ge(x_got[s], i + 1)
                                dve.wait_ge(x_put[s], i + 1)
                                return normalise(s, u[s], row[s], 1, u_ready[s], i * (NL + 1) + 1)

                            both(first)
                            for l in range(NL):
                                n = i * NL + l + 1
                                both(lambda s: normalise(s, row[s], u[s], 2 + 2 * l, n1_row[s], n))
                                dve.wait_ge(r_in, 16 * R_ARRAYS)
                                for s in range(SLOTS):
                                    dve.wait_ge(q_done[s], n)
                                    nc.vector.tensor_tensor(part[s][:], bank(s, 1), cos_q[:], ALU.mult)
                                    step(nc.vector.tensor_tensor(q[s][:], bank(s, 2), sin_q[:], ALU.mult))
                                    nc.vector.tensor_tensor(q[s][:], q[s][:], part[s][:], ALU.add
                                                            ).then_inc(q_ready[s], 1)
                                    dve.wait_ge(q_ready[s], n)
                                    dve.wait_ge(k_done[s], n)
                                    nc.vector.tensor_tensor(part[s][:], bank(s, 3), cos_k[:], ALU.mult)
                                    step(nc.vector.tensor_tensor(k[s][:], bank(s, 0), sin_k[:], ALU.mult))
                                    nc.vector.tensor_tensor(k[s][:], k[s][:], part[s][:], ALU.add
                                                            ).then_inc(k_ready[s], 1)
                                for s in range(SLOTS):
                                    dve.wait_ge(kt_done[s], n)
                                    nc.vector.tensor_tensor(kd[s][:], bank_c(s, 3),
                                                            decay_k[:].unsqueeze(1).to_broadcast([P, NC, P]),
                                                            ALU.mult).then_inc(kd_ready[s], 1)

                                def decay(s, c):
                                    at = (i * NL + l) * NC + c
                                    dve.wait_ge(sc_done[s], at + 1)
                                    if c > 1:
                                        dve.wait_ge(y_done[s], at - 1)
                                    nc.vector.tensor_tensor(
                                        scores[s][c % 2],
                                        psum[:, 4 * s:4 * s + 2].rearrange("p a (h t) -> p (a h) t", t=P),
                                        decay_qk[:], ALU.mult).then_inc(sc_ready[s], 1)

                                for s in range(SLOTS):
                                    decay(s, 0)
                                for s in range(SLOTS):
                                    dve.wait_ge(kv_done[s], n)
                                    step(nc.vector.tensor_tensor(state[s][:, 1:4], bank_c(s, 2)[:, 0:3],
                                                                 same_head[:].unsqueeze(1).to_broadcast([P, 3, P]),
                                                                 ALU.mult))
                                    step(nc.vector.scalar_tensor_tensor(
                                        out=state[s][:, 2], in0=state[s][:, 1], scalar=col("decay_chunk"),
                                        in1=state[s][:, 2], op0=ALU.mult, op1=ALU.add))
                                    nc.vector.scalar_tensor_tensor(
                                        out=state[s][:, 3], in0=state[s][:, 2], scalar=col("decay_chunk"),
                                        in1=state[s][:, 3], op0=ALU.mult, op1=ALU.add).then_inc(state_ready[s], 1)
                                for c in range(1, NC):
                                    for s in range(SLOTS):
                                        decay(s, c)

                                def group_norm(s):
                                    dve.wait_ge(y_done[s], n * NC)
                                    y = bank(s, 3).rearrange("p (g f) -> p g f", f=HD)
                                    yc = row[s][:].rearrange("p c (h f) -> p (c h) f", f=HD)
                                    sq = part[s][:].rearrange("p (g f) -> p g f", f=HD)
                                    step(nc.vector.tensor_reduce(mean[s][:], y, AX_X, ALU.add))
                                    step(nc.vector.tensor_scalar(mean[s][:], mean[s][:], 1.0 / HD, None, ALU.mult))
                                    step(nc.vector.tensor_tensor(
                                        yc, y, mean[s][:].unsqueeze(2).to_broadcast([P, NC * NH, HD]), ALU.subtract))
                                    step(nc.vector.tensor_tensor(sq, yc, yc, ALU.mult))
                                    step(nc.vector.tensor_reduce(var_eps[s][:], sq, AX_X, ALU.add))
                                    step(nc.vector.tensor_scalar(var_eps[s][:], var_eps[s][:], 1.0 / HD, EPS,
                                                                 ALU.mult, ALU.add))
                                    nc.vector.reciprocal(var_eps[s][:], var_eps[s][:]).then_inc(y_inv[s], 1)

                                    def rest():
                                        dve.wait_ge(y_rstd[s], n)
                                        nc.vector.tensor_tensor(
                                            yc, yc, rstd[s][:].unsqueeze(2).to_broadcast([P, NC * NH, HD]),
                                            ALU.mult).then_inc(y_row[s], 1)
                                    return rest

                                both(group_norm)
                                for s in range(SLOTS):
                                    dve.wait_ge(y_col[s], n)
                                    dve.wait_ge(g_ready[s], n)
                                    nc.vector.tensor_tensor(col_in[s][:], col_in[s][:], gate[s][:], ALU.mult
                                                            ).then_inc(gy_ready[s], 1)

                                def second(s):
                                    dve.wait_ge(wo_done[s], n)
                                    nc.vector.tensor_tensor(u[s][:], bank_c(s, 1), u[s][:], ALU.add
                                                            ).then_inc(u2_ready[s], 1)
                                    dve.wait_ge(u2_ready[s], n)
                                    dve.wait_ge(y_turned[s], n)
                                    return normalise(s, row[s], u[s], 3 + 2 * l, n2_row[s], n)

                                both(second)
                                for s in range(SLOTS):
                                    dve.wait_ge(w2_done[s], n + 1)
                                    dve.wait_ge(ub_ready[s], n)
                                    nc.vector.tensor_tensor(u[s][:], bank_c(s, 3),
                                                            part[s][:].rearrange("p (c f) -> p c f", f=P), ALU.add
                                                            ).then_inc(u_ready[s], 1)
                                    dve.wait_ge(u_ready[s], i * (NL + 1) + l + 2)
                            assert done[0] == R_STEPS, done

                    @block.scalar
                    def _(act):
                        for s in range(SLOTS):
                            act.sem_inc(h_ready[s], 1)
                        with act.Fori(0, ITER) as i:
                            for l in range(NL):
                                n = i * NL + l + 1
                                for s in range(SLOTS):
                                    act.wait_ge(n1_turned[s], n)
                                    nc.scalar.activation(col_in[s][:], bank(s, 0), ACT.Identity, bias=col("ln1_b", l),
                                                         scale=col("ln1_w", l)).then_inc(n1_col[s], 1)
                                for s in range(SLOTS):
                                    act.wait_ge(g_done[s], n)
                                    nc.scalar.activation(gate[s][:], bank(s, 1), ACT.Silu).then_inc(g_ready[s], 1)
                                    act.wait_ge(v_done[s], n)
                                    nc.scalar.activation(v[s][:], bank_c(s, 2), ACT.Copy).then_inc(v_ready[s], 1)
                                for s in range(SLOTS):
                                    act.wait_ge(y_inv[s], n)
                                    nc.scalar.activation(rstd[s][:], var_eps[s][:], ACT.Sqrt).then_inc(y_rstd[s], 1)
                                for s in range(SLOTS):
                                    act.wait_ge(y_turned[s], n)
                                    nc.scalar.activation(col_in[s][:], bank(s, 0), ACT.Identity, bias=col("gn_b", l),
                                                         scale=col("gn_w", l)).then_inc(y_col[s], 1)
                                for s in range(SLOTS):
                                    act.wait_ge(n2_turned[s], n + 1)
                                    nc.scalar.activation(col_in[s][:], bank(s, 2), ACT.Identity, bias=col("ln2_b", l),
                                                         scale=col("ln2_w", l)).then_inc(n2_col[s], 1)
                                for j in range(4):
                                    for s in range(SLOTS):
                                        act.wait_ge(h_done[s], (i * NL + l) * 4 + j + 1)
                                        nc.scalar.activation(big[s][:, j], bank(s, j % 3), ACT.Silu,
                                                             bias=col("ffn_b1", 4 * l + j)).then_inc(h_ready[s], 1)

                    @block.tensor
                    def _(pe):
                        pe.wait_ge(qk_in, 32)
                        pe.wait_ge(rot_done, 4)
                        for s in range(SLOTS):
                            pe.sem_inc(n2_turned[s], 1)
                            pe.sem_inc(w2_done[s], 1)
                        with pe.Fori(0, ITER) as i:
                            def turn(dst, src, done_sem):
                                for c in range(NC):
                                    last = nc.tensor.transpose(dst[:, c], src[:, c], ident[:])
                                last.then_inc(done_sem, 1)

                            def product(dst, w, rhs):
                                return nc.tensor.matmul(dst, w, rhs, start=True, stop=True)

                            for l in range(NL):
                                n = i * NL + l + 1
                                at = (i * NL + l) * NC
                                for s in range(SLOTS):
                                    pe.wait_ge(n1_row[s], n)
                                    pe.wait_ge(h_ready[s], at + 1)
                                    turn(bank_c(s, 0), row[s], n1_turned[s])
                                for s in range(SLOTS):
                                    pe.wait_ge(n1_col[s], n)
                                    product(bank(s, 1), wq[:, l], col_in[s][:])
                                    product(bank(s, 2), wq_rot[:, l], col_in[s][:]).then_inc(q_done[s], 1)
                                    pe.wait_ge(u_ready[s], i * (NL + 1) + l + 1)
                                    product(bank(s, 3), wk[:, l], col_in[s][:])
                                    product(bank(s, 0), wk_rot[:, l], col_in[s][:]).then_inc(k_done[s], 1)
                                pe.wait_ge(r_in, 16 * R_ARRAYS)
                                for s in range(SLOTS):
                                    pe.wait_ge(q_ready[s], n)
                                    product(bank(s, 1), wg[:, l], col_in[s][:]).then_inc(g_done[s], 1)
                                    for c in range(NC):
                                        last = product(bank_c(s, 2)[:, c], col_in[s][:, c * P:(c + 1) * P], wv[:, l])
                                    last.then_inc(v_done[s], 1)
                                    pe.wait_ge(k_ready[s], n)
                                    turn(bank_c(s, 3), k[s][:].rearrange("p (c t) -> p c t", t=P), kt_done[s])

                                def score(s, c):
                                    pe.wait_ge(kh_ready[s], at + c + 1)
                                    if c == 0:
                                        pe.wait_ge(g_ready[s], n)
                                    else:
                                        pe.wait_ge(sc_ready[s], at + c)
                                    for h in range(NH):
                                        last = product(bank_c(s, h // 4)[:, h % 4], k_head[s][c % 2][:, h],
                                                       q[s][:, c * P:(c + 1) * P])
                                    last.then_inc(sc_done[s], 1)

                                def output(s, c):
                                    pe.wait_ge(sc_ready[s], at + c + 1)
                                    if c == 0:
                                        pe.wait_ge(kd_ready[s], n)
                                    if c == 1:
                                        pe.wait_ge(state_ready[s], n)
                                        pe.wait_ge(qd_ready[s], n)
                                    dst = bank_c(s, 3)[:, c]
                                    if c:
                                        nc.tensor.matmul(dst, qd[s][:, c * P:(c + 1) * P], state[s][:, c],
                                                         start=True, stop=False, skip_group_check=True)
                                    for h in range(NH):
                                        last = nc.tensor.matmul(dst[:, h * HD:(h + 1) * HD], scores[s][c % 2][:, h],
                                                                v[s][:, c, h * HD:(h + 1) * HD],
                                                                start=(c == 0 and h == 0), stop=(h == NH - 1),
                                                                skip_group_check=True)
                                    last.then_inc(y_done[s], 1)

                                for s in range(SLOTS):
                                    score(s, 0)
                                for s in range(SLOTS):
                                    pe.wait_ge(v_ready[s], n)
                                    pe.wait_ge(kd_ready[s], n)
                                    for c in range(NC - 1):
                                        last = product(bank_c(s, 2)[:, c], kd[s][:, c], v[s][:, c])
                                    last.then_inc(kv_done[s], 1)
                                for c in range(1, NC):
                                    for s in range(SLOTS):
                                        score(s, c)
                                    for s in range(SLOTS):
                                        output(s, c - 1)
                                for s in range(SLOTS):
                                    output(s, NC - 1)
                                for s in range(SLOTS):
                                    pe.wait_ge(y_row[s], n)
                                    turn(bank_c(s, 0), row[s], y_turned[s])
                                for s in range(SLOTS):
                                    pe.wait_ge(gy_ready[s], n)
                                    for c in range(NC):
                                        last = product(bank_c(s, 1)[:, c], col_in[s][:, c * P:(c + 1) * P], wo[:, l])
                                    last.then_inc(wo_done[s], 1)
                                for s in range(SLOTS):
                                    pe.wait_ge(n2_row[s], n)
                                    turn(bank_c(s, 2), row[s], n2_turned[s])
                                for j in range(4):
                                    for s in range(SLOTS):
                                        if j == 0:
                                            pe.wait_ge(n2_col[s], n)
                                        if j == 3:
                                            pe.wait_ge(h_ready[s], at + 2)
                                        product(bank(s, j % 3), fw1[:, l, j * P:(j + 1) * P],
                                                col_in[s][:]).then_inc(h_done[s], 1)
                                for s in range(SLOTS):
                                    for c in range(NC):
                                        for j in range(4):
                                            if c == 0:
                                                pe.wait_ge(h_ready[s], at + j + 2)
                                            last = nc.tensor.matmul(bank_c(s, 3)[:, c],
                                                                    big[s][:, j, c * P:(c + 1) * P], fw2[:, l, j],
                                                                    start=(j == 0), stop=(j == 3))
                                    last.then_inc(w2_done[s], 1)

        feed_forward("a", 0)
        retention()
        feed_forward("b", NT)

        x_out = sem("x_out")
        with nc.Block() as block:
            @block.sync
            def _(sp):
                sp.dma_start(A["out"], x_all[:]).then_inc(x_out, 16)
                sp.wait_ge(x_out, 16)


def constants():
    half = HD // 2
    scale_vec = (np.arange(0, HD, 2) + 0.4 * HD) / (1.4 * HD)
    scale = scale_vec[None, :] ** (np.arange(S, dtype=np.float64) / 64)[:, None]
    ang = np.arange(S, dtype=np.float64)[:, None] / 10000.0 ** (np.arange(half, dtype=np.float64) / half)[None, :]
    sin, cos = np.sin(ang), np.cos(ang)
    gammas = 1.0 - np.exp(np.linspace(np.log(1.0 / 32), np.log(1.0 / 64), NH))
    head = np.arange(P) // HD
    t = np.arange(P)

    def by_feature(m):
        return np.ascontiguousarray(np.tile(np.repeat(m, 2, axis=-1).T, (NH, 1)).astype(np.float32))

    diff = t[None, :] - t[:, None]
    decay = np.where(diff[None] >= 0, gammas[:, None, None] ** np.maximum(diff, 0)[None], 0.0)
    return {
        "ident": np.eye(P, dtype=np.float32),
        "tril": np.ascontiguousarray(np.broadcast_to(np.tril(np.ones((8, 8), np.float32), -1), (P, 8, 8))),
        "cos_q": by_feature(cos * scale), "sin_q": by_feature(sin * scale),
        "cos_k": by_feature(cos / scale), "sin_k": by_feature(sin / scale),
        "decay_q": (gammas[head][:, None] ** t[None, :]).astype(np.float32),
        "decay_k": (gammas[head][None, :] ** (P - t)[:, None]).astype(np.float32),
        "decay_qk": np.ascontiguousarray(decay.transpose(1, 0, 2).astype(np.float32)),
        "same_head": (head[:, None] == head[None, :]).astype(np.float32),
        "neg_half_grid": np.ascontiguousarray(np.broadcast_to(NEG_HALF_GRID, (P, NG))),
        "head_mask": (head[:, None] == np.arange(NH)[None, :]).astype(np.float32),
        "decay_chunk": (gammas[head] ** P).astype(np.float32)[:, None],
    }


def kernel(**inputs):
    import concourse.bacc as _bacc
    from concourse.bass_utils import run_bass_kernel_spmd as _run

    a = {k.replace("L0_attn_", "").replace("L0_ffn_", "f_"): np.asarray(v) for k, v in inputs.items()}
    con = constants()
    vectors = {
        "gate": a["f_gate_W"], "kan_g0": a["f_kan_ln_g0"].T, "kan_b0": a["f_kan_ln_b0"].T,
        "kan_g1": a["f_kan_ln_g1"].reshape(2 * NE, P).T, "kan_b1": a["f_kan_ln_b1"].reshape(2 * NE, P).T,
        "mlp_b1": a["f_mlp_b1"].reshape(4 * NE, P).T, "mlp_b2": a["f_mlp_b2"].T,
        "ln1_w": a["ln1_w"].T, "ln1_b": a["ln1_b"].T, "ln2_w": a["ln2_w"].T, "ln2_b": a["ln2_b"].T,
        "gn_w": a["gn_w"].T, "gn_b": a["gn_b"].T, "ffn_b1": a["ffn_b1"].reshape(4 * NL, P).T,
        "neg_half_grid": con.pop("neg_half_grid"), "head_mask": con.pop("head_mask"),
        "decay_chunk": con.pop("decay_chunk"),
    }
    arrays = {
        "x": a["X"].reshape(NB * NC, P, P).transpose(1, 0, 2),
        "cols": np.concatenate([vectors[k] for k in COLS], axis=1),
        "kan_rows": np.concatenate([a["f_kan_sl_b0"], a["f_kan_sl_b1"]], axis=1)[None],
        "w0": a["f_kan_sl_W0"].reshape(NE, P, NG, F2).transpose(1, 0, 2, 3),
        "w1": a["f_kan_sl_W1"].reshape(NE, 2, P, NG, P).transpose(2, 0, 1, 3, 4),
        "mw1": a["f_mlp_W1"].transpose(1, 0, 2),
        "mw2": a["f_mlp_W2"].reshape(NE, 4, P, P).transpose(2, 0, 1, 3),
        "wq": a["WQ"].transpose(2, 0, 1, 3).reshape(P, NL, P),
        "wk": a["WK"].transpose(2, 0, 1, 3).reshape(P, NL, P),
        "wv": a["WV"].transpose(2, 0, 1, 3).reshape(P, NL, P),
        "wg": a["WG"].transpose(1, 0, 2),
        "wo": a["WO"].transpose(1, 0, 2),
        "fw1": a["ffn_w1"].transpose(1, 0, 2),
        "fw2": a["ffn_w2"].reshape(NL, 4, P, P).transpose(2, 0, 1, 3),
        "b2_rows": np.broadcast_to(a["ffn_b2"][None], (P, NL, P)),
        **con,
    }
    nc = _bacc.Bacc("TRN2", target_bir_lowering=False, num_devices=1)
    arrays = {f"in_{k}": np.ascontiguousarray(v) for k, v in arrays.items()}
    args = {k[3:]: nc.dram_tensor(k, v.shape, F32, kind="ExternalInput").ap() for k, v in arrays.items()}
    args["out"] = nc.dram_tensor("out", (P, NB * NC, P), F32, kind="ExternalOutput").ap()
    build(nc, args)
    r = _run(nc, [arrays], core_ids=[0])
    got = r.results[0]["out"]
    return np.ascontiguousarray(got.transpose(1, 0, 2)).reshape(NB, S, P)
```
